# Optimizing a Trainium2 kernel written in Bass

```python
import numpy as np
import jax
import jax.numpy as jnp

def _softmax(x, axis=-1):
    return jax.nn.softmax(x, axis=axis)

def _gelu(x):
    return jax.nn.gelu(x, approximate=True)

def _silu(x):
    return jax.nn.silu(x)

def _sigmoid(x):
    return jax.nn.sigmoid(x)

def _layernorm(x, axis=-1, eps=1e-05):
    m = jnp.mean(x, axis=axis, keepdims=True)
    v = jnp.var(x, axis=axis, keepdims=True)
    return (x - m) / jnp.sqrt(v + eps)

def _scatter_add(tgt, idx, src, axis=0):
    return tgt.at[idx].add(src)

def _segment_sum(src, seg, n):
    return jax.ops.segment_sum(src, seg, n)
kernel_name = 'mk_gps_d1_gnn_r8_eb946f'

def setup_inputs(seed: int=0):
    np.random.seed(seed)
    _w = jnp.asarray

    def _rec_inputs():
        import jax
        import jax.numpy as jnp
        _gk = jax.random.key(seed)
        x = -0.0003713 + 1 * jax.random.normal(jax.random.fold_in(_gk, 1), (6250, 256), jnp.float32)
        _s = jax.random.randint(jax.random.fold_in(_gk, 2), (100000,), 0, 6250, jnp.int32)
        _d = jax.random.randint(jax.random.fold_in(_gk, 3), (100000,), 0, 6250, jnp.int32)
        _loop = jnp.arange(6250, dtype=jnp.int32)
        src = jnp.concatenate([_s, _d, _loop])
        dst = jnp.concatenate([_d, _s, _loop])
        _o = jnp.argsort(dst, stable=True)
        src = src[_o]
        dst = dst[_o]
        return (x, src, dst)
    x, src, dst = _rec_inputs()

    def _L0_gnn_setup():
        import jax, jax.numpy as jnp
        import numpy as np
        N_NODES = 6250
        N_EDGES = 200000
        D_IN = 256
        D_HID = 256

        def _gcn_norm(edge_index, num_nodes):
            loops = jnp.arange(num_nodes, dtype=edge_index.dtype)
            src = jnp.concatenate([edge_index[0], loops])
            dst = jnp.concatenate([edge_index[1], loops])
            ones = jnp.ones_like(src, dtype=jnp.float32)
            deg = jax.ops.segment_sum(ones, dst, num_segments=num_nodes)
            dinv = jnp.where(deg > 0, jax.lax.rsqrt(deg), 0.0)
            norm = dinv[src] * dinv[dst]
            return (src, dst, norm)

        def _gcn_layer(x, W, b, src, dst, norm, num_nodes):
            h = x @ W
            msg = h[src] * norm[:, None]
            agg = jax.ops.segment_sum(msg, dst, num_segments=num_nodes)
            return agg + b
        key = jax.random.key(seed)
        k_x, k_e, k_w1, k_w2 = jax.random.split(key, 4)
        glorot = lambda k, fi, fo: jax.random.uniform(k, (fi, fo), jnp.float32, -jnp.sqrt(6.0 / (fi + fo)), jnp.sqrt(6.0 / (fi + fo)))
        return {'x': jax.random.normal(k_x, (N_NODES, D_IN), jnp.float32), 'edge_index': jax.random.randint(k_e, (2, N_EDGES), 0, N_NODES, jnp.int64), 'W1': glorot(k_w1, D_IN, D_HID), 'b1': jnp.zeros((D_HID,), jnp.float32), 'W2': glorot(k_w2, D_HID, D_HID), 'b2': jnp.zeros((D_HID,), jnp.float32)}
    _L0_gnn_all = _L0_gnn_setup()
    _L0_gnn_in = {k: v for k, v in _L0_gnn_all.items() if k in ('W1', 'b1', 'W2', 'b2')}
    del _L0_gnn_all

    def _L0_mix_setup():
        import math
        import jax, jax.numpy as jnp
        import numpy as np
        EPS_DIV = 1e-07
        EPS_NORM = 1e-12

        def _l2_normalize(x, axis):
            n = jnp.sqrt(jnp.sum(x * x, axis=axis, keepdims=True))
            return x / jnp.maximum(n, EPS_NORM)
        key = jax.random.key(seed)
        ks = jax.random.split(key, 5)
        b, N, C = (8, 512, 256)
        x = jax.random.normal(ks[0], (b, N, C), dtype=jnp.float32)
        W_qkv = jax.random.normal(ks[1], (C, 3 * C), dtype=jnp.float32) * (1.0 / math.sqrt(C))
        b_qkv = jax.random.normal(ks[2], (3 * C,), dtype=jnp.float32) * 0.02
        W_out = jax.random.normal(ks[3], (C, C), dtype=jnp.float32) * (1.0 / math.sqrt(C))
        b_out = jax.random.normal(ks[4], (C,), dtype=jnp.float32) * 0.02
        return {'x': x, 'W_qkv': W_qkv, 'b_qkv': b_qkv, 'W_out': W_out, 'b_out': b_out}
    _L0_mix_all = _L0_mix_setup()
    _L0_mix_in = {k: v for k, v in _L0_mix_all.items() if k in ('W_qkv', 'b_qkv', 'W_out', 'b_out')}
    del _L0_mix_all

    def _L0_ffn_setup():
        import jax, jax.numpy as jnp
        import numpy as np
        DIM = 256
        H = 8
        D = 64
        G = 64
        INNER = H * D
        SCALE = D ** (-0.5)
        key = jax.random.key(seed)
        ks = jax.random.split(key, 12)
        B, N = (4, 2048)
        x = jax.random.normal(ks[0], (B, N, DIM), dtype=jnp.float32)
        s = lambda fan_in: 1.0 / np.sqrt(fan_in)
        W_fx = jax.random.normal(ks[1], (DIM, INNER), dtype=jnp.float32) * s(DIM)
        b_fx = jnp.zeros((INNER,), dtype=jnp.float32)
        W_x = jax.random.normal(ks[2], (DIM, INNER), dtype=jnp.float32) * s(DIM)
        b_x = jnp.zeros((INNER,), dtype=jnp.float32)
        A = jax.random.normal(ks[3], (G, D), dtype=jnp.float32)
        Q, _ = jnp.linalg.qr(A.T)
        W_slice = Q[:, :G].astype(jnp.float32)
        b_slice = jnp.zeros((G,), dtype=jnp.float32)
        W_q = jax.random.normal(ks[4], (D, D), dtype=jnp.float32) * s(D)
        W_k = jax.random.normal(ks[5], (D, D), dtype=jnp.float32) * s(D)
        W_v = jax.random.normal(ks[6], (D, D), dtype=jnp.float32) * s(D)
        W_out = jax.random.normal(ks[7], (INNER, DIM), dtype=jnp.float32) * s(INNER)
        b_out = jnp.zeros((DIM,), dtype=jnp.float32)
        temperature = jnp.ones((1, H, 1, 1), dtype=jnp.float32) * 0.5
        return {'x': x, 'W_fx': W_fx, 'b_fx': b_fx, 'W_x': W_x, 'b_x': b_x, 'W_slice': W_slice, 'b_slice': b_slice, 'W_q': W_q, 'W_k': W_k, 'W_v': W_v, 'W_out': W_out, 'b_out': b_out, 'temperature': temperature}
    _L0_ffn_all = _L0_ffn_setup()
    _L0_ffn_in = {k: v for k, v in _L0_ffn_all.items() if k in ('W_fx', 'b_fx', 'W_x', 'b_x', 'W_slice', 'b_slice', 'W_q', 'W_k', 'W_v', 'W_out', 'b_out', 'temperature')}
    del _L0_ffn_all
    return {'x': x, 'src': src, 'dst': dst, 'L0_gnn_W1': _L0_gnn_in['W1'], 'L0_gnn_b1': _L0_gnn_in['b1'], 'L0_gnn_W2': _L0_gnn_in['W2'], 'L0_gnn_b2': _L0_gnn_in['b2'], 'L0_mix_W_qkv': _L0_mix_in['W_qkv'], 'L0_mix_b_qkv': _L0_mix_in['b_qkv'], 'L0_mix_W_out': _L0_mix_in['W_out'], 'L0_mix_b_out': _L0_mix_in['b_out'], 'L0_ffn_W_fx': _L0_ffn_in['W_fx'], 'L0_ffn_b_fx': _L0_ffn_in['b_fx'], 'L0_ffn_W_x': _L0_ffn_in['W_x'], 'L0_ffn_b_x': _L0_ffn_in['b_x'], 'L0_ffn_W_slice': _L0_ffn_in['W_slice'], 'L0_ffn_b_slice': _L0_ffn_in['b_slice'], 'L0_ffn_W_q': _L0_ffn_in['W_q'], 'L0_ffn_W_k': _L0_ffn_in['W_k'], 'L0_ffn_W_v': _L0_ffn_in['W_v'], 'L0_ffn_W_out': _L0_ffn_in['W_out'], 'L0_ffn_b_out': _L0_ffn_in['b_out'], 'L0_ffn_temperature': _L0_ffn_in['temperature']}

def reference(x, src, dst, L0_gnn_W1, L0_gnn_b1, L0_gnn_W2, L0_gnn_b2, L0_mix_W_qkv, L0_mix_b_qkv, L0_mix_W_out, L0_mix_b_out, L0_ffn_W_fx, L0_ffn_b_fx, L0_ffn_W_x, L0_ffn_b_x, L0_ffn_W_slice, L0_ffn_b_slice, L0_ffn_W_q, L0_ffn_W_k, L0_ffn_W_v, L0_ffn_W_out, L0_ffn_b_out, L0_ffn_temperature):
    import jax
    import jax.numpy as jnp

    def _L0_gnn_ref(x, edge_index, W1, b1, W2, b2):
        import jax, jax.numpy as jnp
        import numpy as np
        N_NODES = 6250
        N_EDGES = 200000
        D_IN = 256
        D_HID = 256

        def _gcn_norm(edge_index, num_nodes):
            loops = jnp.arange(num_nodes, dtype=edge_index.dtype)
            src = jnp.concatenate([edge_index[0], loops])
            dst = jnp.concatenate([edge_index[1], loops])
            ones = jnp.ones_like(src, dtype=jnp.float32)
            deg = jax.ops.segment_sum(ones, dst, num_segments=num_nodes)
            dinv = jnp.where(deg > 0, jax.lax.rsqrt(deg), 0.0)
            norm = dinv[src] * dinv[dst]
            return (src, dst, norm)

        def _gcn_layer(x, W, b, src, dst, norm, num_nodes):
            h = x @ W
            msg = h[src] * norm[:, None]
            agg = jax.ops.segment_sum(msg, dst, num_segments=num_nodes)
            return agg + b
        num_nodes = x.shape[0]
        src, dst, norm = _gcn_norm(edge_index, num_nodes)
        z = jax.nn.relu(_gcn_layer(x, W1, b1, src, dst, norm, num_nodes))
        z = jax.nn.relu(_gcn_layer(z, W2, b2, src, dst, norm, num_nodes))
        return z

    def _L0_mix_ref(x, W_qkv, b_qkv, W_out, b_out):
        import math
        import jax, jax.numpy as jnp
        import numpy as np
        EPS_DIV = 1e-07
        EPS_NORM = 1e-12

        def _l2_normalize(x, axis):
            n = jnp.sqrt(jnp.sum(x * x, axis=axis, keepdims=True))
            return x / jnp.maximum(n, EPS_NORM)
        b, N, C = x.shape
        qkv = x @ W_qkv + b_qkv
        q, k, v = jnp.split(qkv, 3, axis=2)
        q = q - jnp.mean(q, axis=2, keepdims=True)
        k = k - jnp.mean(k, axis=2, keepdims=True)
        q2 = q * q
        k2 = k * k
        q2s = jnp.sum(q2, axis=2, keepdims=True)
        k2s = jnp.sum(k2, axis=2, keepdims=True)
        k2 = _l2_normalize(k2 / (k2s + EPS_DIV), axis=-2)
        q2 = _l2_normalize(q2 / (q2s + EPS_DIV), axis=-1)
        kv = jnp.einsum('bnc,bnd->bcd', k2, v)
        t2 = jnp.einsum('bnc,bcd->bnd', q2, kv) / math.sqrt(N)
        attn = v + t2
        return attn @ W_out + b_out

    def _L0_ffn_ref(x, W_fx, b_fx, W_x, b_x, W_slice, b_slice, W_q, W_k, W_v, W_out, b_out, temperature):
        import jax, jax.numpy as jnp
        import numpy as np
        DIM = 256
        H = 8
        D = 64
        G = 64
        INNER = H * D
        SCALE = D ** (-0.5)
        B, N, _ = x.shape
        fx_mid = (x @ W_fx + b_fx).reshape(B, N, H, D).transpose(0, 2, 1, 3)
        x_mid = (x @ W_x + b_x).reshape(B, N, H, D).transpose(0, 2, 1, 3)
        temp = jnp.clip(temperature, 0.1, 5.0)
        slice_weights = jax.nn.softmax((x_mid @ W_slice + b_slice) / temp, axis=-1)
        slice_norm = slice_weights.sum(axis=2)
        slice_token = jnp.einsum('bhnc,bhng->bhgc', fx_mid, slice_weights)
        slice_token = slice_token / (slice_norm[..., None] + 1e-05)
        q = slice_token @ W_q
        k = slice_token @ W_k
        v = slice_token @ W_v
        attn = jax.nn.softmax(jnp.einsum('bhgc,bhkc->bhgk', q, k) * SCALE, axis=-1)
        out_slice = jnp.einsum('bhgk,bhkc->bhgc', attn, v)
        out_x = jnp.einsum('bhgc,bhng->bhnc', out_slice, slice_weights)
        out_x = out_x.transpose(0, 2, 1, 3).reshape(B, N, INNER)
        return out_x @ W_out + b_out
    edge_index = jnp.stack([src, dst])
    xn = _layernorm(x, axis=-1)
    x = x + _L0_gnn_ref(xn, edge_index, L0_gnn_W1, L0_gnn_b1, L0_gnn_W2, L0_gnn_b2) + _L0_mix_ref(xn[None], L0_mix_W_qkv, L0_mix_b_qkv, L0_mix_W_out, L0_mix_b_out)[0]
    x = x + _L0_ffn_ref(_layernorm(x, axis=-1)[None], L0_ffn_W_fx, L0_ffn_b_fx, L0_ffn_W_x, L0_ffn_b_x, L0_ffn_W_slice, L0_ffn_b_slice, L0_ffn_W_q, L0_ffn_W_k, L0_ffn_W_v, L0_ffn_W_out, L0_ffn_b_out, L0_ffn_temperature)[0]
    return x

_drawn_inputs = setup_inputs


def setup_inputs(seed=0):
    import zlib

    import numpy as np

    out = dict(_drawn_inputs(seed))
    spreads = {'L0_gnn_b1': (0.0, 0.1),
     'L0_gnn_b2': (0.0, 0.1),
     'L0_ffn_b_fx': (0.0, 0.1),
     'L0_ffn_b_x': (0.0, 0.8),
     'L0_ffn_b_slice': (0.0, 2.0),
     'L0_ffn_b_out': (0.0, 0.1),
     'L0_ffn_temperature': (0.5, 0.6)}
    factors = {'L0_gnn_W1': 4.216,
     'L0_mix_b_out': 3.481,
     'L0_ffn_W_x': 8.0,
     'L0_ffn_W_slice': 8.0,
     'L0_ffn_W_q': 8.0,
     'L0_ffn_W_k': 8.0}
    for name, (base, spread) in spreads.items():
        noise = np.random.default_rng([zlib.crc32(name.encode()), seed]).standard_normal(out[name].shape)
        drawn = base * np.exp(spread * noise) if base else spread * noise
        out[name] = jnp.asarray(drawn.astype(out[name].dtype))
    for name, factor in factors.items():
        out[name] = (out[name] * factor).astype(out[name].dtype)
    return out
```

```python
from contextlib import ExitStack

import concourse.bass as bass
from concourse import mybir

ALU = mybir.AluOpType
ACT = mybir.ActivationFunctionType
F32 = mybir.dt.float32
F16 = mybir.dt.float16
I32 = mybir.dt.int32
AX = mybir.AxisListType
RMAX = bass.bass_isa.ReduceOp.max

P = 128


def gps_layer(nc, x, src, dst, W1, b1, W2, b2, W_qkv, b_qkv, W_mo, b_mo,
              W_fx, b_fx, W_x, b_x, W_sl, b_sl, W_q, W_k, W_v, W_fo, b_fo, temp, out):
    N, C = x.shape
    E = src.shape[0]
    T = -(-N // P)
    LAST = N - (T - 1) * P
    WIN = 8
    WPT = P // WIN
    NW = T * WPT
    CHUNKS = 3
    CAP = CHUNKS * P
    GW = 112
    G = NW // GW
    KC = T * WIN
    ROWL = 125
    ROWS = E // ROWL
    HP = 110
    HC = ROWS // HP
    HEADS, D = 8, W_sl.shape[0]
    HG = HEADS * D
    CB = C // P
    HB = HG // P
    SH = 2048.0
    assert C == 256 and CB == 2 and D == 64 and HG == 512 and G * GW == NW and T % 2 == 1
    assert ROWS * ROWL == E and HP * HC == ROWS and KC <= 512

    deg_dram = nc.dram_tensor("deg_scratch", (T * P,), F32, kind="Internal").ap()
    at_dram = nc.dram_tensor("at_scratch", (T, P, T * P), F16, kind="Internal").ap()
    base_dram = nc.dram_tensor("base_scratch", (T * P, C), F32, kind="Internal").ap()
    xT_dram = nc.dram_tensor("xT_scratch", (T, 2, P, C), F32, kind="Internal").ap()
    wT_dram = nc.dram_tensor("wT_scratch", (T, P, HG), F32, kind="Internal").ap()
    x1_dram = nc.dram_tensor("x1_scratch", (T * P, C), F32, kind="Internal").ap()

    with ExitStack() as life:
        def sb(name, shape, dt=F32):
            return life.enter_context(nc.sbuf_tensor(name, shape, dt))

        def sem(name):
            return life.enter_context(nc.semaphore(name))

        def carve(region):
            at = [0]

            def take(shape, dt=F32):
                n = 1
                for s in shape[1:]:
                    n *= s
                words = n if dt in (F32, I32) else -(-n // 2)
                a = region[0:shape[0], at[0]:at[0] + words]
                at[0] += words
                assert at[0] <= region.shape[1], (at[0], region.shape)
                if dt != F32:
                    a = a.bitcast(dt)
                if dt == F16 and n % 2:
                    a = a[:, 0:n]
                if len(shape) == 3:
                    a = a.rearrange("p (a b) -> p a b", b=shape[2])
                if len(shape) == 4:
                    a = a.rearrange("p (a b c) -> p a b c", b=shape[2], c=shape[3])
                return a
            return take

        hs = sb("hs", [P, T, 2 * C], F16)
        big = sb("big", [P, 2 * T, C])
        key_lo = sb("key_lo", [P, NW, CHUNKS])
        key_hi = sb("key_hi", [P, NW, CHUNKS])
        at = sb("at", [P, 2, T * P], F16)
        ident = sb("ident", [P, P])
        ident16 = sb("ident16", [P, P], F16)
        w1 = sb("w1", [P, CB, C])
        w2 = sb("w2", [P, CB, C])
        wlog = sb("wlog", [P, CB, HG])
        b1b = sb("b1b", [P, C])
        b2b = sb("b2b", [P, C])
        blogb = sb("blogb", [P, HG])
        dinv = sb("dinv", [P, T])
        dsc = sb("dsc", [P, T])
        dun = sb("dun", [P, T])
        small = sb("small", [P, 24])
        eps = sb("eps", [P, 1])
        tmax = sb("tmax", [P, T])
        ps = life.enter_context(nc.psum_tensor("ps", [P, 8, 512], F32))

        at_f32 = at[:, :, :].rearrange("p a b -> p (a b)").bitcast(F32)
        big_f = big[:, :, :].rearrange("p a b -> p (a b)")
        hs_f32 = hs[:, :, :].rearrange("p a b -> p (a b)").bitcast(F32)
        z1s = big[:, 0:T, :]

        take = carve(at_f32)
        wqk = take([P, CB, 2 * C])
        bqk = take([P, 2 * C])
        wvo = take([P, CB, C])
        bvw = take([P, C])
        bvo = take([P, C])
        mkv = take([P, CB, C])

        ones = sb("ones", [P, 2])
        zeros = sb("zeros", [P, P])
        row0 = sb("row0", [P, P])
        ident_sem = sem("ident_sem")

        with ExitStack() as stage:
            take = carve(big_f)
            heads = take([HP, HC], I32)
            heads_f = take([HP, HC])
            w8 = take([HP, NW], F16)
            past = take([HP, HC, NW], F16)
            wfirst = take([GW, G])
            rbase = take([GW, G])
            ridx_f = take([GW, G])
            ridx = take([GW, G], I32)
            cnt = take([GW, G])
            lo_f = take([GW, G])
            lo = take([GW, G], I32)
            rowd = take([GW, G, ROWL], I32)
            srcg = take([GW, G, CAP], I32)
            dstg = take([GW, G, CAP], I32)
            dl = take([GW, G, CAP])
            tmp_i = take([GW, G, CAP], I32)
            tmp_f = take([GW, G, CAP])
            junk = take([GW, 4, CAP])
            deg = take([GW, G, WIN])
            ones16 = take([P, 2], F16)
            take = carve(hs_f32)
            wqkv = take([P, CB, 3 * C])
            wmo = take([P, CB, C])
            wx = take([P, CB, HG])
            bdsl = take([P, P])
            bx4 = take([P, HB])
            bv2 = take([P, CB])
            bmo = take([P, C])
            bsl = take([P, D])
            tmpr = take([P, HEADS])
            wvT = take([P, CB, CB, P])
            wxT = take([P, HB, CB, P])
            msum = take([P, CB, 2])
            bsum = take([P, 2])
            degr = take([T, P])
            bxb = take([P, HB, P])
            bvb = take([P, CB, P])

            head_loaded, weights_loaded = sem("head_loaded"), sem("weights_loaded")
            iotas_ready, zeros_ready, past_ready = sem("iotas_ready"), sem("zeros_ready"), sem("past_ready")
            rows_counted, ridx_ready, row_gathered = sem("rows_counted"), sem("ridx_ready"), sem("row_gathered")
            lo_ready, src_gathered, dst_gathered = sem("lo_ready"), sem("src_gathered"), sem("dst_gathered")
            keys_made, keys_turned, keys_stored = sem("keys_made"), sem("keys_turned"), sem("keys_stored")
            deg_ready, deg_stored, deg_loaded = sem("deg_ready"), sem("deg_stored"), sem("deg_loaded")
            deg_turned, wt_turned, wt_stored = sem("deg_turned"), sem("wt_turned"), sem("wt_stored")
            wprod, wprod_used, invt_ready, dve_step = sem("wprod"), sem("wprod_used"), sem("invt_ready"), sem("dve_step")
            deg_counted = sem("deg_counted")
            spread_ready, deg_plus, deg_root = sem("spread_ready"), sem("deg_plus"), sem("deg_root")

            block = stage.enter_context(nc.Block())
            NWL = 17

            @block.sync
            def _(sp):
                with nc.allow_non_contiguous_dma(reason="every 125th edge, columns of small biases"):
                    sp.dma_start(heads.rearrange("p (c o) -> p c o", o=1),
                                 dst.rearrange("(p c l) -> p c l", c=HC, l=ROWL)[:, :, 0:1]).then_inc(head_loaded, 16)
                    sp.wait_ge(zeros_ready, 1)
                    loads = [(wqkv, W_qkv.rearrange("(b p) n -> p b n", p=P)),
                             (wmo, W_mo.rearrange("(b p) n -> p b n", p=P)),
                             (wx, W_x.rearrange("(b p) n -> p b n", p=P)),
                             (bdsl[0:D, 0:D], W_sl), (bdsl[D:P, D:P], W_sl),
                             (bx4, b_x.rearrange("(b p) -> p b", p=P)),
                             (bv2, b_qkv[2 * C:3 * C].rearrange("(b p) -> p b", p=P)),
                             (bmo, b_mo.rearrange("(a n) -> a n", a=1).to_broadcast([P, C])),
                             (bsl, b_sl.rearrange("(a n) -> a n", a=1).to_broadcast([P, D])),
                             (bqk, b_qkv[0:2 * C].rearrange("(a n) -> a n", a=1).to_broadcast([P, 2 * C])),
                             (tmpr, temp.rearrange("a h b c -> a (h b c)").to_broadcast([P, HEADS])),
                             (w1[:, :, :], W1.rearrange("(b p) n -> p b n", p=P)),
                             (w2[:, :, :], W2.rearrange("(b p) n -> p b n", p=P)),
                             (b1b[:, :], b1.rearrange("(a n) -> a n", a=1).to_broadcast([P, C])),
                             (b2b[:, :], b2.rearrange("(a n) -> a n", a=1).to_broadcast([P, C]))]
                    assert len(loads) == NWL - 2
                    for to, of in loads:
                        sp.dma_start(to, of).then_inc(weights_loaded, 16)
                sp.wait_ge(deg_counted, G * WIN)
                sp.dma_start(deg_dram.rearrange("(g p j) -> p g j", g=G, j=WIN), deg).then_inc(deg_stored, 16)
                sp.wait_ge(deg_stored, 16)
                sp.dma_start(degr, deg_dram.rearrange("(t p) -> t p", p=P)).then_inc(deg_loaded, 16)
                sp.wait_ge(deg_loaded, 16)

            @block.gpsimd
            def _(pool):
                nc.gpsimd.memset(ident[:, :], 0.0).then_inc(ident_sem, 1)
                nc.gpsimd.memset(bdsl, 0.0).then_inc(zeros_ready, 1)
                nc.gpsimd.iota(w8, [[WIN, NW]], base=0, channel_multiplier=0,
                               allow_small_or_imprecise_dtypes=True)
                nc.gpsimd.iota(wfirst, [[WIN * GW, G]], base=0, channel_multiplier=WIN,
                               allow_small_or_imprecise_dtypes=True).then_inc(iotas_ready, 1)
                pool.wait_ge(ident_sem, 1)
                nc.gpsimd.affine_select(out=ident[:, :], in_=ident[:, :], compare_op=ALU.not_equal, fill=1.0,
                                        base=0, pattern=[[-1, P]], channel_multiplier=1).then_inc(ident_sem, 1)
                pool.wait_ge(ridx_ready, 1)
                for g in range(G):
                    pool.indirect_dma_start(
                        out=rowd[:, g, :], out_offset=None, in_=dst.rearrange("(r l) -> r l", l=ROWL),
                        in_offset=bass.IndirectOffsetOnAxis(ap=ridx[:, g:g + 1], axis=0)).then_inc(row_gathered, 16)
                pool.wait_ge(row_gathered, 16 * G)
                pool.wait_ge(lo_ready, 1)
                for g in range(G):
                    for to, of, s in ((srcg, src, src_gathered), (dstg, dst, dst_gathered)):
                        pool.indirect_dma_start(
                            out=to[:, g, :], out_offset=None, in_=of.rearrange("(e a) -> e a", a=1),
                            in_offset=bass.IndirectOffsetOnAxis(ap=lo[:, g:g + 1], axis=0)).then_inc(s, 16)
                pool.wait_ge(src_gathered, 16 * G)
                pool.wait_ge(dst_gathered, 16 * G)

            @block.vector
            def _(dve):
                steps = [0]

                def step(ins):
                    steps[0] += 1
                    ins.then_inc(dve_step, 1)
                    dve.wait_ge(dve_step, steps[0])

                v = nc.vector
                v.memset(ones[:, :], 1.0)
                v.memset(ones16, 1.0)
                v.memset(row0[:, :], 0.0)
                v.memset(zeros[:, :], 0.0)
                v.memset(eps[:, :], 1e-5)
                dve.wait_ge(head_loaded, 16)
                step(v.tensor_copy(heads_f, heads))
                step(v.memset(row0[0:1, :], 1.0))
                dve.wait_ge(iotas_ready, 1)
                for c in range(HC):
                    v.tensor_scalar(past[:, c, :], w8, heads_f[:, c:c + 1], None, ALU.is_gt).then_inc(past_ready, 1)
                dve.wait_ge(ident_sem, 2)
                v.tensor_copy(ident16[:, :], ident[:, :]).then_inc(ident_sem, 1)
                dve.wait_ge(rows_counted, 1)
                step(v.tensor_scalar(ridx_f, ps[0:GW, 0, 0:G], -1.0, 0.0, ALU.add, ALU.max))
                v.tensor_copy(ridx, ridx_f).then_inc(ridx_ready, 1)
                step(v.tensor_scalar(rbase, ridx_f, float(ROWL), None, ALU.mult))
                dve.wait_ge(weights_loaded, 16 * (NWL - 2))
                qk = wqkv[:, :, 0:2 * C].rearrange("p b (h c) -> p b h c", c=C)
                for b in range(CB):
                    v.tensor_reduce(msum[:, b, :], qk[:, b], AX.X, ALU.add)
                v.tensor_copy(bxb, bx4.rearrange("p (b o) -> p b o", o=1).to_broadcast([P, HB, P]))
                v.tensor_copy(bvb, bv2.rearrange("p (b o) -> p b o", o=1).to_broadcast([P, CB, P])).then_inc(spread_ready, 1)
                step(v.tensor_reduce(bsum, bqk.rearrange("p (h c) -> p h c", c=C), AX.X, ALU.add))
                step(v.tensor_scalar(msum, msum, -1.0 / C, None, ALU.mult))
                step(v.tensor_scalar(bsum, bsum, -1.0 / C, None, ALU.mult))
                for h in range(2):
                    for b in range(CB):
                        v.tensor_scalar(wqk[:, b, h * C:(h + 1) * C], qk[:, b, h, :], msum[:, b, h:h + 1], None, ALU.add)
                    v.tensor_scalar(bqk[:, h * C:(h + 1) * C], bqk[:, h * C:(h + 1) * C],
                                    bsum[:, h:h + 1], None, ALU.add)
                step(v.tensor_scalar(tmpr, tmpr, 0.1, 5.0, ALU.max, ALU.min))
                step(v.reciprocal(tmpr, tmpr))
                dve.wait_ge(row_gathered, 16 * G)
                for g in range(G):
                    last = v.tensor_scalar(junk[:, g % 4, 0:ROWL], rowd[:, g, :], wfirst[:, g:g + 1], 0.0,
                                           ALU.is_lt, ALU.add, accum_out=cnt[:, g:g + 1])
                    step(last)
                step(v.tensor_tensor(lo_f, rbase, cnt, ALU.add))
                step(v.tensor_scalar(lo_f, lo_f, float(E - CAP), None, ALU.min))
                v.tensor_copy(lo, lo_f).then_inc(lo_ready, 1)
                dve.wait_ge(wprod, 1)
                itb = tmpr.rearrange("p (h o) -> p h o", o=1)
                for b in range(CB):
                    v.tensor_tensor(wlog[:, b, :].rearrange("p (h d) -> p h d", d=D),
                                    ps[:, 6 + b, :].rearrange("p (h d) -> p h d", d=D),
                                    itb.to_broadcast([P, HEADS, D]), ALU.mult)
                by_head = blogb[:, :].rearrange("p (h d) -> p h d", d=D)
                step(v.tensor_tensor(by_head, ps[:, 5, :].rearrange("p (h d) -> p h d", d=D),
                                     bsl.rearrange("p (o d) -> p o d", o=1).to_broadcast([P, HEADS, D]), ALU.add))
                v.tensor_tensor(by_head, by_head, itb.to_broadcast([P, HEADS, D]), ALU.mult)
                v.tensor_copy(bvw, ps[:, 1, 0:C])
                v.tensor_tensor(bvo, ps[:, 1, 0:C], bmo, ALU.add).then_inc(wprod_used, 1)
                dve.wait_ge(dst_gathered, 16 * G)
                for g in range(G):
                    last = v.tensor_scalar(dl[:, g, :], dstg[:, g, :], wfirst[:, g:g + 1], None, ALU.subtract)
                step(last)
                dve.wait_ge(src_gathered, 16 * G)
                step(v.tensor_scalar(tmp_i, srcg, P - 1, None, ALU.bitwise_and))
                step(v.tensor_scalar(tmp_f, dl, float(WIN), None, ALU.is_lt))
                step(v.scalar_tensor_tensor(out=tmp_f, in0=dl, scalar=0.0, in1=tmp_f, op0=ALU.is_ge, op1=ALU.mult))
                step(v.scalar_tensor_tensor(out=tmp_f, in0=tmp_i, scalar=1.0, in1=tmp_f, op0=ALU.add, op1=ALU.mult))
                v.tensor_scalar(srcg, srcg, 4, 0xFFF8, ALU.logical_shift_right, ALU.bitwise_and).then_inc(keys_made, 1)
                for g in range(G):
                    for j in range(WIN):
                        n = g * WIN + j
                        if n >= 4:
                            dve.wait_ge(deg_counted, n - 3)
                        v.tensor_scalar(junk[:, n % 4, :], dl[:, g, :], float(j), 0.0, ALU.is_equal, ALU.add,
                                        accum_out=deg[:, g, j:j + 1]).then_inc(deg_counted, 1)
                dve.wait_ge(deg_counted, G * WIN)
                dve.wait_ge(keys_made, 1)
                v.tensor_tensor(dl, srcg, dl, ALU.add).then_inc(keys_made, 1)
                dve.wait_ge(deg_turned, 1)
                v.tensor_scalar(dinv[:, :], ps[:, 5, 0:T], 1.0, None, ALU.add).then_inc(deg_plus, 1)
                dve.wait_ge(deg_root, 1)
                step(v.reciprocal(dinv[:, :], dinv[:, :]))
                step(v.tensor_scalar(dsc[:, :], dinv[:, :], SH, None, ALU.mult))
                step(v.tensor_scalar(dun[:, :], dinv[:, :], 1.0 / SH, None, ALU.mult))
                v.tensor_reduce(small[:, 0:1], ps[:, 5, 0:T], AX.X, ALU.add).then_inc(deg_ready, 1)
                dve.wait_ge(deg_turned, 2)
                v.tensor_scalar(small[0:1, 1:2].bitcast(I32), ps[0:1, 0, 0:1], float(E), None, ALU.not_equal)

            @block.tensor
            def _(pe):
                t = nc.tensor
                for g in range(G):
                    for c in range(HC):
                        if g == 0:
                            pe.wait_ge(past_ready, c + 1)
                        mm = t.matmul(ps[0:GW, 0, g:g + 1], lhsT=past[:, c, g * GW:(g + 1) * GW],
                                      rhs=ones16[0:HP, 0:1], start=(c == 0), stop=(c == HC - 1))
                mm.then_inc(rows_counted, 1)
                pe.wait_ge(ident_sem, 2)
                pe.wait_ge(weights_loaded, 16 * (NWL - 2))
                for i in range(CB):
                    for c in range(CB):
                        mm = t.transpose(ps[:, 1, (c * CB + i) * P:(c * CB + i + 1) * P],
                                         wqkv[:, i, 2 * C + c * P:2 * C + (c + 1) * P], ident[:, :])
                mm.then_inc(wt_turned, 1)
                for i in range(CB):
                    for c in range(HB):
                        n = c * CB + i
                        mm = t.transpose(ps[:, 2 + n // 4, (n % 4) * P:(n % 4 + 1) * P],
                                         wx[:, i, c * P:(c + 1) * P], ident[:, :])
                mm.then_inc(wt_turned, 1)
                pe.wait_ge(wt_stored, 1)
                pe.wait_ge(spread_ready, 1)
                for i in range(CB):
                    for c in range(CB):
                        t.matmul(ps[:, 4, i * C:(i + 1) * C], lhsT=wvT[:, c, i, :], rhs=wmo[:, c, :],
                                 start=(c == 0), stop=(c == CB - 1))
                for c in range(CB):
                    t.matmul(ps[:, 1, 0:C], lhsT=bvb[:, c, :], rhs=wmo[:, c, :],
                             start=(c == 0), stop=(c == CB - 1))
                pe.wait_ge(wt_stored, 2)
                for c in range(HB):
                    for i in range(CB):
                        t.matmul(ps[:, 6 + i, c * P:(c + 1) * P], lhsT=wxT[:, c, i, :], rhs=bdsl, start=True, stop=True)
                    mm = t.matmul(ps[:, 5, c * P:(c + 1) * P], lhsT=bxb[:, c, :], rhs=bdsl, start=True, stop=True)
                mm.then_inc(wprod, 1)
                pe.wait_ge(wprod_used, 2)
                for n in range(2 * G):
                    keys = tmp_f if n < G else dl
                    pe.wait_ge(keys_made, 1 if n < G else 2)
                    if n >= 4:
                        pe.wait_ge(keys_stored, n - 3)
                    for c in range(CHUNKS):
                        mm = t.transpose(ps[:, 1 + n % 4, c * GW:(c + 1) * GW],
                                         keys[:, n % G, c * P:(c + 1) * P], ident[0:GW, 0:GW])
                    mm.then_inc(keys_turned, 1)
                pe.wait_ge(deg_loaded, 16)
                t.transpose(ps[:, 5, 0:T], degr, ident[0:T, 0:T]).then_inc(deg_turned, 1)
                pe.wait_ge(deg_ready, 1)
                t.matmul(ps[0:1, 0, 0:1], lhsT=small[:, 0:1], rhs=ones[:, 0:1], start=True, stop=True).then_inc(deg_turned, 1)

            @block.scalar
            def _(act):
                a = nc.scalar
                act.wait_ge(wt_turned, 1)
                a.copy(wvT.rearrange("p a b c -> p (a b c)"), ps[:, 1, :]).then_inc(wt_stored, 1)
                act.wait_ge(wt_turned, 2)
                a.copy(wxT.rearrange("p a b c -> p (a b c)"), ps[:, 2:4, :].rearrange("p a b -> p (a b)")).then_inc(wt_stored, 1)
                act.wait_ge(wprod, 1)
                a.copy(wvo.rearrange("p a b -> p (a b)"), ps[:, 4, :]).then_inc(wprod_used, 1)
                for n in range(2 * G):
                    act.wait_ge(keys_turned, n + 1)
                    keys, g = (key_lo if n < G else key_hi), n % G
                    a.copy(keys[:, g * GW:(g + 1) * GW, :].rearrange("p w c -> p c w"),
                           ps[:, 1 + n % 4, 0:CHUNKS * GW].rearrange("p (c w) -> p c w", w=GW)).then_inc(keys_stored, 1)
                act.wait_ge(deg_plus, 1)
                a.activation(dinv[:, :], dinv[:, :], ACT.Sqrt).then_inc(deg_root, 1)

        with ExitStack() as stage:
            take = carve(big_f)
            x_in = take([P, 2, C])
            xn = take([P, 2, C + 2])
            xt_now = take([P, 2, CB, P])
            q2t_now = take([P, 2, CB, P])
            qk2 = take([P, 2, 2 * C])
            k2n = take([P, 2, C])
            k4 = take([P, C])
            square = take([P, C])
            st = take([P, 2, 6])
            mv = take([P, 2, 2])
            rstd = take([P, 2])
            sums = take([P, 2, 2])
            rqk = take([P, 2, 2])
            nq = take([P, 2])
            fq = take([P, 2])
            x_loaded = [sem("x_loaded0"), sem("x_loaded1")]
            xn_ready, xn_turned, xnT_stored = sem("xn_ready"), sem("xn_turned"), sem("xnT_stored")
            qk_ready, sq_ready, recip_ready = sem("qk_ready"), sem("sq_ready"), sem("recip_ready")
            k4_ready, k2n_ready, kx_done = sem("k4_ready"), sem("k2n_ready"), sem("kx_done")
            q2f_ready, q2_turned, q2T_stored = sem("q2f_ready"), sem("q2_turned"), sem("q2T_stored")
            x_out, q_out = [sem("x_out0"), sem("x_out1")], [sem("q_out0"), sem("q_out1")]
            std_ready, rstd_ready, nq_root = sem("std_ready"), sem("rstd_ready"), sem("nq_root")
            ln_step, hi_ready, fq_step, zeroed = sem("ln_step"), sem("hi_ready"), sem("fq_step"), sem("zeroed")

            block = stage.enter_context(nc.Block())

            @block.sync
            def _(sp):
                def load(t, b, first=False, rows=P):
                    if not first:
                        sp.wait_ge(xn_ready, t - 1)
                    sp.dma_start(x_in[0:rows, b, :], x[bass.ds(t * P, rows), :]).then_inc(x_loaded[b], 16)

                def store_x(t, b):
                    sp.wait_ge(xnT_stored, t + 1)
                    sp.dma_start(xT_dram[bass.ds(t, 1), 0].rearrange("t p n -> (t p) n"),
                                 xt_now[:, b].rearrange("p a b -> p (a b)")).then_inc(x_out[b], 16)

                def store_q(t, b):
                    sp.wait_ge(q2T_stored, t + 1)
                    sp.dma_start(xT_dram[bass.ds(t, 1), 1].rearrange("t p n -> (t p) n"),
                                 q2t_now[:, b].rearrange("p a b -> p (a b)")).then_inc(q_out[b], 16)

                load(0, 0, first=True)
                load(1, 1, first=True)
                store_x(0, 0)
                with sp.Fori(1, T // 2) as u:
                    load(2 * u, 0)
                    store_x(2 * u - 1, 1)
                    store_q(2 * u - 2, 0)
                    load(2 * u + 1, 1)
                    store_x(2 * u, 0)
                    store_q(2 * u - 1, 1)
                load(T - 1, 0, rows=LAST)
                store_x(T - 2, 1)
                store_q(T - 3, 0)
                store_x(T - 1, 0)
                store_q(T - 2, 1)
                store_q(T - 1, 0)
                for b, n in ((0, T // 2 + 1), (1, T // 2)):
                    sp.wait_ge(x_out[b], 16 * n)
                    sp.wait_ge(q_out[b], 16 * n)

            @block.vector
            def _(dve):
                v = nc.vector
                v.memset(xn[:, :, C:C + 2], 1.0).then_inc(zeroed, 1)
                dve.wait_ge(zeroed, 1)

                def stats(t, b, u):
                    dve.wait_ge(x_loaded[b], 16 * (u + 1))
                    v.bn_stats(st[:, b, :], x_in[:, b, :]).then_inc(ln_step, 1)
                    dve.wait_ge(ln_step, 2 * t + 1)
                    v.memset(rstd[:, b:b + 1], 0.0)
                    v.bn_aggr(mv[:, b, :], st[:, b, :]).then_inc(ln_step, 1)

                def norm(t, b, first=False):
                    dve.wait_ge(std_ready, t + 1)
                    v.reciprocal(rstd[:, b:b + 1], rstd[:, b:b + 1]).then_inc(rstd_ready, 1)
                    dve.wait_ge(rstd_ready, t + 1)
                    if not first:
                        dve.wait_ge(kx_done, t - 1)
                        dve.wait_ge(xn_turned, t - 1)
                    v.tensor_scalar(xn[:, b, 0:C], x_in[:, b, :], mv[:, b, 0:1], rstd[:, b:b + 1],
                                    ALU.subtract, ALU.mult).then_inc(xn_ready, 1)
                    dve.wait_ge(xn_ready, t + 1)
                    v.tensor_scalar(hs[:, bass.ds(t, 1), 0:C].rearrange("p o c -> p (o c)"), xn[:, b, 0:C],
                                    dsc[:, bass.ds(t, 1)], None, ALU.mult).then_inc(hi_ready, 1)
                    dve.wait_ge(hi_ready, t + 1)
                    v.scalar_tensor_tensor(out=hs[:, bass.ds(t, 1), C:2 * C].rearrange("p o c -> p (o c)"),
                                           in0=xn[:, b, 0:C], scalar=dsc[:, bass.ds(t, 1)],
                                           in1=hs[:, bass.ds(t, 1), 0:C].rearrange("p o c -> p (o c)"),
                                           op0=ALU.mult, op1=ALU.subtract)

                def scale(t, b):
                    dve.wait_ge(sq_ready, 2 * t + 2)
                    v.tensor_scalar(rqk[:, b, :], sums[:, b, :], 1e-7, None, ALU.add).then_inc(recip_ready, 1)
                    dve.wait_ge(recip_ready, 2 * t + 1)
                    v.reciprocal(rqk[:, b, :], rqk[:, b, :]).then_inc(recip_ready, 1)
                    dve.wait_ge(recip_ready, 2 * t + 2)
                    v.tensor_scalar(k2n[:, b, :], qk2[:, b, C:2 * C], rqk[:, b, 1:2], None, ALU.mult).then_inc(k2n_ready, 1)
                    dve.wait_ge(nq_root, t + 1)
                    v.tensor_scalar(fq[:, b:b + 1], nq[:, b:b + 1], 1e-12, None, ALU.max).then_inc(fq_step, 1)
                    dve.wait_ge(fq_step, 3 * t + 1)
                    v.reciprocal(fq[:, b:b + 1], fq[:, b:b + 1]).then_inc(fq_step, 1)
                    dve.wait_ge(fq_step, 3 * t + 2)
                    v.tensor_tensor(fq[:, b:b + 1], fq[:, b:b + 1], rqk[:, b, 0:1], ALU.mult).then_inc(fq_step, 1)
                    dve.wait_ge(fq_step, 3 * t + 3)
                    v.tensor_scalar(qk2[:, b, 0:C], qk2[:, b, 0:C], fq[:, b:b + 1], None, ALU.mult).then_inc(q2f_ready, 1)

                stats(0, 0, 0)
                stats(1, 1, 0)
                norm(0, 0, first=True)
                stats(2, 0, 1)
                norm(1, 1, first=True)
                scale(0, 0)
                with dve.Fori(1, T // 2) as u:
                    stats(2 * u + 1, 1, u)
                    norm(2 * u, 0)
                    scale(2 * u - 1, 1)
                    stats(2 * u + 2, 0, u + 1)
                    norm(2 * u + 1, 1)
                    scale(2 * u, 0)
                norm(T - 1, 0)
                scale(T - 2, 1)
                scale(T - 1, 0)

            @block.tensor
            def _(pe):
                te = nc.tensor

                def project(t, b, first=False):
                    pe.wait_ge(xn_ready, t + 1)
                    if not first:
                        pe.wait_ge(xnT_stored, t - 1)
                    for c in range(CB):
                        mm = te.transpose(ps[:, b, c * P:(c + 1) * P], xn[:, b, c * P:(c + 1) * P], ident[:, :])
                    mm.then_inc(xn_turned, 1)
                    pe.wait_ge(xnT_stored, t + 1)
                    if not first:
                        pe.wait_ge(sq_ready, 2 * t - 2)
                    te.matmul(ps[:, 2 + b, :], lhsT=row0[:, :], rhs=bqk, start=True, stop=False)
                    for c in range(CB):
                        mm = te.matmul(ps[:, 2 + b, :], lhsT=xt_now[:, b, c, :], rhs=wqk[:, c, :],
                                       start=False, stop=(c == CB - 1))
                    mm.then_inc(qk_ready, 1)

                def gather(t, b, rows=P, first=False):
                    pe.wait_ge(k2n_ready, t + 1)
                    for c in range(CB):
                        te.matmul(ps[:, 4 + c, 0:C + 2], lhsT=k2n[0:rows, b, c * P:(c + 1) * P],
                                  rhs=xn[0:rows, b, :], start=False, stop=False, skip_group_check=True)
                    pe.wait_ge(k4_ready, 2 * t + 2)
                    for c in range(CB):
                        mm = te.matmul(ps[:, 6, c:c + 1], lhsT=k4[0:rows, c * P:(c + 1) * P],
                                       rhs=ones[0:rows, 0:1], start=False, stop=False, skip_group_check=True)
                    mm.then_inc(kx_done, 1)
                    pe.wait_ge(q2f_ready, t + 1)
                    if not first:
                        pe.wait_ge(q2T_stored, t - 1)
                    for c in range(CB):
                        mm = te.transpose(ps[:, 7, (b * CB + c) * P:(b * CB + c + 1) * P],
                                          qk2[:, b, c * P:(c + 1) * P], ident[:, :])
                    mm.then_inc(q2_turned, 1)

                pe.wait_ge(xn_ready, 1)
                for c in range(CB):
                    te.matmul(ps[:, 4 + c, 0:C + 2], lhsT=zeros[:, :], rhs=xn[:, 0, :], start=True, stop=False,
                              skip_group_check=True)
                te.matmul(ps[:, 6, 0:CB], lhsT=zeros[:, :], rhs=ones[:, 0:CB], start=True, stop=False,
                          skip_group_check=True)
                project(0, 0, first=True)
                project(1, 1, first=True)
                gather(0, 0, first=True)
                with pe.Fori(1, T // 2) as u:
                    project(2 * u, 0)
                    gather(2 * u - 1, 1)
                    project(2 * u + 1, 1)
                    gather(2 * u, 0)
                project(T - 1, 0)
                gather(T - 2, 1)
                gather(T - 1, 0, rows=LAST)

            @block.scalar
            def _(act):
                a = nc.scalar

                def std(t, b):
                    act.wait_ge(ln_step, 2 * t + 2)
                    a.activation(rstd[:, b:b + 1], mv[:, b, 1:2], ACT.Sqrt, bias=eps[:, 0:1]).then_inc(std_ready, 1)

                def keep(t, b, u=None):
                    act.wait_ge(xn_turned, t + 1)
                    if u is not None:
                        act.wait_ge(qk_ready, t - 1)
                        act.wait_ge(x_out[b], 16 * u)
                    a.copy(xt_now[:, b].rearrange("p a b -> p (a b)"), ps[:, b, 0:C]).then_inc(xnT_stored, 1)

                def squares(t, b, first=False):
                    act.wait_ge(qk_ready, t + 1)
                    if not first:
                        act.wait_ge(q2_turned, t - 1)
                        act.wait_ge(k2n_ready, t - 1)
                    for h in range(2):
                        a.activation(qk2[:, b, h * C:(h + 1) * C], ps[:, 2 + b, h * C:(h + 1) * C], ACT.Square,
                                     accum_out=sums[:, b, h:h + 1]).then_inc(sq_ready, 1)

                def norms(t, b, first=False):
                    act.wait_ge(recip_ready, 2 * t + 2)
                    a.activation(square, qk2[:, b, 0:C], ACT.Square, scale=rqk[:, b, 0:1],
                                 accum_out=nq[:, b:b + 1]).then_inc(k4_ready, 1)
                    act.wait_ge(k4_ready, 2 * t + 1)
                    a.activation(nq[:, b:b + 1], nq[:, b:b + 1], ACT.Sqrt).then_inc(nq_root, 1)
                    if not first:
                        act.wait_ge(kx_done, t)
                    a.activation(k4, qk2[:, b, C:2 * C], ACT.Square, scale=rqk[:, b, 1:2]).then_inc(k4_ready, 1)

                def turned(t, b, u=None):
                    act.wait_ge(q2_turned, t + 1)
                    if u is not None:
                        act.wait_ge(q_out[b], 16 * u)
                    a.copy(q2t_now[:, b].rearrange("p a b -> p (a b)"),
                           ps[:, 7, b * C:(b + 1) * C]).then_inc(q2T_stored, 1)

                std(0, 0)
                std(1, 1)
                keep(0, 0)
                squares(0, 0, first=True)
                std(2, 0)
                keep(1, 1)
                norms(0, 0, first=True)
                squares(1, 1, first=True)
                turned(0, 0)
                for t in (2, 3):
                    std(t + 1, 1 - t % 2)
                    keep(t, t % 2, 1)
                    norms(t - 1, (t - 1) % 2)
                    squares(t, t % 2)
                    turned(t - 1, (t - 1) % 2, None if t == 2 else 1)
                with act.Fori(2, T // 2) as u:
                    for b in range(2):
                        std(2 * u + b + 1, 1 - b)
                        keep(2 * u + b, b, u)
                        norms(2 * u + b - 1, 1 - b)
                        squares(2 * u + b, b)
                        turned(2 * u + b - 1, 1 - b, u - 1 + b)
                keep(T - 1, 0, T // 2)
                norms(T - 2, 1)
                squares(T - 1, 0)
                turned(T - 2, 1, T // 2 - 1)
                norms(T - 1, 0)
                turned(T - 1, 0, T // 2)

        with ExitStack() as stage:
            take = carve(big_f)
            kx = take([P, CB, C + 2])
            kxT = take([P, CB, CB, P])
            rn = take([P, CB])
            mp = take([P, CB, C])
            sums_kept, sums_turned, sumsT_kept = sem("sums_kept"), sem("sums_turned"), sem("sumsT_kept")
            m_ready, rn_step, m_kept, rn_root = sem("m_ready"), sem("rn_step"), sem("m_kept"), sem("rn_root")
            block = stage.enter_context(nc.Block())

            @block.scalar
            def _(act):
                nc.scalar.activation(rn, ps[:, 6, 0:CB], ACT.Sqrt).then_inc(rn_root, 1)

            @block.vector
            def _(dve):
                v = nc.vector
                v.tensor_copy(kx, ps[:, 4:6, 0:C + 2]).then_inc(sums_kept, 1)
                dve.wait_ge(rn_root, 1)
                v.tensor_scalar(rn, rn, 1e-12, None, ALU.max).then_inc(rn_step, 1)
                dve.wait_ge(rn_step, 1)
                v.reciprocal(rn, rn).then_inc(rn_step, 1)
                dve.wait_ge(rn_step, 2)
                v.tensor_scalar(rn, rn, float(N) ** -0.5, None, ALU.mult).then_inc(rn_step, 1)
                dve.wait_ge(sums_turned, 1)
                v.tensor_copy(kxT.rearrange("p a b c -> p (a b c)"), ps[:, 0, :]).then_inc(sumsT_kept, 1)
                dve.wait_ge(m_ready, 1)
                dve.wait_ge(rn_step, 3)
                dve.wait_ge(sums_kept, 1)
                for c in range(CB):
                    v.scalar_tensor_tensor(out=mp[:, c, :], in0=bvw, scalar=kx[:, c, C:C + 1],
                                           in1=ps[:, 1, c * C:(c + 1) * C], op0=ALU.mult, op1=ALU.add).then_inc(m_kept, 1)
                dve.wait_ge(m_kept, CB)
                for c in range(CB):
                    v.tensor_scalar(mkv[:, c, :], mp[:, c, :], rn[:, c:c + 1], None, ALU.mult)

            @block.tensor
            def _(pe):
                te = nc.tensor
                pe.wait_ge(sums_kept, 1)
                for i in range(CB):
                    for c in range(CB):
                        mm = te.transpose(ps[:, 0, (i * CB + c) * P:(i * CB + c + 1) * P],
                                          kx[:, c, i * P:(i + 1) * P], ident[:, :])
                mm.then_inc(sums_turned, 1)
                pe.wait_ge(sumsT_kept, 1)
                for c in range(CB):
                    for i in range(CB):
                        mm = te.matmul(ps[:, 1, c * C:(c + 1) * C], lhsT=kxT[:, i, c, :], rhs=wvo[:, i, :],
                                       start=(i == 0), stop=(i == CB - 1))
                mm.then_inc(m_ready, 1)

        with ExitStack() as stage:
            take = carve(big_f)
            NB = 4
            xt_in = take([P, NB, 2, C])
            xr = take([P, NB, C])
            base = take([P, NB, C])
            t_loaded = [sem(f"t_loaded{b}") for b in range(NB)]
            base_out = [sem(f"base_out{b}") for b in range(NB)]
            mixed, xb_ready, base_ready = sem("mixed"), sem("xb_ready"), sem("base_ready")
            block = stage.enter_context(nc.Block())
            R = T // NB

            @block.sync
            def _(sp):
                def load(t, b, first=False, rows=P):
                    if not first:
                        sp.wait_ge(base_ready, t - NB + 1)
                    sp.dma_start(xt_in[:, b, :, :], xT_dram[bass.ds(t, 1)].rearrange("t h p n -> (t p) h n")
                                 ).then_inc(t_loaded[b], 16)
                    sp.dma_start(xr[0:rows, b, :], x[bass.ds(t * P, rows), :]).then_inc(t_loaded[b], 16)

                for b in range(NB):
                    load(b, b, first=True)
                with sp.Fori(1, R) as u:
                    for b in range(NB):
                        load(NB * u + b, b)
                load(T - 1, 0, rows=LAST)

            @block.gpsimd
            def _(pool):
                def add_bias(b, n):
                    pool.wait_ge(t_loaded[b], n)
                    nc.gpsimd.tensor_tensor(xr[:, b, :], xr[:, b, :], bvo, ALU.add).then_inc(xb_ready, 1)

                with pool.Fori(0, R) as u:
                    for b in range(NB):
                        add_bias(b, 32 * u + 32)
                add_bias(0, 32 * R + 32)

            @block.tensor
            def _(pe):
                te = nc.tensor

                def mix(t, b, n, first=False):
                    pe.wait_ge(t_loaded[b], n)
                    if not first:
                        pe.wait_ge(base_ready, t - NB + 1)
                    for h, w in ((0, wvo), (1, mkv)):
                        for c in range(CB):
                            mm = te.matmul(ps[:, b, 0:C], lhsT=xt_in[:, b, h, c * P:(c + 1) * P], rhs=w[:, c, :],
                                           start=(h == 0 and c == 0), stop=(h == 1 and c == 1))
                    mm.then_inc(mixed, 1)

                for b in range(NB):
                    mix(b, b, 32, first=True)
                with pe.Fori(1, R) as u:
                    for b in range(NB):
                        mix(NB * u + b, b, 32 * u + 32)
                mix(T - 1, 0, 32 * R + 32)

            @block.vector
            def _(dve):
                def add(t, b, n=None):
                    dve.wait_ge(mixed, t + 1)
                    dve.wait_ge(xb_ready, t + 1)
                    if n is not None:
                        dve.wait_ge(base_out[b], n)
                    nc.vector.tensor_tensor(base[:, b, :], ps[:, b, 0:C], xr[:, b, :], ALU.add).then_inc(base_ready, 1)

                for b in range(NB):
                    add(b, b)
                with dve.Fori(1, R) as u:
                    for b in range(NB):
                        add(NB * u + b, b, 16 * u)
                add(T - 1, 0, 16 * R)

            @block.scalar
            def _(act):
                def store(t, b):
                    act.wait_ge(base_ready, t + 1)
                    act.dma_start(base_dram[bass.ds(t * P, P), :], base[:, b, :]).then_inc(base_out[b], 16)

                with act.Fori(0, R) as u:
                    for b in range(NB):
                        store(NB * u + b, b)
                store(T - 1, 0)
                for b in range(NB):
                    act.wait_ge(base_out[b], 16 * (R + (b == 0)))

        RING = 4
        with ExitStack() as stage:
            take = carve(big_f[:, T * C:])
            hot_hi = take([P, RING, CHUNKS, KC], F16)
            hot_lo = take([P, RING, CHUNKS, P], F16)
            iota_hi = take([P, KC], F16)
            iota_lo = take([P, P], F16)
            agg = take([P, 2, C])
            low = take([P, 2, C])
            aggT = take([P, 2, CB, P])
            zb = take([P, 2, C])
            iotas_ready = sem("l1_iotas_ready")
            hot_ready, built, at_stored = sem("hot_ready"), sem("built"), sem("at_stored")
            at_out = [sem("at_out0"), sem("at_out1")]
            summed, low_ready, agg_ready = sem("summed"), sem("low_ready"), sem("agg_ready")
            agg_turned, aggT_ready, multiplied = sem("agg_turned"), sem("aggT_ready"), sem("multiplied")
            zb_ready, z_ready, max_done = sem("zb_ready"), sem("z_ready"), sem("max_done")
            block = stage.enter_context(nc.Block())

            @block.gpsimd
            def _(pool):
                nc.gpsimd.iota(iota_hi, [[1, KC]], base=0, channel_multiplier=0, allow_small_or_imprecise_dtypes=True)
                nc.gpsimd.iota(iota_lo, [[1, P]], base=1, channel_multiplier=0,
                               allow_small_or_imprecise_dtypes=True).then_inc(iotas_ready, 1)

            @block.vector
            def _(dve):
                v = nc.vector
                dve.wait_ge(iotas_ready, 1)

                def hots(t, i, first=False):
                    w, s = t * WPT + i, i % RING
                    if not first:
                        dve.wait_ge(built, w - RING + 1)
                    for c in range(CHUNKS):
                        v.tensor_scalar(hot_hi[:, s, c, :], iota_hi, key_hi[:, bass.ds(w, 1), c], None, ALU.is_equal)
                        last = v.tensor_scalar(hot_lo[:, s, c, :], iota_lo, key_lo[:, bass.ds(w, 1), c], None,
                                               ALU.is_equal)
                    last.then_inc(hot_ready, 1)

                def gather(t, b, first=False):
                    dve.wait_ge(low_ready, t + 1)
                    if not first:
                        dve.wait_ge(agg_turned, t - 1)
                    v.tensor_tensor(agg[:, b, :], ps[:, 4 + b, 0:C], low[:, b, :], ALU.add).then_inc(agg_ready, 1)

                def bias(t, b, first=False):
                    dve.wait_ge(multiplied, t + 1)
                    if not first:
                        dve.wait_ge(z_ready, t - 1)
                    v.scalar_tensor_tensor(out=zb[:, b, :], in0=ps[:, 7, b * C:(b + 1) * C],
                                           scalar=dun[:, bass.ds(t, 1)], in1=b1b[:, :],
                                           op0=ALU.mult, op1=ALU.add).then_inc(zb_ready, 1)

                def largest(t):
                    dve.wait_ge(z_ready, t + 1)
                    v.tensor_reduce(tmax[:, bass.ds(t, 1)], z1s[:, bass.ds(t, 1), :].rearrange("p t c -> p (t c)"),
                                    AX.X, ALU.max)

                def tile(t, b, last=False, early=False):
                    for i in range(WPT):
                        if not last:
                            hots(t + 1, i)
                        if i == 3:
                            gather(t - 1, 1 - b, first=early)
                        if i == 7:
                            bias(t - 1, 1 - b, first=early)
                        if i == 11:
                            largest(t - 1)

                for i in range(WPT):
                    hots(0, i, first=(i < RING))
                for i in range(WPT):
                    hots(1, i)
                tile(1, 1, early=True)
                tile(2, 0, early=True)
                with dve.Fori(1, T // 2 - 1) as u:
                    tile(2 * u + 1, 1)
                    tile(2 * u + 2, 0)
                tile(T - 2, 1)
                tile(T - 1, 0, last=True)
                gather(T - 1, 0)
                bias(T - 1, 0)
                largest(T - 1)

            @block.tensor
            def _(pe):
                te = nc.tensor

                def build(t, i, b, first=False):
                    w, s, pair = t * WPT + i, i % RING, (i // 2) % 2
                    pe.wait_ge(hot_ready, w + 1)
                    if i % 2 == 0 and not first:
                        pe.wait_ge(at_stored, t * (WPT // 2) + i // 2 - 1)
                    for c in range(CHUNKS):
                        mm = te.matmul(ps[:, 2 * pair + i % 2, 0:KC], lhsT=hot_lo[:, s, c, :], rhs=hot_hi[:, s, c, :],
                                       start=(c == 0), stop=(c == CHUNKS - 1))
                    mm.then_inc(built, 1)

                def aggregate(t, b, ks, first=False):
                    for k in ks:
                        if k == 0:
                            pe.wait_ge(at_stored, (t + 1) * (WPT // 2))
                            if not first:
                                pe.wait_ge(agg_ready, t - 1)
                        te.matmul(ps[:, 4 + b, :], lhsT=at[:, b, k * P:(k + 1) * P], rhs=hs[:, k, :],
                                  start=(k == 0), stop=False)
                        if k == T - 1:
                            te.matmul(ps[:, 4 + b, :], lhsT=ident16[:, :],
                                      rhs=hs[:, bass.ds(t, 1), :].rearrange("p t c -> p (t c)"),
                                      start=False, stop=True).then_inc(summed, 1)

                def turn(t, b):
                    pe.wait_ge(agg_ready, t + 1)
                    for c in range(CB):
                        mm = te.transpose(ps[:, 6, (b * CB + c) * P:(b * CB + c + 1) * P],
                                          agg[:, b, c * P:(c + 1) * P], ident[:, :])
                    mm.then_inc(agg_turned, 1)

                def multiply(t, b):
                    pe.wait_ge(aggT_ready, t + 1)
                    for c in range(CB):
                        mm = te.matmul(ps[:, 7, b * C:(b + 1) * C], lhsT=aggT[:, b, c, :], rhs=w1[:, c, :],
                                       start=(c == 0), stop=(c == CB - 1))
                    mm.then_inc(multiplied, 1)

                def tile(t, b, first=False, last=False, early=False):
                    for i in range(WPT):
                        if not last:
                            build(t + 1, i, 1 - b)
                        aggregate(t, b, range(i * T // WPT, (i + 1) * T // WPT), first=early)
                        if i == 5 and not first:
                            turn(t - 1, 1 - b)
                        if i == 7 and not first:
                            multiply(t - 1, 1 - b)

                for i in range(WPT):
                    build(0, i, 0, first=(i < 4))
                tile(0, 0, first=True, early=True)
                tile(1, 1, early=True)
                tile(2, 0)
                with pe.Fori(1, T // 2 - 1) as u:
                    tile(2 * u + 1, 1)
                    tile(2 * u + 2, 0)
                tile(T - 2, 1)
                tile(T - 1, 0, last=True)
                turn(T - 1, 0)
                multiply(T - 1, 0)

            @block.scalar
            def _(act):
                a = nc.scalar

                def store(t, m, b, n=None):
                    act.wait_ge(built, t * WPT + 2 * m + 2)
                    if m == 0 and n is not None:
                        act.wait_ge(summed, t - 1)
                        act.wait_ge(at_out[b], n)
                    pair = m % 2
                    to = at[:, b, :].rearrange("p (k i j) -> p i k j", i=WPT, j=WIN)[:, 2 * m:2 * m + 2]
                    a.copy(to, ps[:, 2 * pair:2 * pair + 2, 0:KC].rearrange("p i (k j) -> p i k j", j=WIN)
                           ).then_inc(at_stored, 1)

                def lows(t, b, first=False):
                    act.wait_ge(summed, t + 1)
                    if not first:
                        act.wait_ge(agg_ready, t - 1)
                    a.copy(low[:, b, :], ps[:, 4 + b, C:2 * C]).then_inc(low_ready, 1)

                def keep(t, b, first=False):
                    act.wait_ge(agg_turned, t + 1)
                    if not first:
                        act.wait_ge(multiplied, t - 1)
                    a.copy(aggT[:, b].rearrange("p a b -> p (a b)"), ps[:, 6, b * C:(b + 1) * C]).then_inc(aggT_ready, 1)

                def relu(t, b):
                    act.wait_ge(zb_ready, t + 1)
                    a.activation(z1s[:, bass.ds(t, 1), :].rearrange("p t c -> p (t c)"), zb[:, b, :], ACT.Relu,
                                 scale=dinv[:, bass.ds(t, 1)]).then_inc(z_ready, 1)

                def tile(t, b, n, first=False, early=False, last=False):
                    for m in range(WPT // 2):
                        if not last:
                            store(t + 1, m, 1 - b, n)
                        if first:
                            continue
                        if m == 0:
                            lows(t - 1, 1 - b, first=early)
                        if m == 2:
                            keep(t - 1, 1 - b, first=early)
                        if m == 4:
                            relu(t - 1, 1 - b)

                for m in range(WPT // 2):
                    store(0, m, 0)
                tile(0, 0, None, first=True)
                tile(1, 1, 16, early=True)
                tile(2, 0, 16, early=True)
                with act.Fori(1, T // 2 - 1) as u:
                    tile(2 * u + 1, 1, 16 * u + 16)
                    tile(2 * u + 2, 0, 16 * u + 16)
                tile(T - 2, 1, 16 * (T // 2))
                tile(T - 1, 0, None, last=True)
                lows(T - 1, 0)
                keep(T - 1, 0)
                relu(T - 1, 0)

            @block.sync
            def _(sp):
                def out_at(t, b):
                    sp.wait_ge(at_stored, (t + 1) * (WPT // 2))
                    sp.dma_start(at_dram[bass.ds(t, 1)].rearrange("t p n -> (t p) n"), at[:, b, :]).then_inc(at_out[b], 16)

                with sp.Fori(0, T // 2) as u:
                    out_at(2 * u, 0)
                    out_at(2 * u + 1, 1)
                out_at(T - 1, 0)
                sp.wait_ge(at_out[0], 16 * (T // 2 + 1))
                sp.wait_ge(at_out[1], 16 * (T // 2))

        with ExitStack() as stage:
            max_step, all_max = sem("max_step"), sem("all_max")
            block = stage.enter_context(nc.Block())
            EXP = 0x7F800000

            @block.vector
            def _(dve):
                v = nc.vector
                v.tensor_reduce(small[:, 2:3], tmax[:, :], AX.X, ALU.max).then_inc(max_step, 1)
                dve.wait_ge(all_max, 1)
                v.tensor_scalar(small[:, 4:5], small[:, 3:4], 1e-30, None, ALU.max).then_inc(max_step, 1)
                dve.wait_ge(max_step, 2)
                v.tensor_scalar(small[:, 5:6].bitcast(I32), small[:, 4:5].bitcast(I32), EXP, None, ALU.bitwise_and)
                v.tensor_scalar(small[:, 6:7].bitcast(I32), small[:, 4:5].bitcast(I32), EXP, EXP,
                                ALU.bitwise_and, ALU.bitwise_xor).then_inc(max_step, 1)
                dve.wait_ge(max_step, 3)
                v.tensor_scalar(small[:, 7:8], small[:, 6:7], 2.0 ** 13, None, ALU.mult)
                v.tensor_scalar(small[:, 8:9], small[:, 5:6], 2.0 ** -14, None, ALU.mult).then_inc(max_step, 1)
                dve.wait_ge(max_step, 4)
                v.tensor_scalar(dun[:, :], dinv[:, :], small[:, 8:9], None, ALU.mult)

            @block.gpsimd
            def _(pool):
                pool.wait_ge(max_step, 1)
                nc.gpsimd.partition_all_reduce(small[:, 3:4], small[:, 2:3], P, RMAX).then_inc(all_max, 1)

        scale2 = small[:, 7:8]

        take = carve(key_lo[:, :, :].rearrange("p w c -> p (w c)"))
        s_sum = take([P, HB, C])
        w_sum = take([P, HB])
        w_acc = take([P, HB, P])
        with ExitStack() as stage:
            take = carve(big_f[:, T * C:])
            agg = take([P, 2, C])
            low = take([P, 2, C])
            aggT = take([P, 2, CB, P])
            zb = take([P, 2, C])
            base_in = take([P, 2, C])
            x1 = take([P, 2, C])
            xn2 = take([P, 2, C])
            xn2T = take([P, 2, CB, P])
            lg = take([P, 2, HEADS, D])
            ew = take([P, 2, HEADS, D])
            wt = take([P, 2, HB, P])
            hmax = take([P, 2, HEADS])
            hsum = take([P, 2, HEADS])
            st = take([P, 2, 6])
            mv = take([P, 2, 2])
            rstd = take([P, 2])
            hi_made, hs_made = sem("l2_hi_made"), sem("l2_hs_made")
            at_loaded, base_loaded = [sem(f"l2_at_loaded{b}") for b in range(2)], [sem(f"l2_base_loaded{b}") for b in range(2)]
            x1_out, w_out = [sem(f"x1_out{b}") for b in range(2)], [sem(f"w_out{b}") for b in range(2)]
            summed, low_ready, agg_ready = sem("l2_summed"), sem("l2_low_ready"), sem("l2_agg_ready")
            agg_turned, aggT_ready, multiplied = sem("l2_agg_turned"), sem("l2_aggT_ready"), sem("l2_multiplied")
            x1_ready, ln_step, xn2_ready = sem("x1_ready"), sem("l2_ln_step"), sem("xn2_ready")
            xn2_turned, xn2T_ready, logits_ready = sem("xn2_turned"), sem("xn2T_ready"), sem("logits_ready")
            shifted, exp_ready, soft_step, w_ready = sem("shifted"), sem("exp_ready"), sem("soft_step"), sem("w_ready")
            w_turned, wt_ready, w_added, s_added = sem("w_turned"), sem("wt_ready"), sem("w_added"), sem("s_added")
            zb_ready, std_ready, rstd_ready = sem("l2_zb_ready"), sem("l2_std_ready"), sem("l2_rstd_ready")
            s_kept = sem("s_kept")
            block = stage.enter_context(nc.Block())

            @block.sync
            def _(sp):
                def load(t, b, first=False):
                    if not first:
                        sp.wait_ge(summed, t - 1)
                        sp.wait_ge(x1_ready, t - 1)
                    sp.dma_start(at[:, b, :], at_dram[bass.ds(t, 1)].rearrange("t p n -> (t p) n")).then_inc(at_loaded[b], 16)
                    sp.dma_start(base_in[:, b, :], base_dram[bass.ds(t * P, P), :]).then_inc(base_loaded[b], 16)

                def store_x1(t, b):
                    sp.wait_ge(x1_ready, t + 1)
                    sp.dma_start(x1_dram[bass.ds(t * P, P), :], x1[:, b, :]).then_inc(x1_out[b], 16)

                def store_w(t, b):
                    sp.wait_ge(wt_ready, t + 1)
                    sp.dma_start(wT_dram[bass.ds(t, 1)].rearrange("t p n -> (t p) n"),
                                 wt[:, b].rearrange("p a b -> p (a b)")).then_inc(w_out[b], 16)

                load(0, 0, first=True)
                load(1, 1, first=True)
                store_x1(0, 0)
                with sp.Fori(1, T // 2) as u:
                    load(2 * u, 0)
                    store_x1(2 * u - 1, 1)
                    store_w(2 * u - 2, 0)
                    load(2 * u + 1, 1)
                    store_x1(2 * u, 0)
                    store_w(2 * u - 1, 1)
                load(T - 1, 0)
                store_x1(T - 2, 1)
                store_w(T - 3, 0)
                store_x1(T - 1, 0)
                store_w(T - 2, 1)
                store_w(T - 1, 0)
                for b, n in ((0, T // 2 + 1), (1, T // 2)):
                    sp.wait_ge(x1_out[b], 16 * n)
                    sp.wait_ge(w_out[b], 16 * n)

            @block.tensor
            def _(pe):
                te = nc.tensor

                def aggregate(t, b, ks, u, first=False):
                    for k in ks:
                        if k == 0:
                            pe.wait_ge(at_loaded[b], 16 * u + 16)
                            if not first:
                                pe.wait_ge(agg_ready, t - 1)
                        if first and b == 0:
                            pe.wait_ge(hs_made, k + 1)
                        te.matmul(ps[:, b, :], lhsT=at[:, b, k * P:(k + 1) * P], rhs=hs[:, k, :],
                                  start=(k == 0), stop=False)
                        if k == T - 1:
                            te.matmul(ps[:, b, :], lhsT=ident16[:, :],
                                      rhs=hs[:, bass.ds(t, 1), :].rearrange("p t c -> p (t c)"),
                                      start=False, stop=True).then_inc(summed, 1)

                def turn(t, b):
                    pe.wait_ge(agg_ready, t + 1)
                    for c in range(CB):
                        mm = te.transpose(ps[:, 2, c * P:(c + 1) * P], agg[:, b, c * P:(c + 1) * P], ident[:, :])
                    mm.then_inc(agg_turned, 1)

                def multiply(t, b):
                    pe.wait_ge(aggT_ready, t + 1)
                    for c in range(CB):
                        mm = te.matmul(ps[:, 3, 0:C], lhsT=aggT[:, b, c, :], rhs=w2[:, c, :],
                                       start=(c == 0), stop=(c == CB - 1))
                    mm.then_inc(multiplied, 1)

                def turn_x(t, b):
                    pe.wait_ge(xn2_ready, t + 1)
                    for c in range(CB):
                        mm = te.transpose(ps[:, 2, C + c * P:C + (c + 1) * P], xn2[:, b, c * P:(c + 1) * P], ident[:, :])
                    mm.then_inc(xn2_turned, 1)

                def logits(t, b):
                    pe.wait_ge(xn2T_ready, t + 1)
                    for c in range(CB):
                        mm = te.matmul(ps[:, 4, :], lhsT=xn2T[:, b, c, :], rhs=wlog[:, c, :],
                                       start=(c == 0), stop=(c == CB - 1))
                    mm.then_inc(logits_ready, 1)

                def weigh(t, b, rows=P, opening=False):
                    pe.wait_ge(w_ready, t + 1)
                    if not opening:
                        pe.wait_ge(wt_ready, t)
                    ewf = ew[:, b].rearrange("p h d -> p (h d)")
                    for p in range(HB):
                        mm = te.transpose(ps[:, 5, p * P:(p + 1) * P], ewf[:, p * P:(p + 1) * P], ident[:, :])
                    mm.then_inc(w_turned, 1)
                    for p in range(HB):
                        mm = te.matmul(ps[:, 6 + p // 2, (p % 2) * C:(p % 2 + 1) * C], lhsT=ewf[0:rows, p * P:(p + 1) * P],
                                       rhs=xn2[0:rows, b, :], start=False, stop=False, skip_group_check=True)
                    mm.then_inc(s_added, 1)

                def tile(t, b, u, first=False, early=False, second=False, opening=False):
                    n = 16
                    for i in range(n):
                        aggregate(t, b, range(i * T // n, (i + 1) * T // n), u, first=early)
                        if first:
                            continue
                        if i == 1 and not second:
                            weigh(t - 2, b, opening=opening)
                        if i == 3:
                            turn(t - 1, 1 - b)
                        if i == 5:
                            multiply(t - 1, 1 - b)
                        if i == 9:
                            turn_x(t - 1, 1 - b)
                        if i == 11:
                            logits(t - 1, 1 - b)

                for h in range(2):
                    te.matmul(ps[:, 6 + h, :], lhsT=zeros[:, :], rhs=wlog[:, 0, :], start=True, stop=False,
                              skip_group_check=True)
                tile(0, 0, 0, first=True, early=True)
                tile(1, 1, 0, early=True, second=True)
                tile(2, 0, 1, opening=True)
                tile(3, 1, 1)
                with pe.Fori(2, T // 2) as u:
                    tile(2 * u, 0, u)
                    tile(2 * u + 1, 1, u)
                tile(T - 1, 0, T // 2)
                weigh(T - 2, 1)
                turn(T - 1, 0)
                multiply(T - 1, 0)
                turn_x(T - 1, 0)
                logits(T - 1, 0)
                weigh(T - 1, 0, rows=LAST)

            @block.vector
            def _(dve):
                v = nc.vector

                with dve.Fori(0, T) as t:
                    dve.wait_ge(hi_made, t + 1)
                    z = z1s[:, bass.ds(t, 1), :].rearrange("p t c -> p (t c)")
                    v.scalar_tensor_tensor(out=hs[:, bass.ds(t, 1), C:2 * C].rearrange("p o c -> p (o c)"), in0=z,
                                           scalar=scale2, in1=hs[:, bass.ds(t, 1), 0:C].rearrange("p o c -> p (o c)"),
                                           op0=ALU.mult, op1=ALU.subtract).then_inc(hs_made, 1)

                def gather(t, b, first=False):
                    dve.wait_ge(low_ready, t + 1)
                    v.tensor_tensor(agg[:, b, :], ps[:, b, 0:C], low[:, b, :], ALU.add).then_inc(agg_ready, 1)

                def norm(t, b, u, first=False):
                    dve.wait_ge(multiplied, t + 1)
                    v.scalar_tensor_tensor(out=zb[:, b, :], in0=ps[:, 3, 0:C], scalar=dun[:, bass.ds(t, 1)],
                                           in1=b2b[:, :], op0=ALU.mult, op1=ALU.add).then_inc(zb_ready, 1)
                    dve.wait_ge(zb_ready, t + 1)
                    dve.wait_ge(base_loaded[b], 16 * u + 16)
                    if not first:
                        dve.wait_ge(x1_out[b], 16 * u)
                    v.scalar_tensor_tensor(out=x1[:, b, :], in0=zb[:, b, :], scalar=0.0, in1=base_in[:, b, :],
                                           op0=ALU.max, op1=ALU.add).then_inc(x1_ready, 1)
                    dve.wait_ge(x1_ready, t + 1)
                    v.bn_stats(st[:, b, :], x1[:, b, :]).then_inc(ln_step, 1)
                    dve.wait_ge(ln_step, 2 * t + 1)
                    v.memset(rstd[:, b:b + 1], 0.0)
                    v.bn_aggr(mv[:, b, :], st[:, b, :]).then_inc(ln_step, 1)
                    dve.wait_ge(std_ready, t + 1)
                    v.reciprocal(rstd[:, b:b + 1], rstd[:, b:b + 1]).then_inc(rstd_ready, 1)
                    dve.wait_ge(rstd_ready, t + 1)
                    if not first:
                        dve.wait_ge(s_added, t - 1)
                    v.tensor_scalar(xn2[:, b, :], x1[:, b, :], mv[:, b, 0:1], rstd[:, b:b + 1],
                                    ALU.subtract, ALU.mult).then_inc(xn2_ready, 1)

                def shift(t, b):
                    dve.wait_ge(logits_ready, t + 1)
                    v.tensor_tensor(lg[:, b].rearrange("p h d -> p (h d)"), ps[:, 4, :], blogb[:, :],
                                    ALU.add).then_inc(soft_step, 1)
                    dve.wait_ge(soft_step, 4 * t + 1)
                    v.tensor_reduce(hmax[:, b, :], lg[:, b], AX.X, ALU.max).then_inc(soft_step, 1)
                    dve.wait_ge(soft_step, 4 * t + 2)
                    v.tensor_tensor(lg[:, b], lg[:, b],
                                    hmax[:, b, :].rearrange("p (h o) -> p h o", o=1).to_broadcast([P, HEADS, D]),
                                    ALU.subtract).then_inc(shifted, 1)

                def divide(t, b):
                    dve.wait_ge(exp_ready, t + 1)
                    v.tensor_reduce(hsum[:, b, :], ew[:, b], AX.X, ALU.add).then_inc(soft_step, 1)
                    dve.wait_ge(soft_step, 4 * t + 3)
                    v.reciprocal(hsum[:, b, :], hsum[:, b, :]).then_inc(soft_step, 1)
                    dve.wait_ge(soft_step, 4 * t + 4)
                    v.tensor_tensor(ew[:, b], ew[:, b],
                                    hsum[:, b, :].rearrange("p (h o) -> p h o", o=1).to_broadcast([P, HEADS, D]),
                                    ALU.mult).then_inc(w_ready, 1)

                def rest(t, b, u, first=False):
                    gather(t, b)
                    norm(t, b, u, first)
                    shift(t, b)
                    divide(t, b)

                rest(0, 0, 0, first=True)
                rest(1, 1, 0, first=True)
                with dve.Fori(1, T // 2) as u:
                    rest(2 * u, 0, u)
                    rest(2 * u + 1, 1, u)
                rest(T - 1, 0, T // 2)
                dve.wait_ge(s_added, T)
                v.tensor_copy(s_sum.rearrange("p a b -> p (a b)"), ps[:, 6:8, :].rearrange("p a b -> p (a b)"))

            @block.scalar
            def _(act):
                a = nc.scalar
                with act.Fori(0, T) as t:
                    z = z1s[:, bass.ds(t, 1), :].rearrange("p t c -> p (t c)")
                    a.activation(hs[:, bass.ds(t, 1), 0:C].rearrange("p o c -> p (o c)"), z, ACT.Identity,
                                 scale=scale2).then_inc(hi_made, 1)

                def rest(t, b, u, first=False):
                    act.wait_ge(summed, t + 1)
                    a.copy(low[:, b, :], ps[:, b, C:2 * C]).then_inc(low_ready, 1)
                    act.wait_ge(agg_turned, t + 1)
                    a.copy(aggT[:, b].rearrange("p a b -> p (a b)"), ps[:, 2, 0:C]).then_inc(aggT_ready, 1)
                    act.wait_ge(ln_step, 2 * t + 2)
                    a.activation(rstd[:, b:b + 1], mv[:, b, 1:2], ACT.Sqrt, bias=eps[:, 0:1]).then_inc(std_ready, 1)
                    act.wait_ge(xn2_turned, t + 1)
                    a.copy(xn2T[:, b].rearrange("p a b -> p (a b)"), ps[:, 2, C:2 * C]).then_inc(xn2T_ready, 1)
                    act.wait_ge(shifted, t + 1)
                    a.activation(ew[:, b], lg[:, b], ACT.Exp).then_inc(exp_ready, 1)

                def turned(t, b, n=None):
                    act.wait_ge(w_turned, t + 1)
                    if n is not None:
                        act.wait_ge(w_out[b], n)
                        act.wait_ge(w_added, t - 1)
                    a.copy(wt[:, b].rearrange("p a b -> p (a b)"), ps[:, 5, :]).then_inc(wt_ready, 1)

                rest(0, 0, 0, first=True)
                rest(1, 1, 0, first=True)
                turned(0, 0)
                rest(2, 0, 1)
                turned(1, 1)
                rest(3, 1, 1)
                with act.Fori(2, T // 2) as u:
                    turned(2 * u - 2, 0, 16 * u - 16)
                    rest(2 * u, 0, u)
                    turned(2 * u - 1, 1, 16 * u - 16)
                    rest(2 * u + 1, 1, u)
                turned(T - 3, 0, 16 * (T // 2) - 16)
                rest(T - 1, 0, T // 2)
                turned(T - 2, 1, 16 * (T // 2) - 16)
                turned(T - 1, 0, 16 * (T // 2))

            @block.gpsimd
            def _(pool):
                g = nc.gpsimd
                g.memset(w_acc, 0.0).then_inc(s_kept, 1)
                pool.wait_ge(s_kept, 1)

                def add(t, b, rows=P):
                    pool.wait_ge(wt_ready, t + 1)
                    g.tensor_tensor(w_acc[:, :, 0:rows], w_acc[:, :, 0:rows], wt[:, b, :, 0:rows],
                                    ALU.add).then_inc(w_added, 1)
                    pool.wait_ge(w_added, t + 1)

                with pool.Fori(0, T // 2) as u:
                    add(2 * u, 0)
                    add(2 * u + 1, 1)
                add(T - 1, 0, rows=LAST)

        fin = life.enter_context(ExitStack())
        take = carve(big_f)
        pmat = take([P, HB, C])
        bfb = take([P, C])
        final_rest = big_f[:, HB * C + C:]
        with ExitStack() as stage:
            take = carve(final_rest)
            wfx = take([P, CB, HG])
            wfo = take([P, HB, C])
            bfx = take([P, HG])
            bdq = take([P, P])
            bdk = take([P, P])
            bdv = take([P, P])
            sT = take([P, CB, HB, P])
            tok = take([P, HB, P])
            tokT = take([P, HB, P])
            qT = take([P, HB, P])
            kT = take([P, HB, P])
            vv = take([P, HB, P])
            sc = take([P, HB, D])
            at_w = take([P, HB, P])
            atT = take([P, HB, P])
            oT = take([P, HB, P])
            smax = take([P, HB])
            ssum = take([P, HB])
            wrec = take([P, HB])
            tmp = take([P, D])
            zeroed, loaded = sem("f_zeroed"), sem("f_loaded")
            pe_step, dve_step, act_step = sem("f_pe_step"), sem("f_dve_step"), sem("f_act_step")
            block = stage.enter_context(nc.Block())

            @block.gpsimd
            def _(pool):
                for z in (bdq, bdk, bdv, tok):
                    last = nc.gpsimd.memset(z, 0.0)
                last = nc.gpsimd.memset(at_w, 0.0)
                last.then_inc(zeroed, 1)

            @block.sync
            def _(sp):
                sp.dma_start(wfx, W_fx.rearrange("(b p) n -> p b n", p=P)).then_inc(loaded, 16)
                sp.dma_start(wfo, W_fo.rearrange("(b p) n -> p b n", p=P)).then_inc(loaded, 16)
                sp.dma_start(bfx, b_fx.rearrange("(a n) -> a n", a=1).to_broadcast([P, HG])).then_inc(loaded, 16)
                sp.dma_start(bfb, b_fo.rearrange("(a n) -> a n", a=1).to_broadcast([P, C])).then_inc(loaded, 16)
                sp.wait_ge(zeroed, 1)
                for to, of in ((bdq, W_q), (bdk, W_k), (bdv, W_v)):
                    for h in range(2):
                        sp.dma_start(to[h * D:(h + 1) * D, h * D:(h + 1) * D], of).then_inc(loaded, 16)
                sp.wait_ge(loaded, 160)

            @block.tensor
            def _(pe):
                te = nc.tensor
                pe.wait_ge(loaded, 160)
                for i in range(CB):
                    for p in range(HB):
                        mm = te.transpose(ps[:, i, p * P:(p + 1) * P], s_sum[:, p, i * P:(i + 1) * P], ident[:, :])
                mm.then_inc(pe_step, 1)
                pe.wait_ge(act_step, 1)
                for p in range(HB):
                    for i in range(CB):
                        mm = te.matmul(ps[:, 2, p * P:(p + 1) * P], lhsT=sT[:, i, p, :], rhs=wfx[:, i, p * P:(p + 1) * P],
                                       start=(i == 0), stop=(i == CB - 1))
                mm.then_inc(pe_step, 1)
                pe.wait_ge(dve_step, 1)
                for p in range(HB):
                    mm = te.transpose(ps[:, 3, p * P:(p + 1) * P], tok[:, p, :], ident[:, :])
                mm.then_inc(pe_step, 1)
                pe.wait_ge(act_step, 2)
                for p in range(HB):
                    te.matmul(ps[:, 4, p * P:(p + 1) * P], lhsT=bdq, rhs=tokT[:, p, :], start=True, stop=True)
                for p in range(HB):
                    te.matmul(ps[:, 5, p * P:(p + 1) * P], lhsT=bdk, rhs=tokT[:, p, :], start=True, stop=True)
                for p in range(HB):
                    mm = te.matmul(ps[:, 6, p * P:(p + 1) * P], lhsT=tokT[:, p, :], rhs=bdv, start=True, stop=True)
                mm.then_inc(pe_step, 1)
                pe.wait_ge(act_step, 3)
                pe.wait_ge(dve_step, 2)
                for p in range(HB):
                    mm = te.matmul(ps[:, 7, p * P:(p + 1) * P], lhsT=qT[:, p, :], rhs=kT[:, p, :], start=True, stop=True)
                mm.then_inc(pe_step, 1)
                pe.wait_ge(dve_step, 4)
                for p in range(HB):
                    mm = te.transpose(ps[:, 0, p * P:(p + 1) * P], at_w[:, p, :], ident[:, :])
                mm.then_inc(pe_step, 1)
                pe.wait_ge(act_step, 5)
                for p in range(HB):
                    mm = te.matmul(ps[:, 1, p * P:(p + 1) * P], lhsT=vv[:, p, :], rhs=atT[:, p, :], start=True, stop=True)
                mm.then_inc(pe_step, 1)
                pe.wait_ge(act_step, 6)
                for p in range(HB):
                    mm = te.matmul(ps[:, 2 + p // 2, (p % 2) * C:(p % 2 + 1) * C], lhsT=oT[:, p, :], rhs=wfo[:, p, :],
                                   start=True, stop=True)
                mm.then_inc(pe_step, 1)

            @block.scalar
            def _(act):
                a = nc.scalar

                def flat(y):
                    return y.rearrange("p a b -> p (a b)")

                act.wait_ge(pe_step, 1)
                a.copy(sT.rearrange("p a b c -> p (a b c)"), ps[:, 0:2, :].rearrange("p a b -> p (a b)")).then_inc(act_step, 1)
                act.wait_ge(pe_step, 3)
                a.copy(flat(tokT), ps[:, 3, :]).then_inc(act_step, 1)
                act.wait_ge(pe_step, 4)
                a.mul(flat(qT), ps[:, 4, :], float(D) ** -0.5)
                a.copy(flat(vv), ps[:, 6, :]).then_inc(act_step, 1)
                act.wait_ge(dve_step, 3)
                a.activation(sc, sc, ACT.Exp).then_inc(act_step, 1)
                act.wait_ge(pe_step, 6)
                a.copy(flat(atT), ps[:, 0, :]).then_inc(act_step, 1)
                act.wait_ge(pe_step, 7)
                a.copy(flat(oT), ps[:, 1, :]).then_inc(act_step, 1)

            @block.vector
            def _(dve):
                v = nc.vector
                own = sem("f_own")
                n = [0]

                def step(ins):
                    n[0] += 1
                    ins.then_inc(own, 1)
                    dve.wait_ge(own, n[0])

                step(v.tensor_reduce(w_sum, w_acc, AX.X, ALU.add))
                step(v.tensor_scalar(wrec, w_sum, 1e-5, None, ALU.add))
                step(v.reciprocal(wrec, wrec))
                dve.wait_ge(pe_step, 2)
                dve.wait_ge(loaded, 160)
                dve.wait_ge(zeroed, 1)
                for p in range(HB):
                    for h in range(2):
                        r, c = slice(h * D, (h + 1) * D), slice((2 * p + h) * D, (2 * p + h + 1) * D)
                        v.scalar_tensor_tensor(out=tok[r, p, h * D:(h + 1) * D], in0=bfx[r, c], scalar=w_sum[r, p:p + 1],
                                               in1=ps[r, 2, c], op0=ALU.mult, op1=ALU.add).then_inc(own, 1)
                n[0] += 2 * HB
                dve.wait_ge(own, n[0])
                for p in range(HB):
                    last = v.tensor_scalar(tok[:, p, :], tok[:, p, :], wrec[:, p:p + 1], None, ALU.mult)
                last.then_inc(dve_step, 1)
                dve.wait_ge(pe_step, 4)
                v.tensor_copy(kT.rearrange("p a b -> p (a b)"), ps[:, 5, :]).then_inc(dve_step, 1)
                dve.wait_ge(pe_step, 5)
                for h in range(2):
                    r = slice(h * D, (h + 1) * D)
                    s = ps[r, 7, :].rearrange("p (a b) -> p a b", b=P)[:, :, h * D:(h + 1) * D]
                    step(v.tensor_reduce(smax[r, :], s, AX.X, ALU.max))
                    last = v.tensor_tensor(sc[r], s, smax[r, :].rearrange("p (a o) -> p a o", o=1)
                                           .to_broadcast([D, HB, D]), ALU.subtract)
                last.then_inc(dve_step, 1)
                dve.wait_ge(act_step, 4)
                step(v.tensor_reduce(ssum, sc, AX.X, ALU.add))
                step(v.reciprocal(ssum, ssum))
                for h in range(2):
                    r = slice(h * D, (h + 1) * D)
                    last = v.tensor_tensor(at_w[r, :, h * D:(h + 1) * D], sc[r],
                                           ssum[r, :].rearrange("p (a o) -> p a o", o=1).to_broadcast([D, HB, D]), ALU.mult)
                last.then_inc(dve_step, 1)
                dve.wait_ge(pe_step, 8)
                v.tensor_copy(pmat.rearrange("p a b -> p (a b)"), ps[:, 2:4, :].rearrange("p a b -> p (a b)"))

        with ExitStack() as stage:
            take = carve(final_rest)
            NB = 4
            w_in = take([P, NB, HB, P])
            x1_in = take([P, NB, C])
            res = take([P, NB, C])
            t_loaded = [sem(f"o_loaded{b}") for b in range(NB)]
            res_out = [sem(f"o_out{b}") for b in range(NB)]
            mixed, xb_ready, res_ready = sem("o_mixed"), sem("o_xb_ready"), sem("o_ready")
            block = stage.enter_context(nc.Block())
            R = T // NB

            @block.sync
            def _(sp):
                def load(t, b, first=False):
                    if not first:
                        sp.wait_ge(res_ready, t - NB + 1)
                    sp.dma_start(w_in[:, b].rearrange("p a b -> p (a b)"),
                                 wT_dram[bass.ds(t, 1)].rearrange("t p n -> (t p) n")).then_inc(t_loaded[b], 16)
                    sp.dma_start(x1_in[:, b, :], x1_dram[bass.ds(t * P, P), :]).then_inc(t_loaded[b], 16)

                for b in range(NB):
                    load(b, b, first=True)
                with sp.Fori(1, R) as u:
                    for b in range(NB):
                        load(NB * u + b, b)
                load(T - 1, 0)

            @block.gpsimd
            def _(pool):
                def add_bias(b, n):
                    pool.wait_ge(t_loaded[b], n)
                    nc.gpsimd.tensor_tensor(x1_in[:, b, :], x1_in[:, b, :], bfb, ALU.add).then_inc(xb_ready, 1)

                with pool.Fori(0, R) as u:
                    for b in range(NB):
                        add_bias(b, 32 * u + 32)
                add_bias(0, 32 * R + 32)

            @block.tensor
            def _(pe):
                te = nc.tensor

                def mix(t, b, n, first=False):
                    pe.wait_ge(t_loaded[b], n)
                    if not first:
                        pe.wait_ge(res_ready, t - NB + 1)
                    for p in range(HB):
                        mm = te.matmul(ps[:, b, 0:C], lhsT=w_in[:, b, p, :], rhs=pmat[:, p, :],
                                       start=(p == 0), stop=(p == HB - 1))
                    mm.then_inc(mixed, 1)

                for b in range(NB):
                    mix(b, b, 32, first=True)
                with pe.Fori(1, R) as u:
                    for b in range(NB):
                        mix(NB * u + b, b, 32 * u + 32)
                mix(T - 1, 0, 32 * R + 32)

            @block.vector
            def _(dve):
                def add(t, b, n=None):
                    dve.wait_ge(mixed, t + 1)
                    dve.wait_ge(xb_ready, t + 1)
                    if n is not None:
                        dve.wait_ge(res_out[b], n)
                    nc.vector.tensor_tensor(res[:, b, :], ps[:, b, 0:C], x1_in[:, b, :], ALU.add).then_inc(res_ready, 1)

                for b in range(NB):
                    add(b, b)
                with dve.Fori(1, R) as u:
                    for b in range(NB):
                        add(NB * u + b, b, 16 * u)
                add(T - 1, 0, 16 * R)

            @block.scalar
            def _(act):
                def store(t, b, rows=P):
                    act.wait_ge(res_ready, t + 1)
                    act.dma_start(out[bass.ds(t * P, rows), :], res[0:rows, b, :]).then_inc(res_out[b], 16)

                with act.Fori(0, R) as u:
                    for b in range(NB):
                        store(NB * u + b, b)
                store(T - 1, 0, rows=LAST)
                for b in range(NB):
                    act.wait_ge(res_out[b], 16 * (R + (b == 0)))


_INS = ['x', 'src', 'dst', 'L0_gnn_W1', 'L0_gnn_b1', 'L0_gnn_W2', 'L0_gnn_b2', 'L0_mix_W_qkv', 'L0_mix_b_qkv',
        'L0_mix_W_out', 'L0_mix_b_out', 'L0_ffn_W_fx', 'L0_ffn_b_fx', 'L0_ffn_W_x', 'L0_ffn_b_x', 'L0_ffn_W_slice',
        'L0_ffn_b_slice', 'L0_ffn_W_q', 'L0_ffn_W_k', 'L0_ffn_W_v', 'L0_ffn_W_out', 'L0_ffn_b_out',
        'L0_ffn_temperature']


def kernel(**inputs):
    import numpy as _np
    import concourse.bacc as _bacc
    from concourse import mybir as _mybir
    from concourse.bass_utils import run_bass_kernel_spmd as _run

    nc = _bacc.Bacc("TRN2", target_bir_lowering=False, num_devices=1)
    arrays, args = {}, []
    for name in _INS:
        a = _np.ascontiguousarray(inputs[name])
        arrays[f"in_{name}_dram"] = a
        args.append(nc.dram_tensor(f"in_{name}_dram", a.shape, _mybir.dt.from_np(a.dtype), kind="ExternalInput").ap())
    out = nc.dram_tensor("out_0_dram", inputs["x"].shape, _mybir.dt.float32, kind="ExternalOutput").ap()
    gps_layer(nc, *args, out)
    r = _run(nc, [arrays], core_ids=[0])
    return r.results[0]["out_0_dram"]
```

```python
from contextlib import ExitStack

import concourse.bass as bass
from concourse import mybir

ALU = mybir.AluOpType
ACT = mybir.ActivationFunctionType
F32 = mybir.dt.float32
F16 = mybir.dt.float16
I32 = mybir.dt.int32
AX = mybir.AxisListType
RMAX = bass.bass_isa.ReduceOp.max

P = 128


def divisor(n):
    return max(d for d in range(1, P + 1) if n % d == 0)


def reached(t, least):
    return not isinstance(t, int) or t >= least


def within(t, end):
    return not isinstance(t, int) or t < end


def pipeline(engine, body, tiles, unroll, lead=0, lag=0):
    for t in range(-lead, 2 * unroll):
        body(t, t % unroll, t // unroll)
    rounds = (tiles - 1) // unroll
    if rounds > 2:
        with engine.Fori(2, rounds) as u:
            for b in range(unroll):
                body(u * unroll + b, b, u)
    for t in range(max(rounds, 2) * unroll, tiles + lag):
        body(t, t % unroll, t // unroll)


def gps_layer(nc, x, src, dst, W1, b1, W2, b2, W_qkv, b_qkv, W_mo, b_mo,
              W_fx, b_fx, W_x, b_x, W_sl, b_sl, W_q, W_k, W_v, W_fo, b_fo, temp, out):
    N, C = x.shape
    E = src.shape[0]
    NT = 125
    T = N // NT
    WIN = 5
    WPT = NT // WIN
    NW = T * WPT
    CHUNKS = 2
    CAP = CHUNKS * P
    GW = 125
    G = NW // GW
    KC = T * WIN
    ROWL = divisor(E)
    ROWS = E // ROWL
    HP = divisor(ROWS)
    HC = ROWS // HP
    HEADS, D = 8, W_sl.shape[0]
    HG = HEADS * D
    CB = C // P
    HB = HG // P
    SH = 2048.0
    assert C == 256 and CB == 2 and D == 64 and HG == 512 and G * GW == NW and T * NT == N and T % 2 == 0
    assert 2 * KC <= 512 and E > CAP

    deg_dram = nc.dram_tensor("deg_scratch", (N,), F32, kind="Internal").ap()
    at_dram = nc.dram_tensor("at_scratch", (T, P, T * P), F16, kind="Internal").ap()
    base_dram = nc.dram_tensor("base_scratch", (N, C), F32, kind="Internal").ap()
    xT_dram = nc.dram_tensor("xT_scratch", (T, P, 2 * CB * NT), F32, kind="Internal").ap()
    wT_dram = nc.dram_tensor("wT_scratch", (T, P, HB * NT), F32, kind="Internal").ap()
    x1_dram = nc.dram_tensor("x1_scratch", (N, C), F32, kind="Internal").ap()
    h_dram = nc.dram_tensor("h_scratch", (N, C), F32, kind="Internal").ap()

    with ExitStack() as life:
        def sb(name, shape, dt=F32):
            return life.enter_context(nc.sbuf_tensor(name, shape, dt))

        def sem(name):
            return life.enter_context(nc.semaphore(name))

        def carve(region):
            at = [0]

            def take(shape, dt=F32):
                n = 1
                for s in shape[1:]:
                    n *= s
                words = n if dt in (F32, I32) else -(-n // 2)
                a = region[0:shape[0], at[0]:at[0] + words]
                at[0] += words
                assert at[0] <= region.shape[1], (at[0], region.shape)
                if dt != F32:
                    a = a.bitcast(dt)
                if dt == F16 and n % 2:
                    a = a[:, 0:n]
                if len(shape) == 3:
                    a = a.rearrange("p (a b) -> p a b", b=shape[2])
                if len(shape) == 4:
                    a = a.rearrange("p (a b c) -> p a b c", b=shape[2], c=shape[3])
                return a
            return take

        hs = sb("hs", [P, T, 2 * C], F16)
        big = sb("big", [P, 2 * T, C])
        key_lo = sb("key_lo", [P, NW, CHUNKS])
        key_hi = sb("key_hi", [P, NW, CHUNKS])
        at = sb("at", [P, 2, T * P], F16)
        ident = sb("ident", [P, P])
        ident16 = sb("ident16", [P, P], F16)
        w1 = sb("w1", [P, CB, C])
        wlog = sb("wlog", [P, CB, HG])
        b1b = sb("b1b", [P, C])
        blogb = sb("blogb", [P, HG])
        dinv = sb("dinv", [P, T])
        dsc = sb("dsc", [P, T])
        dun = sb("dun", [P, T])
        small = sb("small", [P, 24])
        eps = sb("eps", [P, 1])
        ps = life.enter_context(nc.psum_tensor("ps", [P, 8, 512], F32))

        at_f32 = at[:, :, :].rearrange("p a b -> p (a b)").bitcast(F32)
        big_f = big[:, :, :].rearrange("p a b -> p (a b)")
        hs_f32 = hs[:, :, :].rearrange("p a b -> p (a b)").bitcast(F32)
        z1s = big[:, 0:T, :]

        take = carve(at_f32)
        wqk = take([P, CB, 2 * C])
        bqk = take([P, 2 * C])
        wvo = take([P, CB, C])
        bvw = take([P, C])
        bvo = take([P, C])
        mkv = take([P, CB, C])
        AT_USED = 2 * CB * C + 2 * C + CB * C + 2 * C + CB * C

        ones = sb("ones", [P, 2])
        zeros = sb("zeros", [P, P])
        degT = sb("degT", [P, T])
        flag = sb("flag", [P, 1], I32)
        ident_sem = sem("ident_sem")

        with ExitStack() as stage:
            take = carve(big_f)
            heads = take([HP, HC], I32)
            heads_f = take([HP, HC])
            w_lo = take([HP, NW])
            past = take([HP, HC, NW], F16)
            wfirst = take([GW, G])
            rbase = take([GW, G])
            ridx_f = take([GW, G])
            ridx = take([GW, G], I32)
            cnt = take([GW, G])
            lo_f = take([GW, G])
            lo = take([GW, G], I32)
            srcg = take([GW, G, CAP], I32)
            dstg = take([GW, G, CAP], I32)
            dl = take([GW, G, CAP])
            tile_of = take([GW, G, CAP])
            tmp_f = take([GW, G, CAP])
            deg = take([GW, G, WIN])
            degr = take([T, NT])
            ones16 = take([P, 2], F16)
            take = carve(at_f32[:, AT_USED:])
            rowd = take([GW, G, ROWL], I32)
            junk = take([GW, 4, CAP])
            take = carve(hs_f32)
            wqkv = take([P, CB, 3 * C])
            wmo = take([P, CB, C])
            wx = take([P, CB, HG])
            bdsl = take([P, P])
            bx4 = take([P, HB])
            bv2 = take([P, CB])
            bmo = take([P, C])
            bsl = take([P, D])
            tmpr = take([P, HEADS])
            wvT = take([P, CB, CB, P])
            wxT = take([P, HB, CB, P])
            msum = take([P, CB, 2])
            bsum = take([P, 2])
            bxb = take([P, HB, P])
            bvb = take([P, CB, P])

            head_loaded, weights_loaded = sem("head_loaded"), sem("weights_loaded")
            iotas_ready, zeros_ready, past_ready = sem("iotas_ready"), sem("zeros_ready"), sem("past_ready")
            rows_counted, ridx_ready, row_gathered = sem("rows_counted"), sem("ridx_ready"), sem("row_gathered")
            lo_ready, src_gathered, dst_gathered = sem("lo_ready"), sem("src_gathered"), sem("dst_gathered")
            keys_made, keys_turned, keys_stored = sem("keys_made"), sem("keys_turned"), sem("keys_stored")
            deg_ready, deg_stored, deg_loaded = sem("deg_ready"), sem("deg_stored"), sem("deg_loaded")
            deg_turned, wt_turned, wt_stored = sem("deg_turned"), sem("wt_turned"), sem("wt_stored")
            wprod, wprod_used, invt_ready, dve_step = sem("wprod"), sem("wprod_used"), sem("invt_ready"), sem("dve_step")
            deg_counted = sem("deg_counted")
            spread_ready = sem("spread_ready")

            block = stage.enter_context(nc.Block())
            NWL = 15

            @block.sync
            def _(sp):
                with nc.allow_non_contiguous_dma(reason="every 125th edge, columns of small biases"):
                    sp.dma_start(heads.rearrange("p (c o) -> p c o", o=1),
                                 dst.rearrange("(p c l) -> p c l", c=HC, l=ROWL)[:, :, 0:1]).then_inc(head_loaded, 16)
                    sp.wait_ge(zeros_ready, 1)
                    loads = [(wqkv, W_qkv.rearrange("(b p) n -> p b n", p=P)),
                             (wmo, W_mo.rearrange("(b p) n -> p b n", p=P)),
                             (wx, W_x.rearrange("(b p) n -> p b n", p=P)),
                             (bdsl[0:D, 0:D], W_sl), (bdsl[D:P, D:P], W_sl),
                             (bx4, b_x.rearrange("(b p) -> p b", p=P)),
                             (bv2, b_qkv[2 * C:3 * C].rearrange("(b p) -> p b", p=P)),
                             (bmo, b_mo.rearrange("(a n) -> a n", a=1).to_broadcast([P, C])),
                             (bsl, b_sl.rearrange("(a n) -> a n", a=1).to_broadcast([P, D])),
                             (bqk, b_qkv[0:2 * C].rearrange("(a n) -> a n", a=1).to_broadcast([P, 2 * C])),
                             (tmpr, temp.rearrange("a h b c -> a (h b c)").to_broadcast([P, HEADS])),
                             (w1[:, :, :], W1.rearrange("(b p) n -> p b n", p=P)),
                             (b1b[:, :], b1.rearrange("(a n) -> a n", a=1).to_broadcast([P, C]))]
                    assert len(loads) == NWL - 2
                    for to, of in loads:
                        sp.dma_start(to, of).then_inc(weights_loaded, 16)
                sp.wait_ge(deg_counted, G * WIN)
                sp.dma_start(deg_dram.rearrange("(g p j) -> p g j", g=G, j=WIN), deg).then_inc(deg_stored, 16)
                sp.wait_ge(deg_stored, 16)
                sp.dma_start(degr, deg_dram.rearrange("(t p) -> t p", p=NT)).then_inc(deg_loaded, 16)
                sp.wait_ge(deg_loaded, 16)

            @block.gpsimd
            def _(pool):
                nc.gpsimd.memset(ident[:, :], 0.0).then_inc(ident_sem, 1)
                nc.gpsimd.memset(bdsl, 0.0).then_inc(zeros_ready, 1)
                nc.gpsimd.iota(w_lo, [[WIN, NW]], base=0, channel_multiplier=0,
                               allow_small_or_imprecise_dtypes=True)
                nc.gpsimd.iota(wfirst, [[WIN * GW, G]], base=0, channel_multiplier=WIN,
                               allow_small_or_imprecise_dtypes=True).then_inc(iotas_ready, 1)
                pool.wait_ge(ident_sem, 1)
                nc.gpsimd.affine_select(out=ident[:, :], in_=ident[:, :], compare_op=ALU.not_equal, fill=1.0,
                                        base=0, pattern=[[-1, P]], channel_multiplier=1).then_inc(ident_sem, 1)
                pool.wait_ge(ridx_ready, 1)
                for g in range(G):
                    pool.indirect_dma_start(
                        out=rowd[:, g, :], out_offset=None, in_=dst.rearrange("(r l) -> r l", l=ROWL),
                        in_offset=bass.IndirectOffsetOnAxis(ap=ridx[:, g:g + 1], axis=0)).then_inc(row_gathered, 16)
                pool.wait_ge(row_gathered, 16 * G)
                pool.wait_ge(lo_ready, 1)
                for g in range(G):
                    for to, of, s in ((srcg, src, src_gathered), (dstg, dst, dst_gathered)):
                        pool.indirect_dma_start(
                            out=to[:, g, :], out_offset=None, in_=of.rearrange("(e a) -> e a", a=1),
                            in_offset=bass.IndirectOffsetOnAxis(ap=lo[:, g:g + 1], axis=0)).then_inc(s, 16)
                pool.wait_ge(src_gathered, 16 * G)
                pool.wait_ge(dst_gathered, 16 * G)
                pool.wait_ge(wprod_used, 2)
                nc.gpsimd.memset(hs_f32[96:P, :], 0.0)

            @block.vector
            def _(dve):
                steps = [0]

                def step(ins):
                    steps[0] += 1
                    ins.then_inc(dve_step, 1)
                    dve.wait_ge(dve_step, steps[0])

                v = nc.vector
                v.memset(ones[:, :], 1.0)
                v.memset(ones16, 1.0)
                v.memset(degT[:, :], 0.0)
                v.memset(small[:, 2:3], 0.0)
                v.memset(zeros[:, :], 0.0)
                v.memset(eps[:, :], 1e-5)
                dve.wait_ge(head_loaded, 16)
                step(v.tensor_copy(heads_f, heads))
                dve.wait_ge(iotas_ready, 1)
                for c in range(HC):
                    v.tensor_scalar(past[:, c, :], w_lo, heads_f[:, c:c + 1], None, ALU.is_gt).then_inc(past_ready, 1)
                dve.wait_ge(ident_sem, 2)
                v.tensor_copy(ident16[:, :], ident[:, :]).then_inc(ident_sem, 1)
                dve.wait_ge(rows_counted, 1)
                step(v.tensor_scalar(ridx_f, ps[0:GW, 0, 0:G], -1.0, 0.0, ALU.add, ALU.max))
                v.tensor_copy(ridx, ridx_f).then_inc(ridx_ready, 1)
                step(v.tensor_scalar(rbase, ridx_f, float(ROWL), None, ALU.mult))
                dve.wait_ge(weights_loaded, 16 * (NWL - 2))
                qk = wqkv[:, :, 0:2 * C].rearrange("p b (h c) -> p b h c", c=C)
                for b in range(CB):
                    v.tensor_reduce(msum[:, b, :], qk[:, b], AX.X, ALU.add)
                v.tensor_copy(bxb, bx4.rearrange("p (b o) -> p b o", o=1).to_broadcast([P, HB, P]))
                v.tensor_copy(bvb, bv2.rearrange("p (b o) -> p b o", o=1).to_broadcast([P, CB, P])).then_inc(spread_ready, 1)
                step(v.tensor_reduce(bsum, bqk.rearrange("p (h c) -> p h c", c=C), AX.X, ALU.add))
                step(v.tensor_scalar(msum, msum, -1.0 / C, None, ALU.mult))
                step(v.tensor_scalar(bsum, bsum, -1.0 / C, None, ALU.mult))
                for h in range(2):
                    for b in range(CB):
                        v.tensor_scalar(wqk[:, b, h * C:(h + 1) * C], qk[:, b, h, :], msum[:, b, h:h + 1], None, ALU.add)
                    v.tensor_scalar(bqk[:, h * C:(h + 1) * C], bqk[:, h * C:(h + 1) * C],
                                    bsum[:, h:h + 1], None, ALU.add)
                step(v.tensor_scalar(tmpr, tmpr, 0.1, 5.0, ALU.max, ALU.min))
                step(v.reciprocal(tmpr, tmpr))
                dve.wait_ge(row_gathered, 16 * G)
                for g in range(G):
                    last = v.tensor_scalar(junk[:, g % 4, 0:ROWL], rowd[:, g, :], wfirst[:, g:g + 1], 0.0,
                                           ALU.is_lt, ALU.add, accum_out=cnt[:, g:g + 1])
                    step(last)
                step(v.tensor_tensor(lo_f, rbase, cnt, ALU.add))
                step(v.tensor_scalar(lo_f, lo_f, float(E - CAP), None, ALU.min))
                v.tensor_copy(lo, lo_f).then_inc(lo_ready, 1)
                dve.wait_ge(wprod, 1)
                itb = tmpr.rearrange("p (h o) -> p h o", o=1)
                for b in range(CB):
                    v.tensor_tensor(wlog[:, b, :].rearrange("p (h d) -> p h d", d=D),
                                    ps[:, 6 + b, :].rearrange("p (h d) -> p h d", d=D),
                                    itb.to_broadcast([P, HEADS, D]), ALU.mult)
                by_head = blogb[:, :].rearrange("p (h d) -> p h d", d=D)
                step(v.tensor_tensor(by_head, ps[:, 5, :].rearrange("p (h d) -> p h d", d=D),
                                     bsl.rearrange("p (o d) -> p o d", o=1).to_broadcast([P, HEADS, D]), ALU.add))
                v.tensor_tensor(by_head, by_head, itb.to_broadcast([P, HEADS, D]), ALU.mult)
                v.tensor_copy(bvw, ps[:, 1, 0:C])
                v.tensor_tensor(bvo, ps[:, 1, 0:C], bmo, ALU.add).then_inc(wprod_used, 1)
                dve.wait_ge(dst_gathered, 16 * G)
                for g in range(G):
                    last = v.tensor_scalar(dl[:, g, :], dstg[:, g, :], wfirst[:, g:g + 1], None, ALU.subtract)
                step(last)
                dve.wait_ge(src_gathered, 16 * G)
                step(v.tensor_scalar(tile_of, srcg, 1.0 / NT, 0.5 / NT - 0.5, ALU.mult, ALU.add))
                step(v.tensor_scalar(tile_of, tile_of, 12582912.0, -12582912.0, ALU.add, ALU.add))
                step(v.tensor_scalar(tmp_f, dl, float(WIN), None, ALU.is_lt))
                step(v.scalar_tensor_tensor(out=tmp_f, in0=dl, scalar=0.0, in1=tmp_f, op0=ALU.is_ge, op1=ALU.mult))
                step(v.scalar_tensor_tensor(out=srcg, in0=tile_of, scalar=-float(NT), in1=srcg, op0=ALU.mult, op1=ALU.add))
                v.scalar_tensor_tensor(out=tmp_f, in0=srcg, scalar=1.0, in1=tmp_f, op0=ALU.add, op1=ALU.mult
                                       ).then_inc(keys_made, 1)
                for g in range(G):
                    for j in range(WIN):
                        n = g * WIN + j
                        if n >= 4:
                            dve.wait_ge(deg_counted, n - 3)
                        v.tensor_scalar(junk[:, n % 4, :], dl[:, g, :], float(j), 0.0, ALU.is_equal, ALU.add,
                                        accum_out=deg[:, g, j:j + 1]).then_inc(deg_counted, 1)
                dve.wait_ge(deg_counted, G * WIN)
                dve.wait_ge(keys_made, 1)
                v.scalar_tensor_tensor(out=dl, in0=tile_of, scalar=float(WIN), in1=dl, op0=ALU.mult, op1=ALU.add
                                       ).then_inc(keys_made, 1)
                dve.wait_ge(deg_turned, 1)
                step(v.tensor_copy(degT[0:NT, :], ps[0:NT, 5, 0:T]))
                v.tensor_reduce(small[:, 0:1], degT[:, :], AX.X, ALU.add).then_inc(deg_ready, 1)
                dve.wait_ge(deg_turned, 2)
                v.tensor_scalar(flag[0:1, :], ps[0:1, 0, 0:1], float(E), None, ALU.not_equal)

            @block.tensor
            def _(pe):
                t = nc.tensor
                for g in range(G):
                    for c in range(HC):
                        if g == 0:
                            pe.wait_ge(past_ready, c + 1)
                        mm = t.matmul(ps[0:GW, 0, g:g + 1], lhsT=past[:, c, g * GW:(g + 1) * GW],
                                      rhs=ones16[0:HP, 0:1], start=(c == 0), stop=(c == HC - 1))
                mm.then_inc(rows_counted, 1)
                pe.wait_ge(ident_sem, 2)
                pe.wait_ge(weights_loaded, 16 * (NWL - 2))
                for i in range(CB):
                    for c in range(CB):
                        mm = t.transpose(ps[:, 1, (c * CB + i) * P:(c * CB + i + 1) * P],
                                         wqkv[:, i, 2 * C + c * P:2 * C + (c + 1) * P], ident[:, :])
                mm.then_inc(wt_turned, 1)
                for i in range(CB):
                    for c in range(HB):
                        n = c * CB + i
                        mm = t.transpose(ps[:, 2 + n // 4, (n % 4) * P:(n % 4 + 1) * P],
                                         wx[:, i, c * P:(c + 1) * P], ident[:, :])
                mm.then_inc(wt_turned, 1)
                pe.wait_ge(wt_stored, 1)
                pe.wait_ge(spread_ready, 1)
                for i in range(CB):
                    for c in range(CB):
                        t.matmul(ps[:, 4, i * C:(i + 1) * C], lhsT=wvT[:, c, i, :], rhs=wmo[:, c, :],
                                 start=(c == 0), stop=(c == CB - 1))
                for c in range(CB):
                    t.matmul(ps[:, 1, 0:C], lhsT=bvb[:, c, :], rhs=wmo[:, c, :],
                             start=(c == 0), stop=(c == CB - 1))
                pe.wait_ge(wt_stored, 2)
                for c in range(HB):
                    for i in range(CB):
                        t.matmul(ps[:, 6 + i, c * P:(c + 1) * P], lhsT=wxT[:, c, i, :], rhs=bdsl, start=True, stop=True)
                    mm = t.matmul(ps[:, 5, c * P:(c + 1) * P], lhsT=bxb[:, c, :], rhs=bdsl, start=True, stop=True)
                mm.then_inc(wprod, 1)
                pe.wait_ge(wprod_used, 2)
                for n in range(2 * G):
                    keys = tmp_f if n < G else dl
                    pe.wait_ge(keys_made, 1 if n < G else 2)
                    if n >= 4:
                        pe.wait_ge(keys_stored, n - 3)
                    for c in range(CHUNKS):
                        mm = t.transpose(ps[:, 1 + n % 4, c * GW:(c + 1) * GW],
                                         keys[:, n % G, c * P:(c + 1) * P], ident[0:GW, 0:GW])
                    mm.then_inc(keys_turned, 1)
                pe.wait_ge(deg_loaded, 16)
                t.transpose(ps[0:NT, 5, 0:T], degr, ident[0:T, 0:T]).then_inc(deg_turned, 1)
                pe.wait_ge(deg_ready, 1)
                t.matmul(ps[0:1, 0, 0:1], lhsT=small[:, 0:1], rhs=ones[:, 0:1], start=True, stop=True).then_inc(deg_turned, 1)

            @block.scalar
            def _(act):
                a = nc.scalar
                act.wait_ge(wt_turned, 1)
                a.copy(wvT.rearrange("p a b c -> p (a b c)"), ps[:, 1, :]).then_inc(wt_stored, 1)
                act.wait_ge(wt_turned, 2)
                a.copy(wxT.rearrange("p a b c -> p (a b c)"), ps[:, 2:4, :].rearrange("p a b -> p (a b)")).then_inc(wt_stored, 1)
                act.wait_ge(wprod, 1)
                a.copy(wvo.rearrange("p a b -> p (a b)"), ps[:, 4, :]).then_inc(wprod_used, 1)
                for n in range(2 * G):
                    act.wait_ge(keys_turned, n + 1)
                    keys, g = (key_lo if n < G else key_hi), n % G
                    a.copy(keys[:, g * GW:(g + 1) * GW, :].rearrange("p w c -> p c w"),
                           ps[:, 1 + n % 4, 0:CHUNKS * GW].rearrange("p (c w) -> p c w", w=GW)).then_inc(keys_stored, 1)

        def shifted_slot(b, u, n, ring):
            return (b + n) % ring, u + (b + n) // ring

        def count_degrees():
            with ExitStack() as stage:
                take = carve(big_f)
                ids = take([ROWL, 1], I32)
                ids_f = take([ROWL, 1])
                tile_id = take([ROWL, 1])
                place = take([ROWL, 1])
                hot_tile = take([ROWL, T])
                hot_place = take([ROWL, NT])
                iota_t = take([ROWL, T])
                iota_p = take([ROWL, NT])
                g_iotas, g_loaded, g_step = sem("gd_iotas"), sem("gd_loaded"), sem("gd_step")
                g_copied, g_hot, g_counted = sem("gd_copied"), sem("gd_hot"), sem("gd_counted")
                block = stage.enter_context(nc.Block())

                @block.sync
                def _(sp):
                    def load(r):
                        if reached(r, 1):
                            sp.wait_ge(g_copied, r)
                        sp.dma_start(ids, dst.rearrange("(r l o) -> r l o", l=ROWL, o=1)[bass.ds(r, 1)]
                                     .rearrange("r l o -> (r l) o")).then_inc(g_loaded, 16)

                    load(0)
                    with sp.Fori(1, ROWS) as r:
                        load(r)

                @block.gpsimd
                def _(pool):
                    nc.gpsimd.iota(iota_t, [[1, T]], base=0, channel_multiplier=0, allow_small_or_imprecise_dtypes=True)
                    nc.gpsimd.iota(iota_p, [[1, NT]], base=0, channel_multiplier=0,
                                   allow_small_or_imprecise_dtypes=True).then_inc(g_iotas, 1)

                @block.vector
                def _(dve):
                    v = nc.vector
                    dve.wait_ge(g_iotas, 1)

                    def hots(r):
                        dve.wait_ge(g_loaded, 16 * r + 16)
                        v.tensor_copy(ids_f, ids).then_inc(g_copied, 1)
                        dve.wait_ge(g_copied, r + 1)
                        v.tensor_scalar(tile_id, ids_f, 1.0 / NT, 0.5 / NT - 0.5, ALU.mult, ALU.add).then_inc(g_step, 1)
                        dve.wait_ge(g_step, 3 * r + 1)
                        v.tensor_scalar(tile_id, tile_id, 12582912.0, -12582912.0, ALU.add, ALU.add).then_inc(g_step, 1)
                        dve.wait_ge(g_step, 3 * r + 2)
                        v.scalar_tensor_tensor(out=place, in0=tile_id, scalar=-float(NT), in1=ids_f, op0=ALU.mult,
                                               op1=ALU.add).then_inc(g_step, 1)
                        dve.wait_ge(g_step, 3 * r + 3)
                        if reached(r, 1):
                            dve.wait_ge(g_counted, r)
                        v.tensor_scalar(hot_tile, iota_t, tile_id, None, ALU.is_equal)
                        v.tensor_scalar(hot_place, iota_p, place, None, ALU.is_equal).then_inc(g_hot, 1)

                    hots(0)
                    with dve.Fori(1, ROWS) as r:
                        hots(r)

                @block.scalar
                def _(act):
                    act.wait_ge(g_counted, ROWS)
                    nc.scalar.copy(degT[0:NT, :], ps[0:NT, 1, 0:T])

                @block.tensor
                def _(pe):
                    def count(r):
                        pe.wait_ge(g_hot, r + 1)
                        nc.tensor.matmul(ps[0:NT, 1, 0:T], lhsT=hot_place, rhs=hot_tile, start=False, stop=False,
                                         skip_group_check=True).then_inc(g_counted, 1)

                    pe.wait_ge(g_hot, 1)
                    nc.tensor.matmul(ps[0:NT, 1, 0:T], lhsT=zeros[0:ROWL, 0:NT], rhs=hot_tile, start=True, stop=False,
                                     skip_group_check=True)
                    count(0)
                    with pe.Fori(1, ROWS) as r:
                        count(r)

        general = nc.values_load(flag[0:1, 0:1], min_val=0, max_val=1)
        with nc.If(general == 1):
            count_degrees()

        with ExitStack() as stage:
            deg_root, dinv_ready = sem("deg_root"), sem("dinv_ready")
            block = stage.enter_context(nc.Block())

            @block.scalar
            def _(act):
                nc.scalar.activation(dinv[:, :], degT[:, :], ACT.Sqrt, bias=ones[:, 0:1]).then_inc(deg_root, 1)

            @block.vector
            def _(dve):
                dve.wait_ge(deg_root, 1)
                nc.vector.reciprocal(dinv[:, :], dinv[:, :]).then_inc(dinv_ready, 1)
                dve.wait_ge(dinv_ready, 1)
                nc.vector.tensor_scalar(dsc[:, :], dinv[:, :], SH, None, ALU.mult)
                nc.vector.tensor_scalar(dun[:, :], dinv[:, :], 1.0 / SH, None, ALU.mult)

        with ExitStack() as stage:
            RING = 4
            take = carve(big_f)
            x_in = take([P, RING, C])
            xn = take([P, RING, C + 2])
            xt_now = take([P, RING, CB, NT])
            q2t_now = take([P, RING, CB, NT])
            qkb = take([P, RING, 2 * C])
            qk2 = take([P, RING, 2 * C])
            k2n = take([P, RING, C])
            k4 = take([P, RING, C])
            square = take([P, C])
            st = take([P, RING, 6])
            mv = take([P, RING, 2])
            rstd = take([P, RING])
            sums = take([P, RING, 2])
            rqk = take([P, RING, 2])
            nq = take([P, RING])
            fq = take([P, RING])
            x_loaded = [sem(f"x_loaded{b}") for b in range(RING)]
            x_out, q_out = [sem(f"x_out{b}") for b in range(RING)], [sem(f"q_out{b}") for b in range(RING)]
            xn_ready, xn_turned, xnT_stored = sem("xn_ready"), sem("xn_turned"), sem("xnT_stored")
            qk_ready, biased, sq_ready, recip_ready = sem("qk_ready"), sem("biased"), sem("sq_ready"), sem("recip_ready")
            k4_ready, k2n_ready, kx_done = sem("k4_ready"), sem("k2n_ready"), sem("kx_done")
            q2f_ready, q2_turned, q2T_stored = sem("q2f_ready"), sem("q2_turned"), sem("q2T_stored")
            std_ready, rstd_ready, nq_root = sem("std_ready"), sem("rstd_ready"), sem("nq_root")
            ln_step, hi_ready, fq_step, zeroed = sem("ln_step"), sem("hi_ready"), sem("fq_step"), sem("zeroed")

            block = stage.enter_context(nc.Block())

            @block.sync
            def _(sp):
                def tile(t, b, u):
                    if within(t, T):
                        if reached(t, RING):
                            sp.wait_ge(xn_ready, t - RING + 1)
                        sp.dma_start(x_in[0:NT, b, :], x[bass.ds(t * NT, NT), :]).then_inc(x_loaded[b], 16)
                    if reached(t, 3) and within(t, T + 3):
                        sp.wait_ge(xnT_stored, t - 2)
                        sp.dma_start(xT_dram[bass.ds(t - 3, 1), :, 0:CB * NT].rearrange("t p n -> (t p) n"),
                                     xt_now[:, (b - 3) % RING].rearrange("p a b -> p (a b)")
                                     ).then_inc(x_out[(b - 3) % RING], 16)
                    if reached(t, 6):
                        sp.wait_ge(q2T_stored, t - 5)
                        sp.dma_start(xT_dram[bass.ds(t - 6, 1), :, CB * NT:2 * CB * NT].rearrange("t p n -> (t p) n"),
                                     q2t_now[:, (b - 6) % RING].rearrange("p a b -> p (a b)")
                                     ).then_inc(q_out[(b - 6) % RING], 16)

                pipeline(sp, tile, T, RING, lag=6)
                for b in range(RING):
                    sp.wait_ge(x_out[b], 16 * len(range(b, T, RING)))
                    sp.wait_ge(q_out[b], 16 * len(range(b, T, RING)))

            @block.vector
            def _(dve):
                v = nc.vector
                v.memset(xn[:, :, C:C + 2], 1.0).then_inc(zeroed, 1)
                dve.wait_ge(zeroed, 1)

                def stats(t, b, u):
                    dve.wait_ge(x_loaded[b], 16 * u + 16)
                    v.bn_stats(st[0:NT, b, :], x_in[0:NT, b, :]).then_inc(ln_step, 1)
                    dve.wait_ge(ln_step, 2 * t + 1)
                    v.memset(rstd[0:NT, b:b + 1], 0.0)
                    v.bn_aggr(mv[0:NT, b, :], st[0:NT, b, :]).then_inc(ln_step, 1)

                def norm(t, b):
                    dve.wait_ge(std_ready, t + 1)
                    v.reciprocal(rstd[0:NT, b:b + 1], rstd[0:NT, b:b + 1]).then_inc(rstd_ready, 1)
                    dve.wait_ge(rstd_ready, t + 1)
                    if reached(t, RING):
                        dve.wait_ge(kx_done, t - RING + 1)
                    v.tensor_scalar(xn[0:NT, b, 0:C], x_in[0:NT, b, :], mv[0:NT, b, 0:1], rstd[0:NT, b:b + 1],
                                    ALU.subtract, ALU.mult).then_inc(xn_ready, 1)
                    dve.wait_ge(xn_ready, t + 1)
                    v.tensor_scalar(hs[0:NT, bass.ds(t, 1), 0:C].rearrange("p o c -> p (o c)"), xn[0:NT, b, 0:C],
                                    dsc[0:NT, bass.ds(t, 1)], None, ALU.mult).then_inc(hi_ready, 1)

                def halves(t, b):
                    dve.wait_ge(hi_ready, t + 1)
                    v.scalar_tensor_tensor(out=hs[0:NT, bass.ds(t, 1), C:2 * C].rearrange("p o c -> p (o c)"),
                                           in0=xn[0:NT, b, 0:C], scalar=dsc[0:NT, bass.ds(t, 1)],
                                           in1=hs[0:NT, bass.ds(t, 1), 0:C].rearrange("p o c -> p (o c)"),
                                           op0=ALU.mult, op1=ALU.subtract)

                def bias(t, b):
                    dve.wait_ge(qk_ready, t + 1)
                    if reached(t, RING):
                        dve.wait_ge(sq_ready, 2 * (t - RING) + 2)
                    v.tensor_tensor(qkb[0:NT, b, :], ps[0:NT, 1 + b % 2, :], bqk[0:NT, :], ALU.add).then_inc(biased, 1)

                def over_sums(t, b):
                    dve.wait_ge(sq_ready, 2 * t + 2)
                    if reached(t, RING):
                        dve.wait_ge(k4_ready, 2 * (t - RING) + 2)
                    v.tensor_scalar(rqk[0:NT, b, :], sums[0:NT, b, :], 1e-7, None, ALU.add).then_inc(recip_ready, 1)
                    dve.wait_ge(recip_ready, 2 * t + 1)
                    v.reciprocal(rqk[0:NT, b, :], rqk[0:NT, b, :]).then_inc(recip_ready, 1)
                    dve.wait_ge(recip_ready, 2 * t + 2)
                    v.tensor_scalar(k2n[0:NT, b, :], qk2[0:NT, b, C:2 * C], rqk[0:NT, b, 1:2], None,
                                    ALU.mult).then_inc(k2n_ready, 1)

                def over_norm(t, b):
                    dve.wait_ge(nq_root, t + 1)
                    v.tensor_scalar(fq[0:NT, b:b + 1], nq[0:NT, b:b + 1], 1e-12, None, ALU.max).then_inc(fq_step, 1)
                    dve.wait_ge(fq_step, 3 * t + 1)
                    v.reciprocal(fq[0:NT, b:b + 1], fq[0:NT, b:b + 1]).then_inc(fq_step, 1)
                    dve.wait_ge(fq_step, 3 * t + 2)
                    v.tensor_tensor(fq[0:NT, b:b + 1], fq[0:NT, b:b + 1], rqk[0:NT, b, 0:1], ALU.mult).then_inc(fq_step, 1)
                    dve.wait_ge(fq_step, 3 * t + 3)
                    v.tensor_scalar(qk2[0:NT, b, 0:C], qk2[0:NT, b, 0:C], fq[0:NT, b:b + 1], None,
                                    ALU.mult).then_inc(q2f_ready, 1)

                def tile(t, b, u):
                    if within(t, T - 2):
                        stats(t + 2, *shifted_slot(b, u, 2, RING))
                    if reached(t, 1) and within(t, T + 1):
                        over_sums(t - 1, (b - 1) % RING)
                    if reached(t, -1) and within(t, T - 1):
                        norm(t + 1, (b + 1) % RING)
                    if reached(t, 0) and within(t, T):
                        bias(t, b)
                    if reached(t, -1) and within(t, T - 1):
                        halves(t + 1, (b + 1) % RING)
                    if reached(t, 1) and within(t, T + 1):
                        over_norm(t - 1, (b - 1) % RING)

                pipeline(dve, tile, T, RING, lead=2, lag=1)

            @block.tensor
            def _(pe):
                te = nc.tensor

                def turn(t, b):
                    pe.wait_ge(xn_ready, t + 1)
                    if reached(t, 2):
                        pe.wait_ge(xnT_stored, t - 1)
                    for c in range(CB):
                        mm = te.transpose(ps[:, 3 * (b % 2), c * NT:(c + 1) * NT],
                                          xn[0:NT, b, c * P:(c + 1) * P], ident[0:NT, 0:NT])
                    mm.then_inc(xn_turned, 1)

                def project(t, b):
                    pe.wait_ge(xnT_stored, t + 1)
                    if reached(t, 2):
                        pe.wait_ge(biased, t - 1)
                    for c in range(CB):
                        mm = te.matmul(ps[0:NT, 1 + b % 2, :], lhsT=xt_now[:, b, c, :], rhs=wqk[:, c, :],
                                       start=(c == 0), stop=(c == CB - 1))
                    mm.then_inc(qk_ready, 1)

                def gather(t, b):
                    pe.wait_ge(k2n_ready, t + 1)
                    for c in range(CB):
                        te.matmul(ps[:, 4 + c, 0:C + 2], lhsT=k2n[0:NT, b, c * P:(c + 1) * P],
                                  rhs=xn[0:NT, b, :], start=False, stop=False, skip_group_check=True)
                    pe.wait_ge(k4_ready, 2 * t + 2)
                    for c in range(CB):
                        mm = te.matmul(ps[:, 4 + c, C + 2:C + 3], lhsT=k4[0:NT, b, c * P:(c + 1) * P],
                                       rhs=ones[0:NT, 0:1], start=False, stop=False, skip_group_check=True)
                    mm.then_inc(kx_done, 1)
                    pe.wait_ge(q2f_ready, t + 1)
                    if reached(t, 2):
                        pe.wait_ge(q2T_stored, t - 1)
                    for c in range(CB):
                        mm = te.transpose(ps[:, 6 + b % 2, c * NT:(c + 1) * NT],
                                          qk2[0:NT, b, c * P:(c + 1) * P], ident[0:NT, 0:NT])
                    mm.then_inc(q2_turned, 1)

                def tile(t, b, u):
                    if within(t, T - 1):
                        turn(t + 1, (b + 1) % RING)
                    if reached(t, 0) and within(t, T):
                        project(t, b)
                    if reached(t, 2):
                        gather(t - 2, (b - 2) % RING)

                for c in range(CB):
                    te.matmul(ps[:, 4 + c, 0:C + 3], lhsT=zeros[:, :], rhs=wqk[:, 0, 0:C + 3], start=True, stop=False,
                              skip_group_check=True)
                pipeline(pe, tile, T, RING, lead=1, lag=2)

            @block.scalar
            def _(act):
                a = nc.scalar

                def std(t, b):
                    act.wait_ge(ln_step, 2 * t + 2)
                    a.activation(rstd[0:NT, b:b + 1], mv[0:NT, b, 1:2], ACT.Sqrt, bias=eps[0:NT, 0:1]).then_inc(std_ready, 1)

                def keep(t, b, u):
                    act.wait_ge(xn_turned, t + 1)
                    if reached(t, RING):
                        act.wait_ge(qk_ready, t - RING + 1)
                        act.wait_ge(x_out[b], 16 * u)
                    a.copy(xt_now[:, b].rearrange("p a b -> p (a b)"),
                           ps[:, 3 * (b % 2), 0:CB * NT]).then_inc(xnT_stored, 1)

                def squares(t, b):
                    act.wait_ge(biased, t + 1)
                    if reached(t, RING):
                        act.wait_ge(q2_turned, t - RING + 1)
                        act.wait_ge(k2n_ready, t - RING + 1)
                    for h in range(2):
                        a.activation(qk2[0:NT, b, h * C:(h + 1) * C], qkb[0:NT, b, h * C:(h + 1) * C], ACT.Square,
                                     accum_out=sums[0:NT, b, h:h + 1]).then_inc(sq_ready, 1)

                def norms(t, b):
                    act.wait_ge(recip_ready, 2 * t + 2)
                    a.activation(square[0:NT, :], qk2[0:NT, b, 0:C], ACT.Square, scale=rqk[0:NT, b, 0:1],
                                 accum_out=nq[0:NT, b:b + 1]).then_inc(k4_ready, 1)
                    act.wait_ge(k4_ready, 2 * t + 1)
                    a.activation(nq[0:NT, b:b + 1], nq[0:NT, b:b + 1], ACT.Sqrt).then_inc(nq_root, 1)
                    if reached(t, RING):
                        act.wait_ge(kx_done, t - RING + 1)
                    a.activation(k4[0:NT, b, :], qk2[0:NT, b, C:2 * C], ACT.Square, scale=rqk[0:NT, b, 1:2]).then_inc(k4_ready, 1)

                def turned(t, b, u):
                    act.wait_ge(q2_turned, t + 1)
                    if reached(t, RING):
                        act.wait_ge(q_out[b], 16 * u)
                    a.copy(q2t_now[:, b].rearrange("p a b -> p (a b)"),
                           ps[:, 6 + b % 2, 0:CB * NT]).then_inc(q2T_stored, 1)

                def tile(t, b, u):
                    if within(t, T - 2):
                        std(t + 2, (b + 2) % RING)
                    if reached(t, 1) and within(t, T + 1):
                        norms(t - 1, (b - 1) % RING)
                    if reached(t, -1) and within(t, T - 1):
                        keep(t + 1, *shifted_slot(b, u, 1, RING))
                    if reached(t, 0) and within(t, T):
                        squares(t, b)
                    if reached(t, 2):
                        turned(t - 2, *shifted_slot(b, u, -2, RING))

                pipeline(act, tile, T, RING, lead=2, lag=2)

        with ExitStack() as stage:
            take = carve(big_f)
            kx = take([P, CB, C + 3])
            kxT = take([P, CB, CB, P])
            rn = take([P, CB])
            mp = take([P, CB, C])
            sums_kept, sums_turned, sumsT_kept = sem("sums_kept"), sem("sums_turned"), sem("sumsT_kept")
            m_ready, rn_step, m_kept, rn_root = sem("m_ready"), sem("rn_step"), sem("m_kept"), sem("rn_root")
            block = stage.enter_context(nc.Block())

            @block.scalar
            def _(act):
                act.wait_ge(sums_kept, 1)
                nc.scalar.activation(rn, kx[:, :, C + 2], ACT.Sqrt).then_inc(rn_root, 1)

            @block.vector
            def _(dve):
                v = nc.vector
                v.tensor_copy(kx, ps[:, 4:6, 0:C + 3]).then_inc(sums_kept, 1)
                dve.wait_ge(rn_root, 1)
                v.tensor_scalar(rn, rn, 1e-12, None, ALU.max).then_inc(rn_step, 1)
                dve.wait_ge(rn_step, 1)
                v.reciprocal(rn, rn).then_inc(rn_step, 1)
                dve.wait_ge(rn_step, 2)
                v.tensor_scalar(rn, rn, float(N) ** -0.5, None, ALU.mult).then_inc(rn_step, 1)
                dve.wait_ge(sums_turned, 1)
                v.tensor_copy(kxT.rearrange("p a b c -> p (a b c)"), ps[:, 0, :]).then_inc(sumsT_kept, 1)
                dve.wait_ge(m_ready, 1)
                dve.wait_ge(rn_step, 3)
                dve.wait_ge(sums_kept, 1)
                for c in range(CB):
                    v.scalar_tensor_tensor(out=mp[:, c, :], in0=bvw, scalar=kx[:, c, C:C + 1],
                                           in1=ps[:, 1, c * C:(c + 1) * C], op0=ALU.mult, op1=ALU.add).then_inc(m_kept, 1)
                dve.wait_ge(m_kept, CB)
                for c in range(CB):
                    v.tensor_scalar(mkv[:, c, :], mp[:, c, :], rn[:, c:c + 1], None, ALU.mult)

            @block.tensor
            def _(pe):
                te = nc.tensor
                pe.wait_ge(sums_kept, 1)
                for i in range(CB):
                    for c in range(CB):
                        mm = te.transpose(ps[:, 0, (i * CB + c) * P:(i * CB + c + 1) * P],
                                          kx[:, c, i * P:(i + 1) * P], ident[:, :])
                mm.then_inc(sums_turned, 1)
                pe.wait_ge(sumsT_kept, 1)
                for c in range(CB):
                    for i in range(CB):
                        mm = te.matmul(ps[:, 1, c * C:(c + 1) * C], lhsT=kxT[:, i, c, :], rhs=wvo[:, i, :],
                                       start=(i == 0), stop=(i == CB - 1))
                mm.then_inc(m_ready, 1)

        NB = 4
        s_loaded, s_out = [sem(f"s_loaded{b}") for b in range(NB)], [sem(f"s_out{b}") for b in range(NB)]
        s_mixed, s_biased, s_ready = sem("s_mixed"), sem("s_biased"), sem("s_ready")

        def stream(call, region, turned_of, residual, weights, bias, to):
            past = T * call

            def past_in(b):
                return call * len(range(b, T, NB))

            with ExitStack() as stage:
                take = carve(region)
                turned_in = take([P, NB, len(weights) * NT])
                rows_in = take([P, NB, C])
                res = take([P, NB, C])
                block = stage.enter_context(nc.Block())

                @block.sync
                def _(sp):
                    def tile(t, b, u):
                        if reached(t, NB):
                            sp.wait_ge(s_ready, t - NB + 1 + past)
                        sp.dma_start(turned_in[:, b, :], turned_of(t)).then_inc(s_loaded[b], 16)
                        sp.dma_start(rows_in[0:NT, b, :], residual[bass.ds(t * NT, NT), :]).then_inc(s_loaded[b], 16)

                    pipeline(sp, tile, T, NB)

                @block.gpsimd
                def _(pool):
                    def tile(t, b, u):
                        pool.wait_ge(s_loaded[b], 32 * u + 32 + 32 * past_in(b))
                        nc.gpsimd.tensor_tensor(rows_in[0:NT, b, :], rows_in[0:NT, b, :], bias[0:NT, :],
                                                ALU.add).then_inc(s_biased, 1)

                    pipeline(pool, tile, T, NB)

                @block.tensor
                def _(pe):
                    def tile(t, b, u):
                        pe.wait_ge(s_loaded[b], 32 * u + 32 + 32 * past_in(b))
                        if reached(t, NB):
                            pe.wait_ge(s_ready, t - NB + 1 + past)
                        for i, w in enumerate(weights):
                            mm = nc.tensor.matmul(ps[0:NT, b, 0:C], lhsT=turned_in[:, b, i * NT:(i + 1) * NT], rhs=w,
                                                  start=(i == 0), stop=(i == len(weights) - 1))
                        mm.then_inc(s_mixed, 1)

                    pipeline(pe, tile, T, NB)

                @block.vector
                def _(dve):
                    def tile(t, b, u):
                        dve.wait_ge(s_mixed, t + 1 + past)
                        dve.wait_ge(s_biased, t + 1 + past)
                        if reached(t, NB):
                            dve.wait_ge(s_out[b], 16 * (u + past_in(b)))
                        nc.vector.tensor_tensor(res[0:NT, b, :], ps[0:NT, b, 0:C], rows_in[0:NT, b, :],
                                                ALU.add).then_inc(s_ready, 1)

                    pipeline(dve, tile, T, NB)

                @block.scalar
                def _(act):
                    def tile(t, b, u):
                        act.wait_ge(s_ready, t + 1 + past)
                        act.dma_start(to[bass.ds(t * NT, NT), :], res[0:NT, b, :]).then_inc(s_out[b], 16)

                    pipeline(act, tile, T, NB)
                    for b in range(NB):
                        act.wait_ge(s_out[b], 16 * (len(range(b, T, NB)) + past_in(b)))

        stream(0, big_f, lambda t: xT_dram[bass.ds(t, 1)].rearrange("t p n -> (t p) n"), x,
               [wvo[:, 0, :], wvo[:, 1, :], mkv[:, 0, :], mkv[:, 1, :]], bvo, base_dram)

        def power_of_two(stage, name):
            max_step, all_max = sem(f"{name}_max_step"), sem(f"{name}_all_max")
            block = stage.enter_context(nc.Block())
            EXP = 0x7F800000

            @block.vector
            def _(dve):
                v = nc.vector
                v.tensor_reduce(small[0:NT, 2:3], big_f[0:NT, 0:T * C], AX.X, ALU.max,
                                apply_absolute_value=True).then_inc(max_step, 1)
                dve.wait_ge(all_max, 1)
                v.tensor_scalar(small[:, 4:5], small[:, 3:4], 1e-30, None, ALU.max).then_inc(max_step, 1)
                dve.wait_ge(max_step, 2)
                v.tensor_scalar(small[:, 5:6].bitcast(I32), small[:, 4:5].bitcast(I32), EXP, None, ALU.bitwise_and)
                v.tensor_scalar(small[:, 6:7].bitcast(I32), small[:, 4:5].bitcast(I32), EXP, EXP,
                                ALU.bitwise_and, ALU.bitwise_xor).then_inc(max_step, 1)
                dve.wait_ge(max_step, 3)
                v.tensor_scalar(small[:, 7:8], small[:, 6:7], 2.0 ** 13, None, ALU.mult)
                v.tensor_scalar(small[:, 8:9], small[:, 5:6], 2.0 ** -14, None, ALU.mult).then_inc(max_step, 1)
                dve.wait_ge(max_step, 4)
                v.tensor_scalar(dun[:, :], dinv[:, :], small[:, 8:9], None, ALU.mult)

            @block.gpsimd
            def _(pool):
                pool.wait_ge(max_step, 1)
                nc.gpsimd.partition_all_reduce(small[:, 3:4], small[:, 2:3], P, RMAX).then_inc(all_max, 1)

        BATCH = 10
        assert T % BATCH == 0
        BATCHES = T // BATCH
        e_nodes, e_stored, e_src, e_dst_ids = sem("e_nodes"), sem("e_stored"), sem("e_src"), sem("e_dst_ids")
        e_widened = sem("e_widened")
        e_turn, e_gathered, e_dst, e_hot, e_multiplied, e_added = (
            sem("e_turn"), sem("e_gathered"), sem("e_dst"), sem("e_hot"), sem("e_multiplied"), sem("e_added"))

        def sum_edges(layer):
            with ExitStack() as stage:
                take = carve(hs_f32)
                src_ids = take([ROWL, 1], I32)
                dst_ids = take([ROWL, 1], I32)
                dst_f = take([ROWL, 1])
                msg = take([ROWL, C])
                turn = take([ROWL, 1])
                hot = take([ROWL, BATCH * NT])
                nodes = take([ROWL, N])
                acc = big[:, T:2 * T, :]
                ADDED = (layer + 1) * (ROWS * BATCHES + 1)
                rows_before, steps_before = layer * ROWS, layer * ROWS * BATCHES
                block = stage.enter_context(nc.Block())

                @block.sync
                def _(sp):
                    sp.dma_start(h_dram.rearrange("(t p) c -> p t c", p=NT), z1s[0:NT]).then_inc(e_stored, 16)

                    def load(r):
                        if reached(r, 1):
                            sp.wait_ge(e_multiplied, r * BATCHES + steps_before)
                        for to, of, s in ((src_ids, src, e_src), (dst_ids, dst, e_dst_ids)):
                            sp.dma_start(to, of.rearrange("(r l o) -> r l o", l=ROWL, o=1)[bass.ds(r, 1)]
                                         .rearrange("r l o -> (r l) o")).then_inc(s, 16)

                    load(0)
                    with sp.Fori(1, ROWS) as r:
                        load(r)

                @block.scalar
                def _(act):
                    with act.Fori(0, ROWS) as r:
                        act.wait_ge(e_dst_ids, 16 * r + 16 + 16 * rows_before)
                        nc.scalar.copy(dst_f, dst_ids).then_inc(e_dst, 1)

                @block.gpsimd
                def _(pool):
                    nc.gpsimd.iota(nodes, [[1, N]], base=0, channel_multiplier=0,
                                   allow_small_or_imprecise_dtypes=True).then_inc(e_nodes, 1)
                    pool.wait_ge(e_stored, 16 * layer + 16)
                    nc.gpsimd.memset(turn, 0.0).then_inc(e_turn, 1)
                    with pool.Fori(0, ROWS) as r:
                        pool.wait_ge(e_turn, r + 1 + rows_before + layer)
                        pool.wait_ge(e_src, 16 * r + 16 + 16 * rows_before)
                        nc.gpsimd.tensor_tensor(turn, turn, turn, ALU.add).then_inc(e_turn, 1)
                        pool.indirect_dma_start(
                            out=msg, out_offset=None, in_=h_dram,
                            in_offset=bass.IndirectOffsetOnAxis(ap=src_ids[:, 0:1], axis=0)).then_inc(e_gathered, 16)
                    pool.wait_ge(e_added, ADDED)
                    nc.gpsimd.memset(hs_f32[96:P, :], 0.0)

                @block.vector
                def _(dve):
                    v = nc.vector
                    dve.wait_ge(e_nodes, layer + 1)
                    v.tensor_copy(acc[0:NT], z1s[0:NT]).then_inc(e_added, 1)
                    with dve.Fori(0, ROWS) as r:
                        with dve.Fori(0, BATCHES) as m:
                            dve.wait_ge(e_dst, r + 1 + rows_before)
                            n = r * BATCHES + m + steps_before
                            dve.wait_ge(e_added, n + 1 + layer)
                            v.tensor_scalar(hot, nodes[:, bass.ds(m * (BATCH * NT), BATCH * NT)], dst_f, None,
                                            ALU.is_equal).then_inc(e_hot, 1)
                            dve.wait_ge(e_multiplied, n + 1)
                            rows = acc[0:NT, bass.ds(m * BATCH, BATCH), :].rearrange("p t c -> p (t c)")
                            v.tensor_tensor(rows, rows, ps[0:NT, 0:BATCH // 2, :].rearrange("p b c -> p (b c)"),
                                            ALU.add).then_inc(e_added, 1)
                    dve.wait_ge(e_stored, 16 * layer + 16)
                    dve.wait_ge(e_added, ADDED)
                    v.tensor_copy(z1s[0:NT], acc[0:NT])

                @block.tensor
                def _(pe):
                    with pe.Fori(0, ROWS) as r:
                        with pe.Fori(0, BATCHES) as m:
                            pe.wait_ge(e_gathered, 16 * r + 16 + 16 * rows_before)
                            pe.wait_ge(e_hot, r * BATCHES + m + 1 + steps_before)
                            for h in range(BATCH):
                                mm = nc.tensor.matmul(ps[0:NT, h // 2, (h % 2) * C:(h % 2 + 1) * C],
                                                      lhsT=hot[:, h * NT:(h + 1) * NT], rhs=msg, start=True, stop=True)
                            mm.then_inc(e_multiplied, 1)

        scale2 = small[:, 7:8]

        with nc.If(general == 1):
            with ExitStack() as stage:
                block = stage.enter_context(nc.Block())

                @block.vector
                def _(dve):
                    nc.vector.tensor_tensor(z1s[0:NT], hs[0:NT, :, 0:C], hs[0:NT, :, C:2 * C], ALU.add)
                    nc.vector.memset(key_lo[:, :, :], 0.0).then_inc(e_widened, 1)

                @block.scalar
                def _(act):
                    act.wait_ge(e_widened, 1)

                @block.gpsimd
                def _(pool):
                    pool.wait_ge(e_widened, 1)

                @block.tensor
                def _(pe):
                    pe.wait_ge(e_widened, 1)

                @block.sync
                def _(sp):
                    sp.wait_ge(e_widened, 1)

            sum_edges(0)
            with ExitStack() as stage:
                power_of_two(stage, "gl1")
            with ExitStack() as stage:
                hi_made = sem("gl1_hi_made")
                block = stage.enter_context(nc.Block())

                @block.scalar
                def _(act):
                    nc.scalar.activation(hs[0:NT, :, 0:C], z1s[0:NT], ACT.Identity, scale=scale2[0:NT]).then_inc(hi_made, 1)

                @block.vector
                def _(dve):
                    nc.vector.tensor_scalar(dun[:, :], dun[:, :], 1.0 / SH, None, ALU.mult)
                    dve.wait_ge(hi_made, 1)
                    nc.vector.scalar_tensor_tensor(out=hs[0:NT, :, C:2 * C], in0=z1s[0:NT], scalar=scale2[0:NT],
                                                   in1=hs[0:NT, :, 0:C], op0=ALU.mult, op1=ALU.subtract)

        RING = 5
        UNITS = -(-WPT // 2)
        with ExitStack() as stage:
            take = carve(big_f[:, T * C:])
            hot_hi = take([P, RING, CHUNKS, KC], F16)
            hot_lo = take([P, RING, CHUNKS, P], F16)
            iota_hi = take([P, KC], F16)
            iota_lo = take([P, P], F16)
            agg = take([P, 2, C])
            low = take([P, 2, C])
            aggT = take([P, 2, CB, NT])
            zb = take([P, 2, C])
            iotas_ready, pads_ready = sem("l1_iotas_ready"), sem("pads_ready")
            hot_ready, built, at_stored = sem("hot_ready"), sem("built"), sem("at_stored")
            at_out = [sem("at_out0"), sem("at_out1")]
            summed, low_ready, agg_ready = sem("summed"), sem("low_ready"), sem("agg_ready")
            agg_turned, aggT_ready, multiplied = sem("agg_turned"), sem("aggT_ready"), sem("multiplied")
            zb_ready, z_ready = sem("zb_ready"), sem("z_ready")
            block = stage.enter_context(nc.Block())

            @block.gpsimd
            def _(pool):
                g = nc.gpsimd
                g.iota(iota_hi, [[1, KC]], base=0, channel_multiplier=0, allow_small_or_imprecise_dtypes=True)
                g.iota(iota_lo, [[1, P]], base=1, channel_multiplier=0,
                       allow_small_or_imprecise_dtypes=True).then_inc(iotas_ready, 1)
                for b in range(2):
                    g.memset(at[:, b, :].rearrange("p (k d) -> p k d", d=P)[:, :, NT:P], 0.0).then_inc(pads_ready, 1)

            @block.vector
            def _(dve):
                v = nc.vector
                dve.wait_ge(iotas_ready, 1)

                def hots(t, i):
                    w, s = t * WPT + i, i % RING
                    if reached(w, RING):
                        dve.wait_ge(built, w - RING + 1)
                    for c in range(CHUNKS):
                        v.tensor_scalar(hot_hi[:, s, c, :], iota_hi, key_hi[:, bass.ds(w, 1), c], None, ALU.is_equal)
                        last = v.tensor_scalar(hot_lo[:, s, c, :], iota_lo, key_lo[:, bass.ds(w, 1), c], None,
                                               ALU.is_equal)
                    last.then_inc(hot_ready, 1)

                def gather(t, b):
                    dve.wait_ge(low_ready, t + 1)
                    if reached(t, 2):
                        dve.wait_ge(agg_turned, t - 1)
                    v.tensor_tensor(agg[0:NT, b, :], ps[0:NT, 2 + b, 0:C], low[0:NT, b, :], ALU.add).then_inc(agg_ready, 1)

                def bias(t, b):
                    dve.wait_ge(multiplied, t + 1)
                    if reached(t, 2):
                        dve.wait_ge(z_ready, t - 1)
                    v.scalar_tensor_tensor(out=zb[0:NT, b, :], in0=ps[0:NT, 5, b * C:(b + 1) * C],
                                           scalar=dun[0:NT, bass.ds(t, 1)], in1=b1b[0:NT, :],
                                           op0=ALU.mult, op1=ALU.add).then_inc(zb_ready, 1)

                def tile(t, b, u):
                    for i in range(WPT):
                        if within(t, T - 1):
                            hots(t + 1, i)
                        if i == 7 and reached(t, 1):
                            gather(t - 1, 1 - b)
                        if i == 17 and reached(t, 1):
                            bias(t - 1, 1 - b)

                pipeline(dve, tile, T, 2, lead=1, lag=1)

            @block.tensor
            def _(pe):
                te = nc.tensor

                def build(t, i, b):
                    w, s, unit = t * WPT + i, i % RING, t * UNITS + i // 2
                    pe.wait_ge(hot_ready, w + 1)
                    if i % 2 == 0 and reached(unit, 2):
                        pe.wait_ge(at_stored, unit - 1)
                    for c in range(CHUNKS):
                        mm = te.matmul(ps[:, (b * UNITS + i // 2) % 2, i % 2 * KC:(i % 2 + 1) * KC],
                                       lhsT=hot_lo[:, s, c, :], rhs=hot_hi[:, s, c, :],
                                       start=(c == 0), stop=(c == CHUNKS - 1))
                    mm.then_inc(built, 1)

                def aggregate(t, b, ks):
                    for k in ks:
                        if k == 0:
                            pe.wait_ge(at_stored, (t + 1) * UNITS)
                            if reached(t, 2):
                                pe.wait_ge(agg_ready, t - 1)
                        te.matmul(ps[:, 2 + b, :], lhsT=at[:, b, k * P:(k + 1) * P], rhs=hs[:, k, :],
                                  start=(k == 0), stop=False)
                        if k == T - 1:
                            te.matmul(ps[:, 2 + b, :], lhsT=ident16[:, :],
                                      rhs=hs[:, bass.ds(t, 1), :].rearrange("p t c -> p (t c)"),
                                      start=False, stop=True).then_inc(summed, 1)

                def turn(t, b):
                    pe.wait_ge(agg_ready, t + 1)
                    for c in range(CB):
                        mm = te.transpose(ps[:, 4, (b * CB + c) * NT:(b * CB + c + 1) * NT],
                                          agg[0:NT, b, c * P:(c + 1) * P], ident[0:NT, 0:NT])
                    mm.then_inc(agg_turned, 1)

                def multiply(t, b):
                    pe.wait_ge(aggT_ready, t + 1)
                    for c in range(CB):
                        mm = te.matmul(ps[0:NT, 5, b * C:(b + 1) * C], lhsT=aggT[:, b, c, :], rhs=w1[:, c, :],
                                       start=(c == 0), stop=(c == CB - 1))
                    mm.then_inc(multiplied, 1)

                def tile(t, b, u):
                    for i in range(WPT):
                        if within(t, T - 1):
                            build(t + 1, i, 1 - b)
                        if reached(t, 0) and within(t, T) and i >= 2:
                            aggregate(t, b, range((i - 2) * T // (WPT - 2), (i - 1) * T // (WPT - 2)))
                        if i == 8 and reached(t, 1):
                            turn(t - 1, 1 - b)
                        if i == 11 and reached(t, 1):
                            multiply(t - 1, 1 - b)

                pe.wait_ge(pads_ready, 2)
                pipeline(pe, tile, T, 2, lead=1, lag=1)

            @block.scalar
            def _(act):
                a = nc.scalar

                def store(t, m, b, u):
                    here = min(2, WPT - 2 * m)
                    act.wait_ge(built, t * WPT + 2 * m + here)
                    if m == 0 and reached(t, 2):
                        act.wait_ge(summed, t - 1)
                        act.wait_ge(at_out[b], 16 * u)
                    bank = (b * UNITS + m) % 2
                    to = at[:, b, :].rearrange("p (k d) -> p k d", d=P)[:, :, 2 * m * WIN:(2 * m + here) * WIN]
                    a.copy(to.rearrange("p k (i j) -> p i k j", j=WIN),
                           ps[:, bank, 0:here * KC].rearrange("p (i k j) -> p i k j", i=here, j=WIN)
                           ).then_inc(at_stored, 1)

                def lows(t, b):
                    act.wait_ge(summed, t + 1)
                    if reached(t, 2):
                        act.wait_ge(agg_ready, t - 1)
                    a.copy(low[0:NT, b, :], ps[0:NT, 2 + b, C:2 * C]).then_inc(low_ready, 1)

                def keep(t, b):
                    act.wait_ge(agg_turned, t + 1)
                    if reached(t, 2):
                        act.wait_ge(multiplied, t - 1)
                    a.copy(aggT[:, b].rearrange("p a b -> p (a b)"), ps[:, 4, b * CB * NT:(b + 1) * CB * NT]).then_inc(aggT_ready, 1)

                def relu(t, b):
                    act.wait_ge(zb_ready, t + 1)
                    a.activation(z1s[0:NT, bass.ds(t, 1), :].rearrange("p t c -> p (t c)"), zb[0:NT, b, :], ACT.Relu,
                                 scale=dinv[0:NT, bass.ds(t, 1)]).then_inc(z_ready, 1)

                def tile(t, b, u):
                    for m in range(UNITS):
                        if within(t, T - 1):
                            store(t + 1, m, *shifted_slot(b, u, 1, 2))
                        if m == 0 and reached(t, 1):
                            lows(t - 1, 1 - b)
                        if m == 4 and reached(t, 1):
                            keep(t - 1, 1 - b)
                        if m == 10 and reached(t, 1):
                            relu(t - 1, 1 - b)

                pipeline(act, tile, T, 2, lead=1, lag=1)

            @block.sync
            def _(sp):
                def tile(t, b, u):
                    sp.wait_ge(at_stored, (t + 1) * UNITS)
                    sp.wait_ge(pads_ready, 2)
                    sp.dma_start(at_dram[bass.ds(t, 1)].rearrange("t p n -> (t p) n"), at[:, b, :]).then_inc(at_out[b], 16)

                pipeline(sp, tile, T, 2)
                sp.wait_ge(at_out[0], 16 * (T // 2))
                sp.wait_ge(at_out[1], 16 * (T // 2))

        with nc.If(general == 1):
            sum_edges(1)

        with ExitStack() as stage:
            power_of_two(stage, "l2")

        take = carve(key_lo[:, :, :].rearrange("p w c -> p (w c)"))
        s_sum = take([P, HB, C])
        w_sum = take([P, HB])
        w_acc = take([P, HB, NT])
        take = carve(key_hi[:, :, :].rearrange("p w c -> p (w c)"))
        w2 = take([P, CB, C])
        b2b = take([P, C])
        with ExitStack() as stage:
            take = carve(big_f[:, T * C:])
            agg = take([P, 2, C])
            low = take([P, 2, C])
            aggT = take([P, 2, CB, NT])
            zb = take([P, 2, C])
            base_in = take([P, 2, C])
            x1 = take([P, 2, C])
            xn2 = take([P, 2, C])
            xn2T = take([P, 2, CB, NT])
            lg = take([P, 2, HEADS, D])
            ew = take([P, 2, HEADS, D])
            wt = take([P, 2, HB, NT])
            hmax = take([P, 2, HEADS])
            hsum = take([P, 2, HEADS])
            st = take([P, 2, 6])
            mv = take([P, 2, 2])
            rstd = take([P, 2])
            hi_made, hs_made, w2_loaded = sem("l2_hi_made"), sem("l2_hs_made"), sem("w2_loaded")
            at_loaded, base_loaded = [sem(f"l2_at_loaded{b}") for b in range(2)], [sem(f"l2_base_loaded{b}") for b in range(2)]
            x1_out, w_out = [sem(f"x1_out{b}") for b in range(2)], [sem(f"w_out{b}") for b in range(2)]
            summed, low_ready, agg_ready = sem("l2_summed"), sem("l2_low_ready"), sem("l2_agg_ready")
            agg_turned, aggT_ready, multiplied = sem("l2_agg_turned"), sem("l2_aggT_ready"), sem("l2_multiplied")
            x1_ready, ln_step, xn2_ready = sem("x1_ready"), sem("l2_ln_step"), sem("xn2_ready")
            xn2_turned, xn2T_ready, logits_ready = sem("xn2_turned"), sem("xn2T_ready"), sem("logits_ready")
            shifted, exp_ready, soft_step, w_ready = sem("shifted"), sem("exp_ready"), sem("soft_step"), sem("w_ready")
            w_turned, wt_ready, w_added, s_added = sem("w_turned"), sem("wt_ready"), sem("w_added"), sem("s_added")
            zb_ready, std_ready, rstd_ready = sem("l2_zb_ready"), sem("l2_std_ready"), sem("l2_rstd_ready")
            acc_ready = sem("acc_ready")
            block = stage.enter_context(nc.Block())

            @block.sync
            def _(sp):
                sp.dma_start(w2, W2.rearrange("(b p) n -> p b n", p=P)).then_inc(w2_loaded, 16)
                sp.dma_start(b2b, b2.rearrange("(a n) -> a n", a=1).to_broadcast([P, C])).then_inc(w2_loaded, 16)

                def tile(t, b, u):
                    if reached(t, 2):
                        sp.wait_ge(summed, t - 1)
                    sp.dma_start(at[:, b, :], at_dram[bass.ds(t, 1)].rearrange("t p n -> (t p) n")).then_inc(at_loaded[b], 16)
                    if reached(t, 2):
                        sp.wait_ge(x1_ready, t - 1)
                    sp.dma_start(base_in[0:NT, b, :], base_dram[bass.ds(t * NT, NT), :]).then_inc(base_loaded[b], 16)

                pipeline(sp, tile, T, 2)

            @block.tensor
            def _(pe):
                te = nc.tensor

                def sum_tile(t, b, u, k):
                    if k == 0:
                        pe.wait_ge(at_loaded[b], 16 * u + 16)
                        if reached(t, 2):
                            pe.wait_ge(agg_ready, t - 1)
                    if not reached(t, 1):
                        pe.wait_ge(hs_made, k + 1)
                    te.matmul(ps[:, b, :], lhsT=at[:, b, k * P:(k + 1) * P], rhs=hs[:, k, :],
                              start=(k == 0), stop=False)
                    if k == T - 1:
                        te.matmul(ps[:, b, :], lhsT=ident16[:, :],
                                  rhs=hs[:, bass.ds(t, 1), :].rearrange("p t c -> p (t c)"),
                                  start=False, stop=True).then_inc(summed, 1)

                def turn(t, b):
                    pe.wait_ge(agg_ready, t + 1)
                    for c in range(CB):
                        mm = te.transpose(ps[:, 2, c * NT:(c + 1) * NT], agg[0:NT, b, c * P:(c + 1) * P], ident[0:NT, 0:NT])
                    mm.then_inc(agg_turned, 1)

                def multiply(t, b):
                    pe.wait_ge(aggT_ready, t + 1)
                    for c in range(CB):
                        mm = te.matmul(ps[0:NT, 3, 0:C], lhsT=aggT[:, b, c, :], rhs=w2[:, c, :],
                                       start=(c == 0), stop=(c == CB - 1))
                    mm.then_inc(multiplied, 1)

                def turn_x(t, b):
                    pe.wait_ge(xn2_ready, t + 1)
                    for c in range(CB):
                        mm = te.transpose(ps[:, 2, C + c * NT:C + (c + 1) * NT], xn2[0:NT, b, c * P:(c + 1) * P],
                                          ident[0:NT, 0:NT])
                    mm.then_inc(xn2_turned, 1)

                def logits(t, b):
                    pe.wait_ge(xn2T_ready, t + 1)
                    for c in range(CB):
                        mm = te.matmul(ps[0:NT, 4, :], lhsT=xn2T[:, b, c, :], rhs=wlog[:, c, :],
                                       start=(c == 0), stop=(c == CB - 1))
                    mm.then_inc(logits_ready, 1)

                def weigh(t, b):
                    pe.wait_ge(w_ready, t + 1)
                    if reached(t, 1):
                        pe.wait_ge(wt_ready, t)
                    ewf = ew[:, b].rearrange("p h d -> p (h d)")
                    for p in range(HB):
                        mm = te.transpose(ps[:, 5, p * NT:(p + 1) * NT], ewf[0:NT, p * P:(p + 1) * P], ident[0:NT, 0:NT])
                    mm.then_inc(w_turned, 1)
                    for p in range(HB):
                        mm = te.matmul(ps[:, 6 + p // 2, (p % 2) * C:(p % 2 + 1) * C], lhsT=ewf[0:NT, p * P:(p + 1) * P],
                                       rhs=xn2[0:NT, b, :], start=False, stop=False, skip_group_check=True)
                    mm.then_inc(s_added, 1)

                def tile(t, b, u):
                    for k in range(T):
                        if reached(t, 0) and within(t, T):
                            sum_tile(t, b, u, k)
                        if reached(t, 1) and within(t, T + 1):
                            for at_k, do in ((6, turn), (12, multiply), (28, turn_x), (34, logits)):
                                if k == at_k:
                                    do(t - 1, 1 - b)
                        if k == 42 and reached(t, 2):
                            weigh(t - 2, b)

                for h in range(2):
                    te.matmul(ps[:, 6 + h, :], lhsT=zeros[:, :], rhs=wlog[:, 0, :], start=True, stop=False,
                              skip_group_check=True)
                pe.wait_ge(w2_loaded, 32)
                pipeline(pe, tile, T, 2, lag=2)

            @block.vector
            def _(dve):
                v = nc.vector

                with dve.Fori(0, T) as t:
                    dve.wait_ge(hi_made, t + 1)
                    z = z1s[0:NT, bass.ds(t, 1), :].rearrange("p t c -> p (t c)")
                    v.scalar_tensor_tensor(out=hs[0:NT, bass.ds(t, 1), C:2 * C].rearrange("p o c -> p (o c)"), in0=z,
                                           scalar=scale2[0:NT], in1=hs[0:NT, bass.ds(t, 1), 0:C].rearrange("p o c -> p (o c)"),
                                           op0=ALU.mult, op1=ALU.subtract).then_inc(hs_made, 1)

                def gather(t, b):
                    dve.wait_ge(low_ready, t + 1)
                    v.tensor_tensor(agg[0:NT, b, :], ps[0:NT, b, 0:C], low[0:NT, b, :], ALU.add).then_inc(agg_ready, 1)

                def norm(t, b, u):
                    dve.wait_ge(multiplied, t + 1)
                    v.scalar_tensor_tensor(out=zb[0:NT, b, :], in0=ps[0:NT, 3, 0:C], scalar=dun[0:NT, bass.ds(t, 1)],
                                           in1=b2b[0:NT, :], op0=ALU.mult, op1=ALU.add).then_inc(zb_ready, 1)
                    dve.wait_ge(zb_ready, t + 1)
                    dve.wait_ge(base_loaded[b], 16 * u + 16)
                    if reached(t, 2):
                        dve.wait_ge(x1_out[b], 16 * u)
                    v.scalar_tensor_tensor(out=x1[0:NT, b, :], in0=zb[0:NT, b, :], scalar=0.0, in1=base_in[0:NT, b, :],
                                           op0=ALU.max, op1=ALU.add).then_inc(x1_ready, 1)
                    dve.wait_ge(x1_ready, t + 1)
                    v.bn_stats(st[0:NT, b, :], x1[0:NT, b, :]).then_inc(ln_step, 1)
                    dve.wait_ge(ln_step, 2 * t + 1)
                    v.memset(rstd[0:NT, b:b + 1], 0.0)
                    v.bn_aggr(mv[0:NT, b, :], st[0:NT, b, :]).then_inc(ln_step, 1)
                    dve.wait_ge(std_ready, t + 1)
                    v.reciprocal(rstd[0:NT, b:b + 1], rstd[0:NT, b:b + 1]).then_inc(rstd_ready, 1)
                    dve.wait_ge(rstd_ready, t + 1)
                    if reached(t, 2):
                        dve.wait_ge(s_added, t - 1)
                    v.tensor_scalar(xn2[0:NT, b, :], x1[0:NT, b, :], mv[0:NT, b, 0:1], rstd[0:NT, b:b + 1],
                                    ALU.subtract, ALU.mult).then_inc(xn2_ready, 1)

                def shift(t, b):
                    dve.wait_ge(logits_ready, t + 1)
                    v.tensor_tensor(lg[0:NT, b].rearrange("p h d -> p (h d)"), ps[0:NT, 4, :], blogb[0:NT, :],
                                    ALU.add).then_inc(soft_step, 1)
                    dve.wait_ge(soft_step, 4 * t + 1)
                    v.tensor_reduce(hmax[0:NT, b, :], lg[0:NT, b], AX.X, ALU.max).then_inc(soft_step, 1)
                    dve.wait_ge(soft_step, 4 * t + 2)
                    v.tensor_tensor(lg[0:NT, b], lg[0:NT, b],
                                    hmax[0:NT, b, :].rearrange("p (h o) -> p h o", o=1).to_broadcast([NT, HEADS, D]),
                                    ALU.subtract).then_inc(shifted, 1)

                def divide(t, b):
                    dve.wait_ge(exp_ready, t + 1)
                    v.tensor_reduce(hsum[0:NT, b, :], ew[0:NT, b], AX.X, ALU.add).then_inc(soft_step, 1)
                    dve.wait_ge(soft_step, 4 * t + 3)
                    v.reciprocal(hsum[0:NT, b, :], hsum[0:NT, b, :]).then_inc(soft_step, 1)
                    dve.wait_ge(soft_step, 4 * t + 4)
                    v.tensor_tensor(ew[0:NT, b], ew[0:NT, b],
                                    hsum[0:NT, b, :].rearrange("p (h o) -> p h o", o=1).to_broadcast([NT, HEADS, D]),
                                    ALU.mult).then_inc(w_ready, 1)

                def tile(t, b, u):
                    gather(t, b)
                    norm(t, b, u)
                    shift(t, b)
                    divide(t, b)

                dve.wait_ge(w2_loaded, 32)
                pipeline(dve, tile, T, 2)
                dve.wait_ge(s_added, T)
                v.tensor_copy(s_sum.rearrange("p a b -> p (a b)"), ps[:, 6:8, :].rearrange("p a b -> p (a b)"))

            @block.scalar
            def _(act):
                a = nc.scalar
                with act.Fori(0, T) as t:
                    z = z1s[0:NT, bass.ds(t, 1), :].rearrange("p t c -> p (t c)")
                    a.activation(hs[0:NT, bass.ds(t, 1), 0:C].rearrange("p o c -> p (o c)"), z, ACT.Identity,
                                 scale=scale2[0:NT]).then_inc(hi_made, 1)

                def rest(t, b):
                    act.wait_ge(summed, t + 1)
                    a.copy(low[0:NT, b, :], ps[0:NT, b, C:2 * C]).then_inc(low_ready, 1)
                    act.wait_ge(agg_turned, t + 1)
                    a.copy(aggT[:, b].rearrange("p a b -> p (a b)"), ps[:, 2, 0:CB * NT]).then_inc(aggT_ready, 1)
                    act.wait_ge(ln_step, 2 * t + 2)
                    a.activation(rstd[0:NT, b:b + 1], mv[0:NT, b, 1:2], ACT.Sqrt, bias=eps[0:NT, 0:1]).then_inc(std_ready, 1)
                    act.wait_ge(xn2_turned, t + 1)
                    a.copy(xn2T[:, b].rearrange("p a b -> p (a b)"), ps[:, 2, C:C + CB * NT]).then_inc(xn2T_ready, 1)
                    act.wait_ge(shifted, t + 1)
                    a.activation(ew[0:NT, b], lg[0:NT, b], ACT.Exp).then_inc(exp_ready, 1)
                    act.dma_start(x1_dram[bass.ds(t * NT, NT), :], x1[0:NT, b, :]).then_inc(x1_out[b], 16)

                def turned(t, b, u):
                    act.wait_ge(w_turned, t + 1)
                    if reached(t, 2):
                        act.wait_ge(w_out[b], 16 * u)
                        act.wait_ge(w_added, t - 1)
                    a.copy(wt[:, b].rearrange("p a b -> p (a b)"), ps[:, 5, 0:HB * NT]).then_inc(wt_ready, 1)
                    act.wait_ge(wt_ready, t + 1)
                    act.dma_start(wT_dram[bass.ds(t, 1)].rearrange("t p n -> (t p) n"),
                                  wt[:, b].rearrange("p a b -> p (a b)")).then_inc(w_out[b], 16)

                def tile(t, b, u):
                    if within(t, T):
                        rest(t, b)
                    if reached(t, 1):
                        turned(t - 1, *shifted_slot(b, u, -1, 2))

                pipeline(act, tile, T, 2, lag=1)
                for b in range(2):
                    act.wait_ge(x1_out[b], 16 * (T // 2))
                    act.wait_ge(w_out[b], 16 * (T // 2))

            @block.gpsimd
            def _(pool):
                g = nc.gpsimd
                g.memset(w_acc, 0.0).then_inc(acc_ready, 1)
                pool.wait_ge(acc_ready, 1)

                def tile(t, b, u):
                    pool.wait_ge(wt_ready, t + 1)
                    g.tensor_tensor(w_acc, w_acc, wt[:, b], ALU.add).then_inc(w_added, 1)
                    pool.wait_ge(w_added, t + 1)

                pipeline(pool, tile, T, 2)

        fin = life.enter_context(ExitStack())
        take = carve(big_f)
        pmat = take([P, HB, C])
        bfb = take([P, C])
        final_rest = big_f[:, HB * C + C:]
        with ExitStack() as stage:
            take = carve(final_rest)
            wfx = take([P, CB, HG])
            wfo = take([P, HB, C])
            bfx = take([P, HG])
            bdq = take([P, P])
            bdk = take([P, P])
            bdv = take([P, P])
            sT = take([P, CB, HB, P])
            tok = take([P, HB, P])
            tokT = take([P, HB, P])
            qT = take([P, HB, P])
            kT = take([P, HB, P])
            vv = take([P, HB, P])
            sc = take([P, HB, D])
            at_w = take([P, HB, P])
            atT = take([P, HB, P])
            oT = take([P, HB, P])
            smax = take([P, HB])
            ssum = take([P, HB])
            wrec = take([P, HB])
            tmp = take([P, D])
            zeroed, loaded = sem("f_zeroed"), sem("f_loaded")
            pe_step, dve_step, act_step = sem("f_pe_step"), sem("f_dve_step"), sem("f_act_step")
            block = stage.enter_context(nc.Block())

            @block.gpsimd
            def _(pool):
                for z in (bdq, bdk, bdv, tok):
                    last = nc.gpsimd.memset(z, 0.0)
                last = nc.gpsimd.memset(at_w, 0.0)
                last.then_inc(zeroed, 1)

            @block.sync
            def _(sp):
                sp.dma_start(wfx, W_fx.rearrange("(b p) n -> p b n", p=P)).then_inc(loaded, 16)
                sp.dma_start(wfo, W_fo.rearrange("(b p) n -> p b n", p=P)).then_inc(loaded, 16)
                sp.dma_start(bfx, b_fx.rearrange("(a n) -> a n", a=1).to_broadcast([P, HG])).then_inc(loaded, 16)
                sp.dma_start(bfb, b_fo.rearrange("(a n) -> a n", a=1).to_broadcast([P, C])).then_inc(loaded, 16)
                sp.wait_ge(zeroed, 1)
                for to, of in ((bdq, W_q), (bdk, W_k), (bdv, W_v)):
                    for h in range(2):
                        sp.dma_start(to[h * D:(h + 1) * D, h * D:(h + 1) * D], of).then_inc(loaded, 16)
                sp.wait_ge(loaded, 160)

            @block.tensor
            def _(pe):
                te = nc.tensor
                pe.wait_ge(loaded, 160)
                for i in range(CB):
                    for p in range(HB):
                        mm = te.transpose(ps[:, i, p * P:(p + 1) * P], s_sum[:, p, i * P:(i + 1) * P], ident[:, :])
                mm.then_inc(pe_step, 1)
                pe.wait_ge(act_step, 1)
                for p in range(HB):
                    for i in range(CB):
                        mm = te.matmul(ps[:, 2, p * P:(p + 1) * P], lhsT=sT[:, i, p, :], rhs=wfx[:, i, p * P:(p + 1) * P],
                                       start=(i == 0), stop=(i == CB - 1))
                mm.then_inc(pe_step, 1)
                pe.wait_ge(dve_step, 1)
                for p in range(HB):
                    mm = te.transpose(ps[:, 3, p * P:(p + 1) * P], tok[:, p, :], ident[:, :])
                mm.then_inc(pe_step, 1)
                pe.wait_ge(act_step, 2)
                for p in range(HB):
                    te.matmul(ps[:, 4, p * P:(p + 1) * P], lhsT=bdq, rhs=tokT[:, p, :], start=True, stop=True)
                for p in range(HB):
                    te.matmul(ps[:, 5, p * P:(p + 1) * P], lhsT=bdk, rhs=tokT[:, p, :], start=True, stop=True)
                for p in range(HB):
                    mm = te.matmul(ps[:, 6, p * P:(p + 1) * P], lhsT=tokT[:, p, :], rhs=bdv, start=True, stop=True)
                mm.then_inc(pe_step, 1)
                pe.wait_ge(act_step, 3)
                pe.wait_ge(dve_step, 2)
                for p in range(HB):
                    mm = te.matmul(ps[:, 7, p * P:(p + 1) * P], lhsT=qT[:, p, :], rhs=kT[:, p, :], start=True, stop=True)
                mm.then_inc(pe_step, 1)
                pe.wait_ge(dve_step, 4)
                for p in range(HB):
                    mm = te.transpose(ps[:, 0, p * P:(p + 1) * P], at_w[:, p, :], ident[:, :])
                mm.then_inc(pe_step, 1)
                pe.wait_ge(act_step, 5)
                for p in range(HB):
                    mm = te.matmul(ps[:, 1, p * P:(p + 1) * P], lhsT=vv[:, p, :], rhs=atT[:, p, :], start=True, stop=True)
                mm.then_inc(pe_step, 1)
                pe.wait_ge(act_step, 6)
                for p in range(HB):
                    mm = te.matmul(ps[:, 2 + p // 2, (p % 2) * C:(p % 2 + 1) * C], lhsT=oT[:, p, :], rhs=wfo[:, p, :],
                                   start=True, stop=True)
                mm.then_inc(pe_step, 1)

            @block.scalar
            def _(act):
                a = nc.scalar

                def flat(y):
                    return y.rearrange("p a b -> p (a b)")

                act.wait_ge(pe_step, 1)
                a.copy(sT.rearrange("p a b c -> p (a b c)"), ps[:, 0:2, :].rearrange("p a b -> p (a b)")).then_inc(act_step, 1)
                act.wait_ge(pe_step, 3)
                a.copy(flat(tokT), ps[:, 3, :]).then_inc(act_step, 1)
                act.wait_ge(pe_step, 4)
                a.mul(flat(qT), ps[:, 4, :], float(D) ** -0.5)
                a.copy(flat(vv), ps[:, 6, :]).then_inc(act_step, 1)
                act.wait_ge(dve_step, 3)
                a.activation(sc, sc, ACT.Exp).then_inc(act_step, 1)
                act.wait_ge(pe_step, 6)
                a.copy(flat(atT), ps[:, 0, :]).then_inc(act_step, 1)
                act.wait_ge(pe_step, 7)
                a.copy(flat(oT), ps[:, 1, :]).then_inc(act_step, 1)

            @block.vector
            def _(dve):
                v = nc.vector
                own = sem("f_own")
                n = [0]

                def step(ins):
                    n[0] += 1
                    ins.then_inc(own, 1)
                    dve.wait_ge(own, n[0])

                step(v.tensor_reduce(w_sum, w_acc, AX.X, ALU.add))
                step(v.tensor_scalar(wrec, w_sum, 1e-5, None, ALU.add))
                step(v.reciprocal(wrec, wrec))
                dve.wait_ge(pe_step, 2)
                dve.wait_ge(loaded, 160)
                dve.wait_ge(zeroed, 1)
                for p in range(HB):
                    for h in range(2):
                        r, c = slice(h * D, (h + 1) * D), slice((2 * p + h) * D, (2 * p + h + 1) * D)
                        v.scalar_tensor_tensor(out=tok[r, p, h * D:(h + 1) * D], in0=bfx[r, c], scalar=w_sum[r, p:p + 1],
                                               in1=ps[r, 2, c], op0=ALU.mult, op1=ALU.add).then_inc(own, 1)
                n[0] += 2 * HB
                dve.wait_ge(own, n[0])
                for p in range(HB):
                    last = v.tensor_scalar(tok[:, p, :], tok[:, p, :], wrec[:, p:p + 1], None, ALU.mult)
                last.then_inc(dve_step, 1)
                dve.wait_ge(pe_step, 4)
                v.tensor_copy(kT.rearrange("p a b -> p (a b)"), ps[:, 5, :]).then_inc(dve_step, 1)
                dve.wait_ge(pe_step, 5)
                for h in range(2):
                    r = slice(h * D, (h + 1) * D)
                    s = ps[r, 7, :].rearrange("p (a b) -> p a b", b=P)[:, :, h * D:(h + 1) * D]
                    step(v.tensor_reduce(smax[r, :], s, AX.X, ALU.max))
                    last = v.tensor_tensor(sc[r], s, smax[r, :].rearrange("p (a o) -> p a o", o=1)
                                           .to_broadcast([D, HB, D]), ALU.subtract)
                last.then_inc(dve_step, 1)
                dve.wait_ge(act_step, 4)
                step(v.tensor_reduce(ssum, sc, AX.X, ALU.add))
                step(v.reciprocal(ssum, ssum))
                for h in range(2):
                    r = slice(h * D, (h + 1) * D)
                    last = v.tensor_tensor(at_w[r, :, h * D:(h + 1) * D], sc[r],
                                           ssum[r, :].rearrange("p (a o) -> p a o", o=1).to_broadcast([D, HB, D]), ALU.mult)
                last.then_inc(dve_step, 1)
                dve.wait_ge(pe_step, 8)
                v.tensor_copy(pmat.rearrange("p a b -> p (a b)"), ps[:, 2:4, :].rearrange("p a b -> p (a b)"))

        stream(1, final_rest, lambda t: wT_dram[bass.ds(t, 1)].rearrange("t p n -> (t p) n"), x1_dram,
               [pmat[:, p, :] for p in range(HB)], bfb, out)


_INS = ['x', 'src', 'dst', 'L0_gnn_W1', 'L0_gnn_b1', 'L0_gnn_W2', 'L0_gnn_b2', 'L0_mix_W_qkv', 'L0_mix_b_qkv',
        'L0_mix_W_out', 'L0_mix_b_out', 'L0_ffn_W_fx', 'L0_ffn_b_fx', 'L0_ffn_W_x', 'L0_ffn_b_x', 'L0_ffn_W_slice',
        'L0_ffn_b_slice', 'L0_ffn_W_q', 'L0_ffn_W_k', 'L0_ffn_W_v', 'L0_ffn_W_out', 'L0_ffn_b_out',
        'L0_ffn_temperature']


def kernel(**inputs):
    import numpy as _np
    import concourse.bacc as _bacc
    from concourse import mybir as _mybir
    from concourse.bass_utils import run_bass_kernel_spmd as _run

    nc = _bacc.Bacc("TRN2", target_bir_lowering=False, num_devices=1)
    arrays, args = {}, []
    for name in _INS:
        a = _np.ascontiguousarray(inputs[name])
        arrays[f"in_{name}_dram"] = a
        args.append(nc.dram_tensor(f"in_{name}_dram", a.shape, _mybir.dt.from_np(a.dtype), kind="ExternalInput").ap())
    out = nc.dram_tensor("out_0_dram", inputs["x"].shape, _mybir.dt.float32, kind="ExternalOutput").ap()
    gps_layer(nc, *args, out)
    r = _run(nc, [arrays], core_ids=[0])
    return r.results[0]["out_0_dram"]
```

```python
from contextlib import ExitStack

import concourse.bass as bass
from concourse import mybir

ALU = mybir.AluOpType
ACT = mybir.ActivationFunctionType
F32 = mybir.dt.float32
F16 = mybir.dt.float16
BF16 = mybir.dt.bfloat16
I32 = mybir.dt.int32
AX = mybir.AxisListType
RMAX = bass.bass_isa.ReduceOp.max

P = 128


def divisor(n):
    return max(d for d in range(1, P + 1) if n % d == 0)


def reached(t, least):
    return not isinstance(t, int) or t >= least


def within(t, end):
    return not isinstance(t, int) or t < end


def pipeline(engine, body, tiles, unroll, lead=0, lag=0):
    for t in range(-lead, 2 * unroll):
        body(t, t % unroll, t // unroll)
    rounds = (tiles - 1) // unroll
    if rounds > 2:
        with engine.Fori(2, rounds) as u:
            for b in range(unroll):
                body(u * unroll + b, b, u)
    for t in range(max(rounds, 2) * unroll, tiles + lag):
        body(t, t % unroll, t // unroll)


def gps_layer(nc, x, src, dst, W1, b1, W2, b2, W_qkv, b_qkv, W_mo, b_mo,
              W_fx, b_fx, W_x, b_x, W_sl, b_sl, W_q, W_k, W_v, W_fo, b_fo, temp, out):
    N, C = x.shape
    E = src.shape[0]
    NT = 125
    T = N // NT
    WIN = 5
    WPT = NT // WIN
    NW = T * WPT
    CHUNKS = 2
    CAP = CHUNKS * P
    GW = 125
    G = NW // GW
    KC = T * WIN
    ROWL = divisor(E)
    ROWS = E // ROWL
    HP = divisor(ROWS)
    HC = ROWS // HP
    HEADS, D = 8, W_sl.shape[0]
    HG = HEADS * D
    CB = C // P
    HB = HG // P
    SH = 2048.0
    assert C == 256 and CB == 2 and D == 64 and HG == 512 and G * GW == NW and T * NT == N and T % 2 == 0
    assert 2 * KC <= 512 and E > CAP

    deg_dram = nc.dram_tensor("deg_scratch", (N,), F32, kind="Internal").ap()
    at_dram = nc.dram_tensor("at_scratch", (T, P, T * P), F16, kind="Internal").ap()
    base_dram = nc.dram_tensor("base_scratch", (N, C), F32, kind="Internal").ap()
    xT_dram = nc.dram_tensor("xT_scratch", (T, P, 2 * CB * NT), F32, kind="Internal").ap()
    wT_dram = nc.dram_tensor("wT_scratch", (T, P, HB * NT), F32, kind="Internal").ap()
    x1_dram = nc.dram_tensor("x1_scratch", (N, C), F32, kind="Internal").ap()
    h_dram = nc.dram_tensor("h_scratch", (N, C), F32, kind="Internal").ap()

    with ExitStack() as life:
        def sb(name, shape, dt=F32):
            return life.enter_context(nc.sbuf_tensor(name, shape, dt))

        def sem(name):
            return life.enter_context(nc.semaphore(name))

        def carve(region):
            at = [0]

            def take(shape, dt=F32):
                n = 1
                for s in shape[1:]:
                    n *= s
                words = n if dt in (F32, I32) else -(-n // 2)
                a = region[0:shape[0], at[0]:at[0] + words]
                at[0] += words
                assert at[0] <= region.shape[1], (at[0], region.shape)
                if dt != F32:
                    a = a.bitcast(dt)
                if dt == F16 and n % 2:
                    a = a[:, 0:n]
                if len(shape) == 3:
                    a = a.rearrange("p (a b) -> p a b", b=shape[2])
                if len(shape) == 4:
                    a = a.rearrange("p (a b c) -> p a b c", b=shape[2], c=shape[3])
                return a
            return take

        hs = sb("hs", [P, T, 2 * C], F16)
        big = sb("big", [P, 2 * T, C])
        key_lo = sb("key_lo", [P, NW, CHUNKS])
        key_hi = sb("key_hi", [P, NW, CHUNKS])
        at = sb("at", [P, 2, T * P], F16)
        ident = sb("ident", [P, P])
        ident16 = sb("ident16", [P, P], F16)
        w1 = sb("w1", [P, CB, C])
        wlog = sb("wlog", [P, CB, HG])
        b1b = sb("b1b", [P, C])
        blogb = sb("blogb", [P, HG])
        dinv = sb("dinv", [P, T])
        dsc = sb("dsc", [P, T])
        dun = sb("dun", [P, T])
        dun2 = sb("dun2", [P, T])
        small = sb("small", [P, 24])
        eps = sb("eps", [P, 1])
        ps = life.enter_context(nc.psum_tensor("ps", [P, 8, 512], F32))

        at_f32 = at[:, :, :].rearrange("p a b -> p (a b)").bitcast(F32)
        big_f = big[:, :, :].rearrange("p a b -> p (a b)")
        hs_f32 = hs[:, :, :].rearrange("p a b -> p (a b)").bitcast(F32)
        hs2 = big_f[:, 0:T * C].bitcast(F16).rearrange("p (t c) -> p t c", c=2 * C)
        wlog16 = (wlog[:, :, :].rearrange("p a b -> p (a b)").bitcast(F16)
                  .rearrange("p (h a b) -> p h a b", h=2, a=CB))
        unscale = small[:, 20:21]
        EXPONENT = 0x7F800000

        take = carve(at_f32)
        wqk = take([P, CB, 2 * C])
        bqk = take([P, 2 * C])
        wvo = take([P, CB, C])
        bvw = take([P, C])
        bvo = take([P, C])
        mkv = take([P, CB, C])
        brow = take([3, 2 * C], BF16)
        ones3 = take([3, P], BF16)
        AT_USED = 2 * CB * C + 2 * C + CB * C + 2 * C + CB * C + C + P // 2

        ones = sb("ones", [P, 2])
        zeros = sb("zeros", [P, P])
        degT = sb("degT", [P, T])
        flag = sb("flag", [P, 1], I32)
        ident_sem = sem("ident_sem")

        with ExitStack() as stage:
            take = carve(big_f)
            heads = take([HP, HC], I32)
            heads_f = take([HP, HC])
            w_lo = take([HP, NW])
            past = take([HP, HC, NW], F16)
            wfirst = take([GW, G])
            rbase = take([GW, G])
            ridx_f = take([GW, G])
            ridx = take([GW, G], I32)
            cnt = take([GW, G])
            lo_f = take([GW, G])
            lo = take([GW, G], I32)
            srcg = take([GW, G, CAP], I32)
            dstg = take([GW, G, CAP], I32)
            dl = take([GW, G, CAP])
            tile_of = take([GW, G, CAP])
            tmp_f = take([GW, G, CAP])
            deg = take([GW, G, WIN])
            degr = take([T, NT])
            ones16 = take([P, 2], F16)
            take = carve(at_f32[:, AT_USED:])
            rowd = take([GW, G, ROWL], I32)
            junk = take([GW, 4, CAP])
            take = carve(hs_f32)
            wqkv = take([P, CB, 3 * C])
            wmo = take([P, CB, C])
            wx = take([P, CB, HG])
            bdsl = take([P, P])
            bx4 = take([P, HB])
            bv2 = take([P, CB])
            bmo = take([P, C])
            bsl = take([P, D])
            tmpr = take([P, HEADS])
            wvT = take([P, CB, CB, P])
            wxT = take([P, HB, CB, P])
            msum = take([P, CB, 2])
            bsum = take([P, 2])
            bxb = take([P, HB, P])
            bvb = take([P, CB, P])
            bpart = take([1, 3, 2 * C], BF16)
            brest = take([1, 2, 2 * C])

            head_loaded, weights_loaded = sem("head_loaded"), sem("weights_loaded")
            iotas_ready, zeros_ready, past_ready = sem("iotas_ready"), sem("zeros_ready"), sem("past_ready")
            rows_counted, ridx_ready, row_gathered = sem("rows_counted"), sem("ridx_ready"), sem("row_gathered")
            lo_ready, src_gathered, dst_gathered = sem("lo_ready"), sem("src_gathered"), sem("dst_gathered")
            keys_made, keys_turned, keys_stored = sem("keys_made"), sem("keys_turned"), sem("keys_stored")
            deg_ready, deg_stored, deg_loaded = sem("deg_ready"), sem("deg_stored"), sem("deg_loaded")
            deg_turned, wt_turned, wt_stored = sem("deg_turned"), sem("wt_turned"), sem("wt_stored")
            wprod, wprod_used, dve_step = sem("wprod"), sem("wprod_used"), sem("dve_step")
            deg_counted, bias_split, bias_moved = sem("deg_counted"), sem("bias_split"), sem("bias_moved")
            spread_ready = sem("spread_ready")

            block = stage.enter_context(nc.Block())
            NWL = 15

            @block.sync
            def _(sp):
                with nc.allow_non_contiguous_dma(reason="every 125th edge, columns of small biases"):
                    sp.dma_start(heads.rearrange("p (c o) -> p c o", o=1),
                                 dst.rearrange("(p c l) -> p c l", c=HC, l=ROWL)[:, :, 0:1]).then_inc(head_loaded, 16)
                    sp.wait_ge(zeros_ready, 1)
                    loads = [(wqkv, W_qkv.rearrange("(b p) n -> p b n", p=P)),
                             (wmo, W_mo.rearrange("(b p) n -> p b n", p=P)),
                             (wx, W_x.rearrange("(b p) n -> p b n", p=P)),
                             (bdsl[0:D, 0:D], W_sl), (bdsl[D:P, D:P], W_sl),
                             (bx4, b_x.rearrange("(b p) -> p b", p=P)),
                             (bv2, b_qkv[2 * C:3 * C].rearrange("(b p) -> p b", p=P)),
                             (bmo, b_mo.rearrange("(a n) -> a n", a=1).to_broadcast([P, C])),
                             (bsl, b_sl.rearrange("(a n) -> a n", a=1).to_broadcast([P, D])),
                             (bqk, b_qkv[0:2 * C].rearrange("(a n) -> a n", a=1).to_broadcast([P, 2 * C])),
                             (tmpr, temp.rearrange("a h b c -> a (h b c)").to_broadcast([P, HEADS])),
                             (w1[:, :, :], W1.rearrange("(b p) n -> p b n", p=P)),
                             (b1b[:, :], b1.rearrange("(a n) -> a n", a=1).to_broadcast([P, C]))]
                    assert len(loads) == NWL - 2
                    for to, of in loads:
                        sp.dma_start(to, of).then_inc(weights_loaded, 16)
                sp.wait_ge(bias_split, 1)
                for i in range(3):
                    sp.dma_start(brow[i:i + 1, :], bpart[0:1, i, :]).then_inc(bias_moved, 16)
                sp.wait_ge(bias_moved, 48)
                sp.wait_ge(deg_counted, G * WIN)
                sp.dma_start(deg_dram.rearrange("(g p j) -> p g j", g=G, j=WIN), deg).then_inc(deg_stored, 16)
                sp.wait_ge(deg_stored, 16)
                sp.dma_start(degr, deg_dram.rearrange("(t p) -> t p", p=NT)).then_inc(deg_loaded, 16)
                sp.wait_ge(deg_loaded, 16)

            @block.gpsimd
            def _(pool):
                nc.gpsimd.memset(ident[:, :], 0.0).then_inc(ident_sem, 1)
                nc.gpsimd.memset(bdsl, 0.0).then_inc(zeros_ready, 1)
                nc.gpsimd.iota(w_lo, [[WIN, NW]], base=0, channel_multiplier=0,
                               allow_small_or_imprecise_dtypes=True)
                nc.gpsimd.iota(wfirst, [[WIN * GW, G]], base=0, channel_multiplier=WIN,
                               allow_small_or_imprecise_dtypes=True).then_inc(iotas_ready, 1)
                pool.wait_ge(ident_sem, 1)
                nc.gpsimd.affine_select(out=ident[:, :], in_=ident[:, :], compare_op=ALU.not_equal, fill=1.0,
                                        base=0, pattern=[[-1, P]], channel_multiplier=1).then_inc(ident_sem, 1)
                pool.wait_ge(ridx_ready, 1)
                for g in range(G):
                    pool.indirect_dma_start(
                        out=rowd[:, g, :], out_offset=None, in_=dst.rearrange("(r l) -> r l", l=ROWL),
                        in_offset=bass.IndirectOffsetOnAxis(ap=ridx[:, g:g + 1], axis=0)).then_inc(row_gathered, 16)
                pool.wait_ge(row_gathered, 16 * G)
                pool.wait_ge(lo_ready, 1)
                for to, of, s in ((dstg, dst, dst_gathered), (srcg, src, src_gathered)):
                    for g in range(G):
                        pool.indirect_dma_start(
                            out=to[:, g, :], out_offset=None, in_=of.rearrange("(e a) -> e a", a=1),
                            in_offset=bass.IndirectOffsetOnAxis(ap=lo[:, g:g + 1], axis=0)).then_inc(s, 16)
                pool.wait_ge(src_gathered, 16 * G)
                pool.wait_ge(dst_gathered, 16 * G)
                pool.wait_ge(wprod_used, 2)
                nc.gpsimd.memset(hs_f32[96:P, :], 0.0)

            @block.vector
            def _(dve):
                steps = [0]

                def step(ins):
                    steps[0] += 1
                    ins.then_inc(dve_step, 1)
                    dve.wait_ge(dve_step, steps[0])

                v = nc.vector
                v.memset(ones[:, :], 1.0)
                v.memset(ones16, 1.0)
                v.memset(ones3, 1.0)
                v.memset(degT[:, :], 0.0)
                v.memset(small[:, 2:3], 0.0)
                v.memset(zeros[:, :], 0.0)
                v.memset(eps[:, :], 1e-5)
                dve.wait_ge(head_loaded, 16)
                step(v.tensor_copy(heads_f, heads))
                dve.wait_ge(iotas_ready, 1)
                for c in range(HC):
                    v.tensor_scalar(past[:, c, :], w_lo, heads_f[:, c:c + 1], None, ALU.is_gt).then_inc(past_ready, 1)
                dve.wait_ge(ident_sem, 2)
                v.tensor_copy(ident16[:, :], ident[:, :]).then_inc(ident_sem, 1)
                dve.wait_ge(rows_counted, 1)
                step(v.tensor_scalar(ridx_f, ps[0:GW, 0, 0:G], -1.0, 0.0, ALU.add, ALU.max))
                v.tensor_copy(ridx, ridx_f).then_inc(ridx_ready, 1)
                step(v.tensor_scalar(rbase, ridx_f, float(ROWL), None, ALU.mult))
                dve.wait_ge(weights_loaded, 16 * (NWL - 2))
                qk = wqkv[:, :, 0:2 * C].rearrange("p b (h c) -> p b h c", c=C)
                for b in range(CB):
                    v.tensor_reduce(msum[:, b, :], qk[:, b], AX.X, ALU.add)
                v.tensor_copy(bxb, bx4.rearrange("p (b o) -> p b o", o=1).to_broadcast([P, HB, P]))
                v.tensor_copy(bvb, bv2.rearrange("p (b o) -> p b o", o=1).to_broadcast([P, CB, P])).then_inc(spread_ready, 1)
                step(v.tensor_reduce(bsum, bqk.rearrange("p (h c) -> p h c", c=C), AX.X, ALU.add))
                step(v.tensor_scalar(msum, msum, -1.0 / C, None, ALU.mult))
                step(v.tensor_scalar(bsum, bsum, -1.0 / C, None, ALU.mult))
                for h in range(2):
                    for b in range(CB):
                        v.tensor_scalar(wqk[:, b, h * C:(h + 1) * C], qk[:, b, h, :], msum[:, b, h:h + 1], None, ALU.add)
                    step(v.tensor_scalar(bqk[:, h * C:(h + 1) * C], bqk[:, h * C:(h + 1) * C],
                                         bsum[:, h:h + 1], None, ALU.add))
                step(v.tensor_copy(bpart[:, 0, :], bqk[0:1, :]))
                step(v.tensor_tensor(brest[:, 0, :], bqk[0:1, :], bpart[:, 0, :], ALU.subtract))
                step(v.tensor_copy(bpart[:, 1, :], brest[:, 0, :]))
                step(v.tensor_tensor(brest[:, 1, :], brest[:, 0, :], bpart[:, 1, :], ALU.subtract))
                v.tensor_copy(bpart[:, 2, :], brest[:, 1, :]).then_inc(bias_split, 1)
                step(v.tensor_scalar(tmpr, tmpr, 0.1, 5.0, ALU.max, ALU.min))
                step(v.reciprocal(tmpr, tmpr))
                dve.wait_ge(row_gathered, 16 * G)
                for g in range(G):
                    last = v.tensor_scalar(junk[:, g % 4, 0:ROWL], rowd[:, g, :], wfirst[:, g:g + 1], 0.0,
                                           ALU.is_lt, ALU.add, accum_out=cnt[:, g:g + 1])
                    step(last)
                step(v.tensor_tensor(lo_f, rbase, cnt, ALU.add))
                step(v.tensor_scalar(lo_f, lo_f, float(E - CAP), None, ALU.min))
                v.tensor_copy(lo, lo_f).then_inc(lo_ready, 1)
                dve.wait_ge(wprod, 1)
                itb = tmpr.rearrange("p (h o) -> p h o", o=1)
                for b in range(CB):
                    v.tensor_tensor(wlog[:, b, :].rearrange("p (h d) -> p h d", d=D),
                                    ps[:, 6 + b, :].rearrange("p (h d) -> p h d", d=D),
                                    itb.to_broadcast([P, HEADS, D]), ALU.mult)
                by_head = blogb[:, :].rearrange("p (h d) -> p h d", d=D)
                step(v.tensor_tensor(by_head, ps[:, 5, :].rearrange("p (h d) -> p h d", d=D),
                                     bsl.rearrange("p (o d) -> p o d", o=1).to_broadcast([P, HEADS, D]), ALU.add))
                v.tensor_tensor(by_head, by_head, itb.to_broadcast([P, HEADS, D]), ALU.mult)
                v.tensor_copy(bvw, ps[:, 1, 0:C])
                v.tensor_tensor(bvo, ps[:, 1, 0:C], bmo, ALU.add).then_inc(wprod_used, 1)
                dve.wait_ge(dst_gathered, 16 * G)
                for g in range(G):
                    step(v.tensor_scalar(dl[:, g, :], dstg[:, g, :], wfirst[:, g:g + 1], None, ALU.subtract))
                    for j in range(WIN):
                        n = g * WIN + j
                        if n >= 4:
                            dve.wait_ge(deg_counted, n - 3)
                        v.tensor_scalar(junk[:, n % 4, :], dl[:, g, :], float(j), 0.0, ALU.is_equal, ALU.add,
                                        accum_out=deg[:, g, j:j + 1]).then_inc(deg_counted, 1)
                dve.wait_ge(src_gathered, 16 * G)
                step(v.tensor_scalar(tile_of, srcg, 1.0 / NT, 0.5 / NT - 0.5, ALU.mult, ALU.add))
                step(v.tensor_scalar(tile_of, tile_of, 12582912.0, -12582912.0, ALU.add, ALU.add))
                step(v.tensor_scalar(tmp_f, dl, float(WIN), None, ALU.is_lt))
                step(v.scalar_tensor_tensor(out=tmp_f, in0=dl, scalar=0.0, in1=tmp_f, op0=ALU.is_ge, op1=ALU.mult))
                step(v.scalar_tensor_tensor(out=srcg, in0=tile_of, scalar=-float(NT), in1=srcg, op0=ALU.mult, op1=ALU.add))
                v.scalar_tensor_tensor(out=tmp_f, in0=srcg, scalar=1.0, in1=tmp_f, op0=ALU.add, op1=ALU.mult
                                       ).then_inc(keys_made, 1)
                dve.wait_ge(keys_made, 1)
                dve.wait_ge(deg_counted, G * WIN)
                v.scalar_tensor_tensor(out=dl, in0=tile_of, scalar=float(WIN), in1=dl, op0=ALU.mult, op1=ALU.add
                                       ).then_inc(keys_made, 1)
                dve.wait_ge(deg_turned, 1)
                step(v.tensor_copy(degT[0:NT, :], ps[0:NT, 5, 0:T]))
                v.tensor_reduce(small[:, 0:1], degT[:, :], AX.X, ALU.add).then_inc(deg_ready, 1)
                dve.wait_ge(deg_turned, 2)
                v.tensor_scalar(flag[0:1, :], ps[0:1, 0, 0:1], float(E), None, ALU.not_equal)

            @block.tensor
            def _(pe):
                t = nc.tensor
                pe.wait_ge(past_ready, 1)
                t.matmul(ps[0:GW, 0, 0:G], lhsT=zeros[:, 0:GW], rhs=zeros[:, 0:G], start=True, stop=False,
                         skip_group_check=True)
                for c in range(HC):
                    pe.wait_ge(past_ready, c + 1)
                    for g in range(G):
                        mm = t.matmul(ps[0:GW, 0, g:g + 1], lhsT=past[:, c, g * GW:(g + 1) * GW],
                                      rhs=ones16[0:HP, 0:1], start=False, stop=False, skip_group_check=True)
                mm.then_inc(rows_counted, 1)
                pe.wait_ge(ident_sem, 2)
                pe.wait_ge(weights_loaded, 16 * (NWL - 2))
                for i in range(CB):
                    for c in range(CB):
                        mm = t.transpose(ps[:, 1, (c * CB + i) * P:(c * CB + i + 1) * P],
                                         wqkv[:, i, 2 * C + c * P:2 * C + (c + 1) * P], ident[:, :])
                mm.then_inc(wt_turned, 1)
                for i in range(CB):
                    for c in range(HB):
                        n = c * CB + i
                        mm = t.transpose(ps[:, 2 + n // 4, (n % 4) * P:(n % 4 + 1) * P],
                                         wx[:, i, c * P:(c + 1) * P], ident[:, :])
                mm.then_inc(wt_turned, 1)
                pe.wait_ge(wt_stored, 1)
                pe.wait_ge(spread_ready, 1)
                for i in range(CB):
                    for c in range(CB):
                        t.matmul(ps[:, 4, i * C:(i + 1) * C], lhsT=wvT[:, c, i, :], rhs=wmo[:, c, :],
                                 start=(c == 0), stop=(c == CB - 1))
                for c in range(CB):
                    t.matmul(ps[:, 1, 0:C], lhsT=bvb[:, c, :], rhs=wmo[:, c, :],
                             start=(c == 0), stop=(c == CB - 1))
                pe.wait_ge(wt_stored, 2)
                for c in range(HB):
                    for i in range(CB):
                        t.matmul(ps[:, 6 + i, c * P:(c + 1) * P], lhsT=wxT[:, c, i, :], rhs=bdsl, start=True, stop=True)
                    mm = t.matmul(ps[:, 5, c * P:(c + 1) * P], lhsT=bxb[:, c, :], rhs=bdsl, start=True, stop=True)
                mm.then_inc(wprod, 1)
                pe.wait_ge(wprod_used, 2)
                for n in range(2 * G):
                    keys = tmp_f if n < G else dl
                    pe.wait_ge(keys_made, 1 if n < G else 2)
                    if n >= 4:
                        pe.wait_ge(keys_stored, n - 3)
                    for c in range(CHUNKS):
                        mm = t.transpose(ps[:, 1 + n % 4, c * GW:(c + 1) * GW],
                                         keys[:, n % G, c * P:(c + 1) * P], ident[0:GW, 0:GW])
                    mm.then_inc(keys_turned, 1)
                pe.wait_ge(deg_loaded, 16)
                t.transpose(ps[0:NT, 5, 0:T], degr, ident[0:T, 0:T]).then_inc(deg_turned, 1)
                pe.wait_ge(deg_ready, 1)
                t.matmul(ps[0:1, 0, 0:1], lhsT=small[:, 0:1], rhs=ones[:, 0:1], start=True, stop=True).then_inc(deg_turned, 1)

            @block.scalar
            def _(act):
                a = nc.scalar
                act.wait_ge(wt_turned, 1)
                a.copy(wvT.rearrange("p a b c -> p (a b c)"), ps[:, 1, :]).then_inc(wt_stored, 1)
                act.wait_ge(wt_turned, 2)
                a.copy(wxT.rearrange("p a b c -> p (a b c)"), ps[:, 2:4, :].rearrange("p a b -> p (a b)")).then_inc(wt_stored, 1)
                act.wait_ge(wprod, 1)
                a.copy(wvo.rearrange("p a b -> p (a b)"), ps[:, 4, :]).then_inc(wprod_used, 1)
                for n in range(2 * G):
                    act.wait_ge(keys_turned, n + 1)
                    keys, g = (key_lo if n < G else key_hi), n % G
                    a.copy(keys[:, g * GW:(g + 1) * GW, :].rearrange("p w c -> p c w"),
                           ps[:, 1 + n % 4, 0:CHUNKS * GW].rearrange("p (c w) -> p c w", w=GW)).then_inc(keys_stored, 1)

        def shifted_slot(b, u, n, ring):
            return (b + n) % ring, u + (b + n) // ring

        def count_degrees():
            with ExitStack() as stage:
                take = carve(big_f)
                ids = take([ROWL, 1], I32)
                ids_f = take([ROWL, 1])
                tile_id = take([ROWL, 1])
                place = take([ROWL, 1])
                hot_tile = take([ROWL, T])
                hot_place = take([ROWL, NT])
                iota_t = take([ROWL, T])
                iota_p = take([ROWL, NT])
                g_iotas, g_loaded, g_step = sem("gd_iotas"), sem("gd_loaded"), sem("gd_step")
                g_copied, g_hot, g_counted = sem("gd_copied"), sem("gd_hot"), sem("gd_counted")
                block = stage.enter_context(nc.Block())

                @block.sync
                def _(sp):
                    def load(r):
                        if reached(r, 1):
                            sp.wait_ge(g_copied, r)
                        sp.dma_start(ids, dst.rearrange("(r l o) -> r l o", l=ROWL, o=1)[bass.ds(r, 1)]
                                     .rearrange("r l o -> (r l) o")).then_inc(g_loaded, 16)

                    load(0)
                    with sp.Fori(1, ROWS) as r:
                        load(r)

                @block.gpsimd
                def _(pool):
                    nc.gpsimd.iota(iota_t, [[1, T]], base=0, channel_multiplier=0, allow_small_or_imprecise_dtypes=True)
                    nc.gpsimd.iota(iota_p, [[1, NT]], base=0, channel_multiplier=0,
                                   allow_small_or_imprecise_dtypes=True).then_inc(g_iotas, 1)

                @block.vector
                def _(dve):
                    v = nc.vector
                    dve.wait_ge(g_iotas, 1)

                    def hots(r):
                        dve.wait_ge(g_loaded, 16 * r + 16)
                        v.tensor_copy(ids_f, ids).then_inc(g_copied, 1)
                        dve.wait_ge(g_copied, r + 1)
                        v.tensor_scalar(tile_id, ids_f, 1.0 / NT, 0.5 / NT - 0.5, ALU.mult, ALU.add).then_inc(g_step, 1)
                        dve.wait_ge(g_step, 3 * r + 1)
                        v.tensor_scalar(tile_id, tile_id, 12582912.0, -12582912.0, ALU.add, ALU.add).then_inc(g_step, 1)
                        dve.wait_ge(g_step, 3 * r + 2)
                        v.scalar_tensor_tensor(out=place, in0=tile_id, scalar=-float(NT), in1=ids_f, op0=ALU.mult,
                                               op1=ALU.add).then_inc(g_step, 1)
                        dve.wait_ge(g_step, 3 * r + 3)
                        if reached(r, 1):
                            dve.wait_ge(g_counted, r)
                        v.tensor_scalar(hot_tile, iota_t, tile_id, None, ALU.is_equal)
                        v.tensor_scalar(hot_place, iota_p, place, None, ALU.is_equal).then_inc(g_hot, 1)

                    hots(0)
                    with dve.Fori(1, ROWS) as r:
                        hots(r)

                @block.scalar
                def _(act):
                    act.wait_ge(g_counted, ROWS)
                    nc.scalar.copy(degT[0:NT, :], ps[0:NT, 1, 0:T])

                @block.tensor
                def _(pe):
                    def count(r):
                        pe.wait_ge(g_hot, r + 1)
                        nc.tensor.matmul(ps[0:NT, 1, 0:T], lhsT=hot_place, rhs=hot_tile, start=False, stop=False,
                                         skip_group_check=True).then_inc(g_counted, 1)

                    pe.wait_ge(g_hot, 1)
                    nc.tensor.matmul(ps[0:NT, 1, 0:T], lhsT=zeros[0:ROWL, 0:NT], rhs=hot_tile, start=True, stop=False,
                                     skip_group_check=True)
                    count(0)
                    with pe.Fori(1, ROWS) as r:
                        count(r)

        general = nc.values_load(flag[0:1, 0:1], min_val=0, max_val=1)
        with nc.If(general == 1):
            count_degrees()

        with ExitStack() as stage:
            deg_root, dinv_ready = sem("deg_root"), sem("dinv_ready")
            block = stage.enter_context(nc.Block())

            @block.scalar
            def _(act):
                nc.scalar.activation(dinv[:, :], degT[:, :], ACT.Sqrt, bias=ones[:, 0:1]).then_inc(deg_root, 1)

            @block.vector
            def _(dve):
                dve.wait_ge(deg_root, 1)
                nc.vector.reciprocal(dinv[:, :], dinv[:, :]).then_inc(dinv_ready, 1)
                dve.wait_ge(dinv_ready, 1)
                nc.vector.tensor_scalar(dsc[:, :], dinv[:, :], SH, None, ALU.mult)
                nc.vector.tensor_scalar(dun[:, :], dinv[:, :], 1.0 / SH, None, ALU.mult)

        with ExitStack() as stage:
            RING = 4
            take = carve(big_f)
            x_in = take([P, RING, C])
            xn = take([P, RING, C + 2])
            xt_now = take([P, RING, CB, NT])
            q2t_now = take([P, RING, CB, NT])
            qk2 = take([P, RING, 2 * C])
            k2n = take([P, RING, C])
            k4 = take([P, RING, C])
            square = take([P, C])
            st = take([P, RING, 6])
            mv = take([P, RING, 2])
            rstd = take([P, RING])
            sums = take([P, RING, 2])
            rqk = take([P, RING, 2])
            nq = take([P, RING])
            fq = take([P, RING])
            x_loaded = [sem(f"x_loaded{b}") for b in range(RING)]
            x_out, q_out = [sem(f"x_out{b}") for b in range(RING)], [sem(f"q_out{b}") for b in range(RING)]
            xn_ready, xn_turned, xnT_stored = sem("xn_ready"), sem("xn_turned"), sem("xnT_stored")
            qk_ready, sq_ready, recip_ready = sem("qk_ready"), sem("sq_ready"), sem("recip_ready")
            k4_ready, k2n_ready, kx_done = sem("k4_ready"), sem("k2n_ready"), sem("kx_done")
            q2f_ready, q2_turned, q2T_stored = sem("q2f_ready"), sem("q2_turned"), sem("q2T_stored")
            std_ready, rstd_ready, nq_root = sem("std_ready"), sem("rstd_ready"), sem("nq_root")
            ln_step, hi_ready, fq_step, zeroed = sem("ln_step"), sem("hi_ready"), sem("fq_step"), sem("zeroed")

            block = stage.enter_context(nc.Block())

            @block.sync
            def _(sp):
                def tile(t, b, u):
                    if within(t, T):
                        if reached(t, RING):
                            sp.wait_ge(xn_ready, t - RING + 1)
                        sp.dma_start(x_in[0:NT, b, :], x[bass.ds(t * NT, NT), :]).then_inc(x_loaded[b], 16)
                    if reached(t, 3) and within(t, T + 3):
                        sp.wait_ge(xnT_stored, t - 2)
                        sp.dma_start(xT_dram[bass.ds(t - 3, 1), :, 0:CB * NT].rearrange("t p n -> (t p) n"),
                                     xt_now[:, (b - 3) % RING].rearrange("p a b -> p (a b)")
                                     ).then_inc(x_out[(b - 3) % RING], 16)
                    if reached(t, 6):
                        sp.wait_ge(q2T_stored, t - 5)
                        sp.dma_start(xT_dram[bass.ds(t - 6, 1), :, CB * NT:2 * CB * NT].rearrange("t p n -> (t p) n"),
                                     q2t_now[:, (b - 6) % RING].rearrange("p a b -> p (a b)")
                                     ).then_inc(q_out[(b - 6) % RING], 16)

                pipeline(sp, tile, T, RING, lag=6)
                for b in range(RING):
                    sp.wait_ge(x_out[b], 16 * len(range(b, T, RING)))
                    sp.wait_ge(q_out[b], 16 * len(range(b, T, RING)))

            @block.vector
            def _(dve):
                v = nc.vector
                v.memset(xn[:, :, C:C + 2], 1.0).then_inc(zeroed, 1)
                dve.wait_ge(zeroed, 1)

                def stats(t, b, u):
                    dve.wait_ge(x_loaded[b], 16 * u + 16)
                    v.bn_stats(st[0:NT, b, :], x_in[0:NT, b, :]).then_inc(ln_step, 1)
                    dve.wait_ge(ln_step, 2 * t + 1)
                    v.memset(rstd[0:NT, b:b + 1], 0.0)
                    v.bn_aggr(mv[0:NT, b, :], st[0:NT, b, :]).then_inc(ln_step, 1)

                def norm(t, b):
                    dve.wait_ge(std_ready, t + 1)
                    v.reciprocal(rstd[0:NT, b:b + 1], rstd[0:NT, b:b + 1]).then_inc(rstd_ready, 1)
                    dve.wait_ge(rstd_ready, t + 1)
                    if reached(t, RING):
                        dve.wait_ge(kx_done, t - RING + 1)
                    v.tensor_scalar(xn[0:NT, b, 0:C], x_in[0:NT, b, :], mv[0:NT, b, 0:1], rstd[0:NT, b:b + 1],
                                    ALU.subtract, ALU.mult).then_inc(xn_ready, 1)
                    dve.wait_ge(xn_ready, t + 1)
                    v.tensor_scalar(hs[0:NT, bass.ds(t, 1), 0:C].rearrange("p o c -> p (o c)"), xn[0:NT, b, 0:C],
                                    dsc[0:NT, bass.ds(t, 1)], None, ALU.mult).then_inc(hi_ready, 1)

                def halves(t, b):
                    dve.wait_ge(hi_ready, t + 1)
                    v.scalar_tensor_tensor(out=hs[0:NT, bass.ds(t, 1), C:2 * C].rearrange("p o c -> p (o c)"),
                                           in0=xn[0:NT, b, 0:C], scalar=dsc[0:NT, bass.ds(t, 1)],
                                           in1=hs[0:NT, bass.ds(t, 1), 0:C].rearrange("p o c -> p (o c)"),
                                           op0=ALU.mult, op1=ALU.subtract)

                def over_sums(t, b):
                    dve.wait_ge(sq_ready, 2 * t + 2)
                    if reached(t, RING):
                        dve.wait_ge(k4_ready, 2 * (t - RING) + 2)
                    v.tensor_scalar(rqk[0:NT, b, :], sums[0:NT, b, :], 1e-7, None, ALU.add).then_inc(recip_ready, 1)
                    dve.wait_ge(recip_ready, 2 * t + 1)
                    v.reciprocal(rqk[0:NT, b, :], rqk[0:NT, b, :]).then_inc(recip_ready, 1)
                    dve.wait_ge(recip_ready, 2 * t + 2)
                    v.tensor_scalar(k2n[0:NT, b, :], qk2[0:NT, b, C:2 * C], rqk[0:NT, b, 1:2], None,
                                    ALU.mult).then_inc(k2n_ready, 1)

                def over_norm(t, b):
                    dve.wait_ge(nq_root, t + 1)
                    v.tensor_scalar(fq[0:NT, b:b + 1], nq[0:NT, b:b + 1], 1e-12, None, ALU.max).then_inc(fq_step, 1)
                    dve.wait_ge(fq_step, 3 * t + 1)
                    v.reciprocal(fq[0:NT, b:b + 1], fq[0:NT, b:b + 1]).then_inc(fq_step, 1)
                    dve.wait_ge(fq_step, 3 * t + 2)
                    v.tensor_tensor(fq[0:NT, b:b + 1], fq[0:NT, b:b + 1], rqk[0:NT, b, 0:1], ALU.mult).then_inc(fq_step, 1)
                    dve.wait_ge(fq_step, 3 * t + 3)
                    v.tensor_scalar(qk2[0:NT, b, 0:C], qk2[0:NT, b, 0:C], fq[0:NT, b:b + 1], None,
                                    ALU.mult).then_inc(q2f_ready, 1)

                def tile(t, b, u):
                    if reached(t, -1) and within(t, T - 1):
                        norm(t + 1, (b + 1) % RING)
                    if within(t, T - 2):
                        stats(t + 2, *shifted_slot(b, u, 2, RING))
                    if reached(t, 2):
                        over_norm(t - 2, (b - 2) % RING)
                    if reached(t, 1) and within(t, T + 1):
                        over_sums(t - 1, (b - 1) % RING)
                    if reached(t, -1) and within(t, T - 1):
                        halves(t + 1, (b + 1) % RING)

                pipeline(dve, tile, T, RING, lead=2, lag=2)

            @block.tensor
            def _(pe):
                te = nc.tensor

                def turn(t, b):
                    pe.wait_ge(xn_ready, t + 1)
                    if reached(t, 2):
                        pe.wait_ge(xnT_stored, t - 1)
                    for c in range(CB):
                        mm = te.transpose(ps[:, 3 * (b % 2), c * NT:(c + 1) * NT],
                                          xn[0:NT, b, c * P:(c + 1) * P], ident[0:NT, 0:NT])
                    mm.then_inc(xn_turned, 1)

                def project(t, b):
                    pe.wait_ge(xnT_stored, t + 1)
                    if reached(t, 2):
                        pe.wait_ge(sq_ready, 2 * t - 2)
                    te.matmul(ps[0:NT, 1 + b % 2, :], lhsT=ones3[:, 0:NT], rhs=brow, start=True, stop=False)
                    for c in range(CB):
                        mm = te.matmul(ps[0:NT, 1 + b % 2, :], lhsT=xt_now[:, b, c, :], rhs=wqk[:, c, :],
                                       start=False, stop=(c == CB - 1))
                    mm.then_inc(qk_ready, 1)

                def gather(t, b):
                    pe.wait_ge(k2n_ready, t + 1)
                    for c in range(CB):
                        te.matmul(ps[:, 4 + c, 0:C + 2], lhsT=k2n[0:NT, b, c * P:(c + 1) * P],
                                  rhs=xn[0:NT, b, :], start=False, stop=False, skip_group_check=True)
                    pe.wait_ge(k4_ready, 2 * t + 2)
                    for c in range(CB):
                        mm = te.matmul(ps[:, 4 + c, C + 2:C + 3], lhsT=k4[0:NT, b, c * P:(c + 1) * P],
                                       rhs=ones[0:NT, 0:1], start=False, stop=False, skip_group_check=True)
                    mm.then_inc(kx_done, 1)
                    pe.wait_ge(q2f_ready, t + 1)
                    if reached(t, 2):
                        pe.wait_ge(q2T_stored, t - 1)
                    for c in range(CB):
                        mm = te.transpose(ps[:, 6 + b % 2, c * NT:(c + 1) * NT],
                                          qk2[0:NT, b, c * P:(c + 1) * P], ident[0:NT, 0:NT])
                    mm.then_inc(q2_turned, 1)

                def tile(t, b, u):
                    if reached(t, 0) and within(t, T):
                        project(t, b)
                    if within(t, T - 1):
                        turn(t + 1, (b + 1) % RING)
                    if reached(t, 2):
                        gather(t - 2, (b - 2) % RING)

                for c in range(CB):
                    te.matmul(ps[:, 4 + c, 0:C + 3], lhsT=zeros[:, :], rhs=wqk[:, 0, 0:C + 3], start=True, stop=False,
                              skip_group_check=True)
                pipeline(pe, tile, T, RING, lead=1, lag=2)

            @block.scalar
            def _(act):
                a = nc.scalar

                def std(t, b):
                    act.wait_ge(ln_step, 2 * t + 2)
                    a.activation(rstd[0:NT, b:b + 1], mv[0:NT, b, 1:2], ACT.Sqrt, bias=eps[0:NT, 0:1]).then_inc(std_ready, 1)

                def keep(t, b, u):
                    act.wait_ge(xn_turned, t + 1)
                    if reached(t, RING):
                        act.wait_ge(qk_ready, t - RING + 1)
                        act.wait_ge(x_out[b], 16 * u)
                    a.copy(xt_now[:, b].rearrange("p a b -> p (a b)"),
                           ps[:, 3 * (b % 2), 0:CB * NT]).then_inc(xnT_stored, 1)

                def squares(t, b):
                    act.wait_ge(qk_ready, t + 1)
                    if reached(t, RING):
                        act.wait_ge(q2_turned, t - RING + 1)
                        act.wait_ge(k2n_ready, t - RING + 1)
                    for h in range(2):
                        a.activation(qk2[0:NT, b, h * C:(h + 1) * C], ps[0:NT, 1 + b % 2, h * C:(h + 1) * C], ACT.Square,
                                     accum_out=sums[0:NT, b, h:h + 1]).then_inc(sq_ready, 1)

                def norms(t, b):
                    act.wait_ge(recip_ready, 2 * t + 2)
                    a.activation(square[0:NT, :], qk2[0:NT, b, 0:C], ACT.Square, scale=rqk[0:NT, b, 0:1],
                                 accum_out=nq[0:NT, b:b + 1]).then_inc(k4_ready, 1)
                    act.wait_ge(k4_ready, 2 * t + 1)
                    a.activation(nq[0:NT, b:b + 1], nq[0:NT, b:b + 1], ACT.Sqrt).then_inc(nq_root, 1)
                    if reached(t, RING):
                        act.wait_ge(kx_done, t - RING + 1)
                    a.activation(k4[0:NT, b, :], qk2[0:NT, b, C:2 * C], ACT.Square, scale=rqk[0:NT, b, 1:2]).then_inc(k4_ready, 1)

                def turned(t, b, u):
                    act.wait_ge(q2_turned, t + 1)
                    if reached(t, RING):
                        act.wait_ge(q_out[b], 16 * u)
                    a.copy(q2t_now[:, b].rearrange("p a b -> p (a b)"),
                           ps[:, 6 + b % 2, 0:CB * NT]).then_inc(q2T_stored, 1)

                def tile(t, b, u):
                    if reached(t, 2) and within(t, T + 2):
                        norms(t - 2, (b - 2) % RING)
                    if within(t, T - 2):
                        std(t + 2, (b + 2) % RING)
                    if reached(t, -1) and within(t, T - 1):
                        keep(t + 1, *shifted_slot(b, u, 1, RING))
                    if reached(t, 0) and within(t, T):
                        squares(t, b)
                    if reached(t, 3):
                        turned(t - 3, *shifted_slot(b, u, -3, RING))

                pipeline(act, tile, T, RING, lead=2, lag=3)

        with ExitStack() as stage:
            take = carve(big_f)
            kx = take([P, CB, C + 3])
            kxT = take([P, CB, CB, P])
            rn = take([P, CB])
            mp = take([P, CB, C])
            wscaled = take([P, CB * HG])
            square = take([P, CB * C])
            wlog_f = wlog[:, :, :].rearrange("p a b -> p (a b)")
            split_step = sem("split_step")
            sums_kept, rn_step, m_kept = sem("sums_kept"), sem("rn_step"), sem("m_kept")
            kv_product = sem("kv_product")
            block = stage.enter_context(nc.Block())

            @block.gpsimd
            def _(pool):
                pool.wait_ge(split_step, 2)
                nc.gpsimd.partition_all_reduce(small[:, 11:13], small[:, 9:11], P, RMAX).then_inc(split_step, 1)

            @block.scalar
            def _(act):
                nc.scalar.activation(square, w1[:, :, :].rearrange("p a b -> p (a b)"), ACT.Square,
                                     accum_out=small[:, 10:11]).then_inc(split_step, 1)
                act.wait_ge(split_step, 3)
                nc.scalar.activation(small[:, 15:16], small[:, 12:13], ACT.Sqrt, scale=float(C * P)).then_inc(split_step, 1)
                act.wait_ge(sums_kept, 1)
                nc.scalar.activation(rn, kx[:, :, C + 2], ACT.Sqrt).then_inc(rn_step, 1)

            @block.vector
            def _(dve):
                v = nc.vector
                v.tensor_copy(kx, ps[:, 4:6, 0:C + 3]).then_inc(sums_kept, 1)
                v.tensor_reduce(small[:, 13:14], b1b[:, :], AX.X, ALU.max, apply_absolute_value=True)
                v.tensor_reduce(small[:, 9:10], wlog_f, AX.X, ALU.max, apply_absolute_value=True).then_inc(split_step, 1)
                dve.wait_ge(rn_step, 1)
                v.tensor_scalar(rn, rn, 1e-12, None, ALU.max).then_inc(rn_step, 1)
                dve.wait_ge(rn_step, 2)
                v.reciprocal(rn, rn).then_inc(rn_step, 1)
                dve.wait_ge(rn_step, 3)
                v.tensor_scalar(rn, rn, float(N) ** -0.5, None, ALU.mult).then_inc(rn_step, 1)
                dve.wait_ge(kv_product, 1)
                v.tensor_copy(kxT.rearrange("p a b c -> p (a b c)"), ps[:, 0, :]).then_inc(sums_kept, 1)
                dve.wait_ge(split_step, 4)
                v.tensor_scalar(small[:, 14:15], small[:, 11:12], 1e-30, None, ALU.max)
                v.tensor_scalar(small[:, 15:16], small[:, 15:16], small[:, 13:14], 1e-30, ALU.add, ALU.max
                                ).then_inc(split_step, 1)
                dve.wait_ge(split_step, 5)
                v.tensor_scalar(small[:, 16:18].bitcast(I32), small[:, 14:16].bitcast(I32), EXPONENT, None, ALU.bitwise_and)
                v.tensor_scalar(small[:, 18:20].bitcast(I32), small[:, 14:16].bitcast(I32), EXPONENT, EXPONENT,
                                ALU.bitwise_and, ALU.bitwise_xor).then_inc(split_step, 1)
                dve.wait_ge(split_step, 6)
                v.tensor_scalar(small[:, 20:22], small[:, 16:18], 2.0 ** -14, None, ALU.mult)
                v.tensor_scalar(small[:, 22:24], small[:, 18:20], 2.0 ** 13, None, ALU.mult).then_inc(split_step, 1)
                dve.wait_ge(split_step, 7)
                v.tensor_scalar(dsc[:, :], dinv[:, :], small[:, 23:24], None, ALU.mult)
                v.tensor_scalar(dun2[:, :], dinv[:, :], small[:, 21:22], None, ALU.mult)
                v.tensor_scalar(wscaled, wlog_f, small[:, 22:23], None, ALU.mult).then_inc(split_step, 1)
                dve.wait_ge(split_step, 8)
                v.tensor_copy(wlog16[:, 0].rearrange("p a b -> p (a b)"), wscaled).then_inc(split_step, 1)
                dve.wait_ge(split_step, 9)
                v.tensor_tensor(wlog16[:, 1].rearrange("p a b -> p (a b)"), wscaled,
                                wlog16[:, 0].rearrange("p a b -> p (a b)"), ALU.subtract)
                dve.wait_ge(kv_product, 2)
                dve.wait_ge(rn_step, 4)
                dve.wait_ge(sums_kept, 1)
                for c in range(CB):
                    v.scalar_tensor_tensor(out=mp[:, c, :], in0=bvw, scalar=kx[:, c, C:C + 1],
                                           in1=ps[:, 1, c * C:(c + 1) * C], op0=ALU.mult, op1=ALU.add).then_inc(m_kept, 1)
                dve.wait_ge(m_kept, CB)
                for c in range(CB):
                    v.tensor_scalar(mkv[:, c, :], mp[:, c, :], rn[:, c:c + 1], None, ALU.mult)

            @block.tensor
            def _(pe):
                te = nc.tensor
                pe.wait_ge(sums_kept, 1)
                for i in range(CB):
                    for c in range(CB):
                        mm = te.transpose(ps[:, 0, (i * CB + c) * P:(i * CB + c + 1) * P],
                                          kx[:, c, i * P:(i + 1) * P], ident[:, :])
                mm.then_inc(kv_product, 1)
                pe.wait_ge(sums_kept, 2)
                for c in range(CB):
                    for i in range(CB):
                        mm = te.matmul(ps[:, 1, c * C:(c + 1) * C], lhsT=kxT[:, i, c, :], rhs=wvo[:, i, :],
                                       start=(i == 0), stop=(i == CB - 1))
                mm.then_inc(kv_product, 1)

        NB = 4
        s_loaded, s_out = [sem(f"s_loaded{b}") for b in range(NB)], [sem(f"s_out{b}") for b in range(NB)]
        s_mixed, s_biased, s_ready = sem("s_mixed"), sem("s_biased"), sem("s_ready")

        def stream(call, region, turned_of, residual, weights, bias, to):
            past = T * call

            def past_in(b):
                return call * len(range(b, T, NB))

            with ExitStack() as stage:
                take = carve(region)
                turned_in = take([P, NB, len(weights) * NT])
                rows_in = take([P, NB, C])
                res = take([P, NB, C])
                block = stage.enter_context(nc.Block())

                @block.sync
                def _(sp):
                    def tile(t, b, u):
                        if reached(t, NB):
                            sp.wait_ge(s_ready, t - NB + 1 + past)
                        sp.dma_start(turned_in[:, b, :], turned_of(t)).then_inc(s_loaded[b], 16)
                        sp.dma_start(rows_in[0:NT, b, :], residual[bass.ds(t * NT, NT), :]).then_inc(s_loaded[b], 16)

                    pipeline(sp, tile, T, NB)

                @block.gpsimd
                def _(pool):
                    def tile(t, b, u):
                        pool.wait_ge(s_loaded[b], 32 * u + 32 + 32 * past_in(b))
                        nc.gpsimd.tensor_tensor(rows_in[0:NT, b, :], rows_in[0:NT, b, :], bias[0:NT, :],
                                                ALU.add).then_inc(s_biased, 1)

                    pipeline(pool, tile, T, NB)

                @block.tensor
                def _(pe):
                    def tile(t, b, u):
                        pe.wait_ge(s_loaded[b], 32 * u + 32 + 32 * past_in(b))
                        if reached(t, NB):
                            pe.wait_ge(s_ready, t - NB + 1 + past)
                        for i, w in enumerate(weights):
                            mm = nc.tensor.matmul(ps[0:NT, b, 0:C], lhsT=turned_in[:, b, i * NT:(i + 1) * NT], rhs=w,
                                                  start=(i == 0), stop=(i == len(weights) - 1))
                        mm.then_inc(s_mixed, 1)

                    pipeline(pe, tile, T, NB)

                @block.vector
                def _(dve):
                    def tile(t, b, u):
                        dve.wait_ge(s_mixed, t + 1 + past)
                        dve.wait_ge(s_biased, t + 1 + past)
                        if reached(t, NB):
                            dve.wait_ge(s_out[b], 16 * (u + past_in(b)))
                        nc.vector.tensor_tensor(res[0:NT, b, :], ps[0:NT, b, 0:C], rows_in[0:NT, b, :],
                                                ALU.add).then_inc(s_ready, 1)

                    pipeline(dve, tile, T, NB)

                @block.scalar
                def _(act):
                    def tile(t, b, u):
                        act.wait_ge(s_ready, t + 1 + past)
                        act.dma_start(to[bass.ds(t * NT, NT), :], res[0:NT, b, :]).then_inc(s_out[b], 16)

                    pipeline(act, tile, T, NB)
                    for b in range(NB):
                        act.wait_ge(s_out[b], 16 * (len(range(b, T, NB)) + past_in(b)))

        stream(0, big_f, lambda t: xT_dram[bass.ds(t, 1)].rearrange("t p n -> (t p) n"), x,
               [wvo[:, 0, :], wvo[:, 1, :], mkv[:, 0, :], mkv[:, 1, :]], bvo, base_dram)

        BATCH = 10
        assert T % BATCH == 0
        BATCHES = T // BATCH
        e_nodes, e_stored, e_src, e_dst_ids = sem("e_nodes"), sem("e_stored"), sem("e_src"), sem("e_dst_ids")
        e_wide, e_scale = sem("e_wide"), sem("e_scale")
        e_turn, e_gathered, e_dst, e_hot, e_multiplied, e_added = (
            sem("e_turn"), sem("e_gathered"), sem("e_dst"), sem("e_hot"), sem("e_multiplied"), sem("e_added"))

        def sum_edges(layer, halves, scratch, un):
            acc = big[:, T:2 * T, :]
            with ExitStack() as stage:
                block = stage.enter_context(nc.Block())

                @block.vector
                def _(dve):
                    nc.vector.tensor_tensor(acc[0:NT], halves[0:NT, :, 0:C], halves[0:NT, :, C:2 * C], ALU.add)
                    nc.vector.memset(key_lo[:, :, :], 0.0).then_inc(e_wide, 1)

                @block.scalar
                def _(act):
                    act.wait_ge(e_wide, layer + 1)

                @block.gpsimd
                def _(pool):
                    pool.wait_ge(e_wide, layer + 1)

                @block.tensor
                def _(pe):
                    pe.wait_ge(e_wide, layer + 1)

                @block.sync
                def _(sp):
                    sp.wait_ge(e_wide, layer + 1)

            with ExitStack() as stage:
                take = carve(scratch)
                src_ids = take([ROWL, 1], I32)
                dst_ids = take([ROWL, 1], I32)
                dst_f = take([ROWL, 1])
                msg = take([ROWL, C])
                turn = take([ROWL, 1])
                hot = take([ROWL, BATCH * NT])
                nodes = take([ROWL, N])
                rows_before, steps_before = layer * ROWS, layer * ROWS * BATCHES
                block = stage.enter_context(nc.Block())

                @block.sync
                def _(sp):
                    sp.dma_start(h_dram.rearrange("(t p) c -> p t c", p=NT), acc[0:NT]).then_inc(e_stored, 16)

                    def load(r):
                        if reached(r, 1):
                            sp.wait_ge(e_multiplied, r * BATCHES + steps_before)
                        for to, of, s in ((src_ids, src, e_src), (dst_ids, dst, e_dst_ids)):
                            sp.dma_start(to, of.rearrange("(r l o) -> r l o", l=ROWL, o=1)[bass.ds(r, 1)]
                                         .rearrange("r l o -> (r l) o")).then_inc(s, 16)

                    load(0)
                    with sp.Fori(1, ROWS) as r:
                        load(r)

                @block.scalar
                def _(act):
                    with act.Fori(0, ROWS) as r:
                        act.wait_ge(e_dst_ids, 16 * r + 16 + 16 * rows_before)
                        nc.scalar.copy(dst_f, dst_ids).then_inc(e_dst, 1)

                @block.gpsimd
                def _(pool):
                    nc.gpsimd.iota(nodes, [[1, N]], base=0, channel_multiplier=0,
                                   allow_small_or_imprecise_dtypes=True).then_inc(e_nodes, 1)
                    pool.wait_ge(e_stored, 16 * layer + 16)
                    nc.gpsimd.memset(turn, 0.0).then_inc(e_turn, 1)
                    with pool.Fori(0, ROWS) as r:
                        pool.wait_ge(e_turn, r + 1 + rows_before + layer)
                        pool.wait_ge(e_src, 16 * r + 16 + 16 * rows_before)
                        nc.gpsimd.tensor_tensor(turn, turn, turn, ALU.add).then_inc(e_turn, 1)
                        pool.indirect_dma_start(
                            out=msg, out_offset=None, in_=h_dram,
                            in_offset=bass.IndirectOffsetOnAxis(ap=src_ids[:, 0:1], axis=0)).then_inc(e_gathered, 16)

                @block.vector
                def _(dve):
                    v = nc.vector
                    dve.wait_ge(e_nodes, layer + 1)
                    dve.wait_ge(e_stored, 16 * layer + 16)
                    v.memset(small[:, 0:1], 0.0).then_inc(e_added, 1)
                    with dve.Fori(0, ROWS) as r:
                        with dve.Fori(0, BATCHES) as m:
                            dve.wait_ge(e_dst, r + 1 + rows_before)
                            n = r * BATCHES + m + steps_before
                            dve.wait_ge(e_added, n + 1 + layer)
                            v.tensor_scalar(hot, nodes[:, bass.ds(m * (BATCH * NT), BATCH * NT)], dst_f, None,
                                            ALU.is_equal).then_inc(e_hot, 1)
                            dve.wait_ge(e_multiplied, n + 1)
                            rows = acc[0:NT, bass.ds(m * BATCH, BATCH), :].rearrange("p t c -> p (t c)")
                            v.tensor_tensor(rows, rows, ps[0:NT, 0:BATCH // 2, :].rearrange("p b c -> p (b c)"),
                                            ALU.add).then_inc(e_added, 1)
                @block.tensor
                def _(pe):
                    with pe.Fori(0, ROWS) as r:
                        with pe.Fori(0, BATCHES) as m:
                            pe.wait_ge(e_gathered, 16 * r + 16 + 16 * rows_before)
                            pe.wait_ge(e_hot, r * BATCHES + m + 1 + steps_before)
                            for h in range(BATCH):
                                mm = nc.tensor.matmul(ps[0:NT, h // 2, (h % 2) * C:(h % 2 + 1) * C],
                                                      lhsT=hot[:, h * NT:(h + 1) * NT], rhs=msg, start=True, stop=True)
                            mm.then_inc(e_multiplied, 1)

            with ExitStack() as stage:
                block = stage.enter_context(nc.Block())
                s0 = layer * 6

                @block.gpsimd
                def _(pool):
                    pool.wait_ge(e_scale, s0 + 1)
                    nc.gpsimd.partition_all_reduce(small[:, 3:4], small[:, 2:3], P, RMAX).then_inc(e_scale, 1)

                @block.scalar
                def _(act):
                    act.wait_ge(e_scale, s0 + 5)
                    nc.scalar.activation(halves[0:NT, :, 0:C], acc[0:NT], ACT.Identity,
                                         scale=small[0:NT, 7:8]).then_inc(e_scale, 1)

                @block.vector
                def _(dve):
                    v = nc.vector
                    v.tensor_reduce(small[0:NT, 2:3], acc[0:NT].rearrange("p t c -> p (t c)"), AX.X, ALU.max,
                                    apply_absolute_value=True).then_inc(e_scale, 1)
                    dve.wait_ge(e_scale, s0 + 2)
                    v.tensor_scalar(small[:, 4:5], small[:, 3:4], 1e-30, None, ALU.max).then_inc(e_scale, 1)
                    dve.wait_ge(e_scale, s0 + 3)
                    v.tensor_scalar(small[:, 5:6].bitcast(I32), small[:, 4:5].bitcast(I32), EXPONENT, None, ALU.bitwise_and)
                    v.tensor_scalar(small[:, 6:7].bitcast(I32), small[:, 4:5].bitcast(I32), EXPONENT, EXPONENT,
                                    ALU.bitwise_and, ALU.bitwise_xor).then_inc(e_scale, 1)
                    dve.wait_ge(e_scale, s0 + 4)
                    v.tensor_scalar(small[:, 7:8], small[:, 6:7], 2.0 ** 13, None, ALU.mult)
                    v.tensor_scalar(small[:, 8:9], small[:, 5:6], 2.0 ** -14, None, ALU.mult).then_inc(e_scale, 1)
                    dve.wait_ge(e_scale, s0 + 5)
                    v.tensor_scalar(un[:, :], un[:, :], small[:, 8:9], None, ALU.mult)
                    dve.wait_ge(e_scale, s0 + 6)
                    v.scalar_tensor_tensor(out=halves[0:NT, :, C:2 * C], in0=acc[0:NT], scalar=small[0:NT, 7:8],
                                           in1=halves[0:NT, :, 0:C], op0=ALU.mult, op1=ALU.subtract)

        with nc.If(general == 1):
            sum_edges(0, hs, big_f[:, 0:T * C], dun)

        RING = 5
        ACT_LO = (4, 9, 14, 19, 24)
        UNITS = -(-WPT // 2)
        with ExitStack() as stage:
            take = carve(big_f[:, T * C:])
            hot_hi = take([P, RING, CHUNKS, KC], F16)
            hot_lo = take([P, RING, CHUNKS, P], F16)
            iota_hi = take([P, KC], F16)
            iota_lo = take([P, P], F16)
            apart = take([P, CHUNKS, P], F16)
            agg = take([P, 2, C])
            low = take([P, 2, C])
            aggT = take([P, 2, CB, NT])
            zb = take([P, 2, C])
            zs = take([P, 2, C])
            low_made, looped = sem("low_made"), sem("looped")
            apart_ready, act_lo_ready = sem("apart_ready"), sem("act_lo_ready")
            iotas_ready, pads_ready = sem("l1_iotas_ready"), sem("pads_ready")
            hot_ready, built, at_stored = sem("hot_ready"), sem("built"), sem("at_stored")
            at_out = [sem("at_out0"), sem("at_out1")]
            summed, low_ready, agg_ready = sem("summed"), sem("low_ready"), sem("agg_ready")
            agg_turned, aggT_ready, multiplied = sem("agg_turned"), sem("aggT_ready"), sem("multiplied")
            zb_ready, z_ready = sem("zb_ready"), sem("z_ready")
            block = stage.enter_context(nc.Block())

            @block.gpsimd
            def _(pool):
                g = nc.gpsimd
                g.iota(iota_hi, [[1, KC]], base=0, channel_multiplier=0, allow_small_or_imprecise_dtypes=True)
                g.iota(iota_lo, [[1, P]], base=1, channel_multiplier=0,
                       allow_small_or_imprecise_dtypes=True).then_inc(iotas_ready, 1)
                for b in range(2):
                    g.memset(at[:, b, :].rearrange("p (k d) -> p k d", d=P)[:, :, NT:P], 0.0).then_inc(pads_ready, 1)
                pool.wait_ge(pads_ready, 2)
                g.memset(big_f[96:P, 0:T * C], 0.0).then_inc(pads_ready, 1)
                pool.wait_ge(pads_ready, 3)

                def self_loops(t, b):
                    last = (UNITS - 1) * 2 * WIN
                    for ready, cols in ((t * UNITS + UNITS - 1, slice(0, last)), (t * UNITS + UNITS, slice(last, NT))):
                        pool.wait_ge(at_stored, ready)
                        block_t = at[:, b, bass.ds(t * P + cols.start, cols.stop - cols.start)]
                        g.tensor_tensor(block_t, block_t, ident16[:, cols], ALU.add).then_inc(looped, 1)

                def lower(t, b):
                    pool.wait_ge(z_ready, t + 1)
                    g.tensor_tensor(hs2[0:NT, bass.ds(t, 1), C:2 * C].rearrange("p t c -> p (t c)"), zs[0:NT, b, :],
                                    hs2[0:NT, bass.ds(t, 1), 0:C].rearrange("p t c -> p (t c)"),
                                    ALU.subtract).then_inc(low_made, 1)

                def tile(t, b, u):
                    if within(t, T - 1):
                        self_loops(t + 1, 1 - b)
                    if reached(t, 1):
                        lower(t - 1, 1 - b)

                pipeline(pool, tile, T, 2, lead=1, lag=1)

            @block.vector
            def _(dve):
                v = nc.vector
                dve.wait_ge(iotas_ready, 1)

                def hots(t, i):
                    w, s = t * WPT + i, i % RING
                    if reached(w, RING):
                        dve.wait_ge(built, w - RING + 1)
                    for c in range(CHUNKS):
                        last = v.tensor_scalar(hot_hi[:, s, c, :], iota_hi, key_hi[:, bass.ds(w, 1), c], None,
                                               ALU.is_equal)
                        if i not in ACT_LO:
                            last = v.tensor_scalar(hot_lo[:, s, c, :], iota_lo, key_lo[:, bass.ds(w, 1), c], None,
                                                   ALU.is_equal)
                    last.then_inc(hot_ready, 1)

                def gather(t, b):
                    dve.wait_ge(low_ready, t + 1)
                    if reached(t, 2):
                        dve.wait_ge(agg_turned, t - 1)
                    v.tensor_tensor(agg[0:NT, b, :], ps[0:NT, 2 + b, 0:C], low[0:NT, b, :], ALU.add).then_inc(agg_ready, 1)

                def bias(t, b):
                    dve.wait_ge(multiplied, t + 1)
                    if reached(t, 2):
                        dve.wait_ge(z_ready, t - 1)
                    v.scalar_tensor_tensor(out=zb[0:NT, b, :], in0=ps[0:NT, 5, b * C:(b + 1) * C],
                                           scalar=dun[0:NT, bass.ds(t, 1)], in1=b1b[0:NT, :],
                                           op0=ALU.mult, op1=ALU.add).then_inc(zb_ready, 1)

                def tile(t, b, u):
                    for i in range(WPT):
                        if within(t, T - 1):
                            hots(t + 1, i)
                        if i == 7 and reached(t, 1):
                            gather(t - 1, 1 - b)
                        if i == 17 and reached(t, 1):
                            bias(t - 1, 1 - b)

                pipeline(dve, tile, T, 2, lead=1, lag=1)

            @block.tensor
            def _(pe):
                te = nc.tensor

                def build(t, i, b):
                    w, s, unit = t * WPT + i, i % RING, t * UNITS + i // 2
                    pe.wait_ge(hot_ready, w + 1)
                    if i in ACT_LO:
                        pe.wait_ge(act_lo_ready, t * len(ACT_LO) + ACT_LO.index(i) + 1)
                    if i % 2 == 0 and reached(unit, 2):
                        pe.wait_ge(at_stored, unit - 1)
                    for c in range(CHUNKS):
                        mm = te.matmul(ps[:, (b * UNITS + i // 2) % 2, i % 2 * KC:(i % 2 + 1) * KC],
                                       lhsT=hot_lo[:, s, c, :], rhs=hot_hi[:, s, c, :],
                                       start=(c == 0), stop=(c == CHUNKS - 1))
                    mm.then_inc(built, 1)

                def aggregate(t, b, ks):
                    for k in ks:
                        if k == 0:
                            pe.wait_ge(looped, 2 * t + 2)
                            if reached(t, 2):
                                pe.wait_ge(agg_ready, t - 1)
                        mm = te.matmul(ps[:, 2 + b, :], lhsT=at[:, b, k * P:(k + 1) * P], rhs=hs[:, k, :],
                                       start=(k == 0), stop=(k == T - 1))
                        if k == T - 1:
                            mm.then_inc(summed, 1)

                def turn(t, b):
                    pe.wait_ge(agg_ready, t + 1)
                    for c in range(CB):
                        mm = te.transpose(ps[:, 4, (b * CB + c) * NT:(b * CB + c + 1) * NT],
                                          agg[0:NT, b, c * P:(c + 1) * P], ident[0:NT, 0:NT])
                    mm.then_inc(agg_turned, 1)

                def multiply(t, b):
                    pe.wait_ge(aggT_ready, t + 1)
                    for c in range(CB):
                        mm = te.matmul(ps[0:NT, 5, b * C:(b + 1) * C], lhsT=aggT[:, b, c, :], rhs=w1[:, c, :],
                                       start=(c == 0), stop=(c == CB - 1))
                    mm.then_inc(multiplied, 1)

                def tile(t, b, u):
                    for i in range(WPT):
                        if within(t, T - 1):
                            build(t + 1, i, 1 - b)
                        if reached(t, 0) and within(t, T) and i >= 2:
                            aggregate(t, b, range((i - 2) * T // (WPT - 2), (i - 1) * T // (WPT - 2)))
                        if i == 8 and reached(t, 1):
                            turn(t - 1, 1 - b)
                        if i == 11 and reached(t, 1):
                            multiply(t - 1, 1 - b)

                pe.wait_ge(pads_ready, 2)
                pipeline(pe, tile, T, 2, lead=1, lag=1)

            @block.scalar
            def _(act):
                a = nc.scalar
                act.wait_ge(iotas_ready, 1)
                LO_BEFORE = [max(0, i // 2 - 2) for i in ACT_LO]

                def store(t, m, b, u):
                    here = min(2, WPT - 2 * m)
                    act.wait_ge(built, t * WPT + 2 * m + here)
                    if m == 0 and reached(t, 2):
                        act.wait_ge(summed, t - 1)
                        act.wait_ge(at_out[b], 16 * u)
                    bank = (b * UNITS + m) % 2
                    to = at[:, b, :].rearrange("p (k d) -> p k d", d=P)[:, :, 2 * m * WIN:(2 * m + here) * WIN]
                    a.copy(to.rearrange("p k (i j) -> p i k j", j=WIN),
                           ps[:, bank, 0:here * KC].rearrange("p (i k j) -> p i k j", i=here, j=WIN)
                           ).then_inc(at_stored, 1)

                def low_hots(t, n):
                    i = ACT_LO[n]
                    w, s, k = t * WPT + i, i % RING, t * len(ACT_LO) + n
                    if reached(w, RING):
                        act.wait_ge(built, w - RING + 1)
                    if reached(k, 1):
                        act.wait_ge(act_lo_ready, k)
                    for c in range(CHUNKS):
                        a.activation(apart[:, c, :], iota_lo, ACT.Square, scale=-1.0,
                                     bias=key_lo[:, bass.ds(w, 1), c]).then_inc(apart_ready, 1)
                    act.wait_ge(apart_ready, CHUNKS * (k + 1))
                    for c in range(CHUNKS):
                        last = a.activation(hot_lo[:, s, c, :], apart[:, c, :], ACT.Relu, scale=-1.0, bias=ones[:, 0:1])
                    last.then_inc(act_lo_ready, 1)

                def lows(t, b):
                    act.wait_ge(summed, t + 1)
                    if reached(t, 2):
                        act.wait_ge(agg_ready, t - 1)
                    a.copy(low[0:NT, b, :], ps[0:NT, 2 + b, C:2 * C]).then_inc(low_ready, 1)

                def keep(t, b):
                    act.wait_ge(agg_turned, t + 1)
                    if reached(t, 2):
                        act.wait_ge(multiplied, t - 1)
                    a.copy(aggT[:, b].rearrange("p a b -> p (a b)"), ps[:, 4, b * CB * NT:(b + 1) * CB * NT]).then_inc(aggT_ready, 1)

                def relu(t, b):
                    act.wait_ge(zb_ready, t + 1)
                    if not reached(t, 1):
                        act.wait_ge(pads_ready, 3)
                    if reached(t, 2):
                        act.wait_ge(low_made, t - 1)
                    for to in (zs[0:NT, b, :], hs2[0:NT, bass.ds(t, 1), 0:C].rearrange("p t c -> p (t c)")):
                        last = a.activation(to, zb[0:NT, b, :], ACT.Relu, scale=dsc[0:NT, bass.ds(t, 1)])
                    last.then_inc(z_ready, 1)

                def tile(t, b, u):
                    for m in range(UNITS):
                        if within(t, T - 1):
                            if m in LO_BEFORE:
                                low_hots(t + 1, LO_BEFORE.index(m))
                            store(t + 1, m, *shifted_slot(b, u, 1, 2))
                        if m == 0 and reached(t, 1):
                            lows(t - 1, 1 - b)
                        if m == 4 and reached(t, 1):
                            keep(t - 1, 1 - b)
                        if m == 10 and reached(t, 1):
                            relu(t - 1, 1 - b)

                pipeline(act, tile, T, 2, lead=1, lag=1)

            @block.sync
            def _(sp):
                def tile(t, b, u):
                    sp.wait_ge(looped, 2 * t + 2)
                    sp.wait_ge(pads_ready, 2)
                    sp.dma_start(at_dram[bass.ds(t, 1)].rearrange("t p n -> (t p) n"), at[:, b, :]).then_inc(at_out[b], 16)

                pipeline(sp, tile, T, 2)
                sp.wait_ge(at_out[0], 16 * (T // 2))
                sp.wait_ge(at_out[1], 16 * (T // 2))

        with nc.If(general == 1):
            sum_edges(1, hs2, hs_f32, dun2)

        take = carve(key_lo[:, :, :].rearrange("p w c -> p (w c)"))
        s_sum = take([P, HB, C])
        w_sum = take([P, HB])
        w_acc = take([P, HB, NT])
        take = carve(key_hi[:, :, :].rearrange("p w c -> p (w c)"))
        w2 = take([P, CB, C])
        b2b = take([P, C])
        take = carve(hs_f32)
        pmat = take([P, HB, C])
        bfb = take([P, C])
        final_rest = hs_f32[:, HB * C + C:]
        take = carve(final_rest)
        wfx = take([P, CB, HG])
        wfo = take([P, HB, C])
        bfx = take([P, HG])
        bdq = take([P, P])
        bdk = take([P, P])
        bdv = take([P, P])
        sT = take([P, CB, HB, P])
        tok = take([P, HB, P])
        tokT = take([P, HB, P])
        qT = take([P, HB, P])
        kT = take([P, HB, P])
        vv = take([P, HB, P])
        sc = take([P, HB, D])
        at_w = take([P, HB, P])
        atT = take([P, HB, P])
        oT = take([P, HB, P])
        smax = take([P, HB])
        ssum = take([P, HB])
        wrec = take([P, HB])
        zeroed, loaded = sem("f_zeroed"), sem("f_loaded")
        WS = 2.0 ** 15
        with ExitStack() as stage:
            take = carve(big_f[:, T * C:])
            agg = take([P, 2, C])
            low = take([P, 2, C])
            aggT = take([P, 2, CB, NT])
            zb = take([P, 2, C])
            base_in = take([P, 2, C])
            x1 = take([P, 2, C])
            xn2 = take([P, 2, C])
            xn2h = take([P, 2, C], F16)
            xn2l = take([P, 2, C], F16)
            xn2T = take([P, 2, 2, CB * NT], F16)
            lg = take([P, 2, HEADS, D])
            ew = take([P, 2, HEADS, D])
            ewh = take([P, 2, HG], F16)
            ewl = take([P, 2, HG], F16)
            wt = take([P, 2, HB, NT])
            hmax = take([P, 2, HEADS])
            hsum = take([P, 2, HEADS])
            st = take([P, 2, 6])
            mv = take([P, 2, 2])
            rstd = take([P, 2])
            w2_loaded = sem("w2_loaded")
            at_loaded, base_loaded = [sem(f"l2_at_loaded{b}") for b in range(2)], [sem(f"l2_base_loaded{b}") for b in range(2)]
            x1_out, w_out = [sem(f"x1_out{b}") for b in range(2)], [sem(f"w_out{b}") for b in range(2)]
            summed, low_ready, agg_ready = sem("l2_summed"), sem("l2_low_ready"), sem("l2_agg_ready")
            agg_turned, aggT_ready, multiplied = sem("l2_agg_turned"), sem("l2_aggT_ready"), sem("l2_multiplied")
            x1_ready, ln_step, xn2_ready = sem("x1_ready"), sem("l2_ln_step"), sem("xn2_ready")
            xn2_turned, xn2T_ready, logits_ready = sem("xn2_turned"), sem("xn2T_ready"), sem("logits_ready")
            shifted, exp_ready, soft_step, w_ready = sem("shifted"), sem("exp_ready"), sem("soft_step"), sem("w_ready")
            w_turned, wt_ready, w_added, s_added = sem("w_turned"), sem("wt_ready"), sem("w_added"), sem("s_added")
            zb_ready, std_ready, xn2_step = sem("l2_zb_ready"), sem("l2_std_ready"), sem("xn2_step")
            acc_ready = sem("acc_ready")
            block = stage.enter_context(nc.Block())

            @block.sync
            def _(sp):
                sp.dma_start(w2, W2.rearrange("(b p) n -> p b n", p=P)).then_inc(w2_loaded, 16)
                sp.dma_start(b2b, b2.rearrange("(a n) -> a n", a=1).to_broadcast([P, C])).then_inc(w2_loaded, 16)

                def tile(t, b, u):
                    if reached(t, 2):
                        sp.wait_ge(summed, t - 1)
                    sp.dma_start(at[:, b, :], at_dram[bass.ds(t, 1)].rearrange("t p n -> (t p) n")).then_inc(at_loaded[b], 16)
                    if reached(t, 2):
                        sp.wait_ge(x1_ready, t - 1)
                    sp.dma_start(base_in[0:NT, b, :], base_dram[bass.ds(t * NT, NT), :]).then_inc(base_loaded[b], 16)

                pipeline(sp, tile, T, 2)

            @block.tensor
            def _(pe):
                te = nc.tensor

                def sum_tile(t, b, u, k):
                    if k == 0:
                        pe.wait_ge(at_loaded[b], 16 * u + 16)
                        if reached(t, 2):
                            pe.wait_ge(agg_ready, t - 1)
                    mm = te.matmul(ps[:, b, :], lhsT=at[:, b, k * P:(k + 1) * P], rhs=hs2[:, k, :],
                                   start=(k == 0), stop=(k == T - 1))
                    if k == T - 1:
                        mm.then_inc(summed, 1)

                def turn(t, b):
                    pe.wait_ge(agg_ready, t + 1)
                    for c in range(CB):
                        mm = te.transpose(ps[:, 2, c * NT:(c + 1) * NT], agg[0:NT, b, c * P:(c + 1) * P], ident[0:NT, 0:NT])
                    mm.then_inc(agg_turned, 1)

                def multiply(t, b):
                    pe.wait_ge(aggT_ready, t + 1)
                    for c in range(CB):
                        mm = te.matmul(ps[0:NT, 3, 0:C], lhsT=aggT[:, b, c, :], rhs=w2[:, c, :],
                                       start=(c == 0), stop=(c == CB - 1))
                    mm.then_inc(multiplied, 1)

                def turn_x(t, b):
                    pe.wait_ge(xn2_ready, t + 1)
                    for h, x_half in enumerate((xn2h, xn2l)):
                        for c in range(CB):
                            n = h * CB + c
                            mm = te.matmul(ps[:, 3, n * NT:(n + 1) * NT], lhsT=x_half[0:NT, b, c * P:(c + 1) * P],
                                           rhs=ident16[0:NT, 0:NT], start=True, stop=True)
                    mm.then_inc(xn2_turned, 1)

                def logits(t, b):
                    pe.wait_ge(xn2T_ready, t + 1)
                    for c in range(CB):
                        for xh, wh in ((0, 0), (0, 1), (1, 0)):
                            mm = te.matmul(ps[0:NT, 4, :], lhsT=xn2T[:, b, xh, c * NT:(c + 1) * NT], rhs=wlog16[:, wh, c, :],
                                           start=(c == 0 and xh == wh == 0), stop=(c == CB - 1 and xh == 1))
                    mm.then_inc(logits_ready, 1)

                def weigh(t, b):
                    pe.wait_ge(w_ready, t + 1)
                    if reached(t, 1):
                        pe.wait_ge(wt_ready, t)
                    for p in range(HB):
                        for w_half in (ewh, ewl):
                            mm = te.matmul(ps[:, 5, p * NT:(p + 1) * NT], lhsT=w_half[0:NT, b, p * P:(p + 1) * P],
                                           rhs=ident16[0:NT, 0:NT], start=(w_half is ewh), stop=(w_half is ewl))
                    mm.then_inc(w_turned, 1)
                    for p in range(HB):
                        for w_half, x_half in ((ewh, xn2h), (ewh, xn2l), (ewl, xn2h)):
                            mm = te.matmul(ps[:, 6 + p // 2, (p % 2) * C:(p % 2 + 1) * C],
                                           lhsT=w_half[0:NT, b, p * P:(p + 1) * P], rhs=x_half[0:NT, b, :],
                                           start=False, stop=False, skip_group_check=True)
                    mm.then_inc(s_added, 1)

                def tile(t, b, u):
                    for k in range(T):
                        if reached(t, 0) and within(t, T):
                            sum_tile(t, b, u, k)
                        if reached(t, 1) and within(t, T + 1):
                            for at_k, do in ((6, turn), (12, multiply), (31, turn_x), (37, logits)):
                                if k == at_k:
                                    do(t - 1, 1 - b)
                        if k == 44 and reached(t, 2):
                            weigh(t - 2, b)

                for h in range(2):
                    te.matmul(ps[:, 6 + h, :], lhsT=zeros[:, :], rhs=w1[:, :, :], start=True, stop=False,
                              skip_group_check=True)
                pe.wait_ge(w2_loaded, 32)
                pipeline(pe, tile, T, 2, lag=2)

            @block.vector
            def _(dve):
                v = nc.vector

                def gather(t, b):
                    dve.wait_ge(low_ready, t + 1)
                    v.tensor_tensor(agg[0:NT, b, :], ps[0:NT, b, 0:C], low[0:NT, b, :], ALU.add).then_inc(agg_ready, 1)

                def norm(t, b, u):
                    dve.wait_ge(multiplied, t + 1)
                    v.scalar_tensor_tensor(out=zb[0:NT, b, :], in0=ps[0:NT, 3, 0:C], scalar=dun2[0:NT, bass.ds(t, 1)],
                                           in1=b2b[0:NT, :], op0=ALU.mult, op1=ALU.add).then_inc(zb_ready, 1)
                    dve.wait_ge(zb_ready, t + 1)
                    dve.wait_ge(base_loaded[b], 16 * u + 16)
                    if reached(t, 2):
                        dve.wait_ge(x1_out[b], 16 * u)
                    v.scalar_tensor_tensor(out=x1[0:NT, b, :], in0=zb[0:NT, b, :], scalar=0.0, in1=base_in[0:NT, b, :],
                                           op0=ALU.max, op1=ALU.add).then_inc(x1_ready, 1)
                    dve.wait_ge(x1_ready, t + 1)
                    v.bn_stats(st[0:NT, b, :], x1[0:NT, b, :]).then_inc(ln_step, 1)
                    dve.wait_ge(ln_step, 2 * t + 1)
                    v.memset(rstd[0:NT, b:b + 1], 0.0)
                    v.bn_aggr(mv[0:NT, b, :], st[0:NT, b, :]).then_inc(ln_step, 1)
                    dve.wait_ge(std_ready, t + 1)
                    v.reciprocal(rstd[0:NT, b:b + 1], rstd[0:NT, b:b + 1]).then_inc(xn2_step, 1)
                    dve.wait_ge(xn2_step, 3 * t + 1)
                    if reached(t, 2):
                        dve.wait_ge(s_added, t - 1)
                    for x_part in (xn2, xn2h):
                        v.tensor_scalar(x_part[0:NT, b, :], x1[0:NT, b, :], mv[0:NT, b, 0:1], rstd[0:NT, b:b + 1],
                                        ALU.subtract, ALU.mult).then_inc(xn2_step, 1)
                    dve.wait_ge(xn2_step, 3 * t + 3)
                    v.tensor_tensor(xn2l[0:NT, b, :], xn2[0:NT, b, :], xn2h[0:NT, b, :], ALU.subtract).then_inc(xn2_ready, 1)

                def shift(t, b):
                    dve.wait_ge(logits_ready, t + 1)
                    v.scalar_tensor_tensor(out=lg[0:NT, b].rearrange("p h d -> p (h d)"), in0=ps[0:NT, 4, :],
                                           scalar=unscale[0:NT], in1=blogb[0:NT, :], op0=ALU.mult, op1=ALU.add
                                           ).then_inc(soft_step, 1)
                    dve.wait_ge(soft_step, 6 * t + 1)
                    v.tensor_reduce(hmax[0:NT, b, :], lg[0:NT, b], AX.X, ALU.max).then_inc(soft_step, 1)
                    dve.wait_ge(soft_step, 6 * t + 2)
                    v.tensor_tensor(lg[0:NT, b], lg[0:NT, b],
                                    hmax[0:NT, b, :].rearrange("p (h o) -> p h o", o=1).to_broadcast([NT, HEADS, D]),
                                    ALU.subtract).then_inc(shifted, 1)

                def divide(t, b):
                    dve.wait_ge(exp_ready, t + 1)
                    v.tensor_reduce(hsum[0:NT, b, :], ew[0:NT, b], AX.X, ALU.add).then_inc(soft_step, 1)
                    dve.wait_ge(soft_step, 6 * t + 3)
                    v.reciprocal(hsum[0:NT, b, :], hsum[0:NT, b, :]).then_inc(soft_step, 1)
                    dve.wait_ge(soft_step, 6 * t + 4)
                    v.scalar_tensor_tensor(out=ew[0:NT, b], in0=ew[0:NT, b], scalar=WS,
                                           in1=hsum[0:NT, b, :].rearrange("p (h o) -> p h o", o=1)
                                           .to_broadcast([NT, HEADS, D]), op0=ALU.mult, op1=ALU.mult).then_inc(soft_step, 1)

                def split(t, b):
                    dve.wait_ge(soft_step, 6 * t + 5)
                    ewf = ew[0:NT, b].rearrange("p h d -> p (h d)")
                    v.tensor_copy(ewh[0:NT, b, :], ewf).then_inc(soft_step, 1)
                    dve.wait_ge(soft_step, 6 * t + 6)
                    v.tensor_tensor(ewl[0:NT, b, :], ewf, ewh[0:NT, b, :], ALU.subtract).then_inc(w_ready, 1)

                def tile(t, b, u):
                    if reached(t, 0):
                        norm(t, b, u)
                        shift(t, b)
                        divide(t, b)
                    if within(t, T - 1):
                        gather(t + 1, 1 - b)
                    if reached(t, 0):
                        split(t, b)

                dve.wait_ge(w2_loaded, 32)
                pipeline(dve, tile, T, 2, lead=1)
                dve.wait_ge(s_added, T)
                v.tensor_scalar(s_sum.rearrange("p a b -> p (a b)"), ps[:, 6:8, :].rearrange("p a b -> p (a b)"),
                                1.0 / WS, None, ALU.mult)

            @block.scalar
            def _(act):
                a = nc.scalar
                def rest(t, b):
                    act.wait_ge(summed, t + 1)
                    a.copy(low[0:NT, b, :], ps[0:NT, b, C:2 * C]).then_inc(low_ready, 1)
                    act.wait_ge(agg_turned, t + 1)
                    a.copy(aggT[:, b].rearrange("p a b -> p (a b)"), ps[:, 2, 0:CB * NT]).then_inc(aggT_ready, 1)
                    act.wait_ge(ln_step, 2 * t + 2)
                    a.activation(rstd[0:NT, b:b + 1], mv[0:NT, b, 1:2], ACT.Sqrt, bias=eps[0:NT, 0:1]).then_inc(std_ready, 1)
                    act.wait_ge(xn2_turned, t + 1)
                    a.copy(xn2T[:, b].rearrange("p a b -> p (a b)"), ps[:, 3, 0:2 * CB * NT]).then_inc(xn2T_ready, 1)
                    act.wait_ge(shifted, t + 1)
                    a.activation(ew[0:NT, b], lg[0:NT, b], ACT.Exp).then_inc(exp_ready, 1)
                    act.dma_start(x1_dram[bass.ds(t * NT, NT), :], x1[0:NT, b, :]).then_inc(x1_out[b], 16)

                def turned(t, b, u):
                    act.wait_ge(w_turned, t + 1)
                    if reached(t, 2):
                        act.wait_ge(w_out[b], 16 * u)
                        act.wait_ge(w_added, t - 1)
                    a.mul(wt[:, b].rearrange("p a b -> p (a b)"), ps[:, 5, 0:HB * NT], 1.0 / WS).then_inc(wt_ready, 1)
                    act.wait_ge(wt_ready, t + 1)
                    act.dma_start(wT_dram[bass.ds(t, 1)].rearrange("t p n -> (t p) n"),
                                  wt[:, b].rearrange("p a b -> p (a b)")).then_inc(w_out[b], 16)

                def tile(t, b, u):
                    if within(t, T):
                        rest(t, b)
                    if reached(t, 1):
                        turned(t - 1, *shifted_slot(b, u, -1, 2))

                pipeline(act, tile, T, 2, lag=1)
                for b in range(2):
                    act.wait_ge(x1_out[b], 16 * (T // 2))
                    act.wait_ge(w_out[b], 16 * (T // 2))

            @block.gpsimd
            def _(pool):
                g = nc.gpsimd
                g.memset(w_acc, 0.0).then_inc(acc_ready, 1)
                for z in (bdq, bdk, bdv, tok, at_w):
                    last = g.memset(z, 0.0)
                last.then_inc(zeroed, 1)
                for to, of in ((wfx, W_fx.rearrange("(b p) n -> p b n", p=P)),
                               (wfo, W_fo.rearrange("(b p) n -> p b n", p=P)),
                               (bfx, b_fx.rearrange("(a n) -> a n", a=1).to_broadcast([P, HG])),
                               (bfb, b_fo.rearrange("(a n) -> a n", a=1).to_broadcast([P, C]))):
                    pool.dma_start(to, of).then_inc(loaded, 16)
                pool.wait_ge(zeroed, 1)
                for to, of in ((bdq, W_q), (bdk, W_k), (bdv, W_v)):
                    for h in range(2):
                        pool.dma_start(to[h * D:(h + 1) * D, h * D:(h + 1) * D], of).then_inc(loaded, 16)
                pool.wait_ge(loaded, 160)
                pool.wait_ge(acc_ready, 1)

                def tile(t, b, u):
                    pool.wait_ge(wt_ready, t + 1)
                    g.tensor_tensor(w_acc, w_acc, wt[:, b], ALU.add).then_inc(w_added, 1)
                    pool.wait_ge(w_added, t + 1)

                pipeline(pool, tile, T, 2)

        with ExitStack() as stage:
            pe_step, dve_step, act_step = sem("f_pe_step"), sem("f_dve_step"), sem("f_act_step")
            block = stage.enter_context(nc.Block())

            @block.tensor
            def _(pe):
                te = nc.tensor
                pe.wait_ge(loaded, 160)
                for i in range(CB):
                    for p in range(HB):
                        mm = te.transpose(ps[:, i, p * P:(p + 1) * P], s_sum[:, p, i * P:(i + 1) * P], ident[:, :])
                mm.then_inc(pe_step, 1)
                pe.wait_ge(act_step, 1)
                for p in range(HB):
                    for i in range(CB):
                        mm = te.matmul(ps[:, 2, p * P:(p + 1) * P], lhsT=sT[:, i, p, :], rhs=wfx[:, i, p * P:(p + 1) * P],
                                       start=(i == 0), stop=(i == CB - 1))
                mm.then_inc(pe_step, 1)
                pe.wait_ge(dve_step, 1)
                for p in range(HB):
                    mm = te.transpose(ps[:, 3, p * P:(p + 1) * P], tok[:, p, :], ident[:, :])
                mm.then_inc(pe_step, 1)
                pe.wait_ge(act_step, 2)
                for p in range(HB):
                    te.matmul(ps[:, 4, p * P:(p + 1) * P], lhsT=bdq, rhs=tokT[:, p, :], start=True, stop=True)
                for p in range(HB):
                    te.matmul(ps[:, 5, p * P:(p + 1) * P], lhsT=bdk, rhs=tokT[:, p, :], start=True, stop=True)
                for p in range(HB):
                    mm = te.matmul(ps[:, 6, p * P:(p + 1) * P], lhsT=tokT[:, p, :], rhs=bdv, start=True, stop=True)
                mm.then_inc(pe_step, 1)
                pe.wait_ge(act_step, 3)
                pe.wait_ge(dve_step, 2)
                for p in range(HB):
                    mm = te.matmul(ps[:, 7, p * P:(p + 1) * P], lhsT=qT[:, p, :], rhs=kT[:, p, :], start=True, stop=True)
                mm.then_inc(pe_step, 1)
                pe.wait_ge(dve_step, 4)
                for p in range(HB):
                    mm = te.transpose(ps[:, 0, p * P:(p + 1) * P], at_w[:, p, :], ident[:, :])
                mm.then_inc(pe_step, 1)
                pe.wait_ge(act_step, 5)
                for p in range(HB):
                    mm = te.matmul(ps[:, 1, p * P:(p + 1) * P], lhsT=vv[:, p, :], rhs=atT[:, p, :], start=True, stop=True)
                mm.then_inc(pe_step, 1)
                pe.wait_ge(act_step, 6)
                for p in range(HB):
                    mm = te.matmul(ps[:, 2 + p // 2, (p % 2) * C:(p % 2 + 1) * C], lhsT=oT[:, p, :], rhs=wfo[:, p, :],
                                   start=True, stop=True)
                mm.then_inc(pe_step, 1)

            @block.scalar
            def _(act):
                a = nc.scalar

                def flat(y):
                    return y.rearrange("p a b -> p (a b)")

                act.wait_ge(pe_step, 1)
                a.copy(sT.rearrange("p a b c -> p (a b c)"), ps[:, 0:2, :].rearrange("p a b -> p (a b)")).then_inc(act_step, 1)
                act.wait_ge(pe_step, 3)
                a.copy(flat(tokT), ps[:, 3, :]).then_inc(act_step, 1)
                act.wait_ge(pe_step, 4)
                a.mul(flat(qT), ps[:, 4, :], float(D) ** -0.5)
                a.copy(flat(vv), ps[:, 6, :]).then_inc(act_step, 1)
                act.wait_ge(dve_step, 3)
                a.activation(sc, sc, ACT.Exp).then_inc(act_step, 1)
                act.wait_ge(pe_step, 6)
                a.copy(flat(atT), ps[:, 0, :]).then_inc(act_step, 1)
                act.wait_ge(pe_step, 7)
                a.copy(flat(oT), ps[:, 1, :]).then_inc(act_step, 1)

            @block.vector
            def _(dve):
                v = nc.vector
                own = sem("f_own")
                n = [0]

                def step(ins):
                    n[0] += 1
                    ins.then_inc(own, 1)
                    dve.wait_ge(own, n[0])

                step(v.tensor_reduce(w_sum, w_acc, AX.X, ALU.add))
                step(v.tensor_scalar(wrec, w_sum, 1e-5, None, ALU.add))
                step(v.reciprocal(wrec, wrec))
                dve.wait_ge(pe_step, 2)
                dve.wait_ge(loaded, 160)
                dve.wait_ge(zeroed, 1)
                for p in range(HB):
                    for h in range(2):
                        r, c = slice(h * D, (h + 1) * D), slice((2 * p + h) * D, (2 * p + h + 1) * D)
                        v.scalar_tensor_tensor(out=tok[r, p, h * D:(h + 1) * D], in0=bfx[r, c], scalar=w_sum[r, p:p + 1],
                                               in1=ps[r, 2, c], op0=ALU.mult, op1=ALU.add).then_inc(own, 1)
                n[0] += 2 * HB
                dve.wait_ge(own, n[0])
                for p in range(HB):
                    last = v.tensor_scalar(tok[:, p, :], tok[:, p, :], wrec[:, p:p + 1], None, ALU.mult)
                last.then_inc(dve_step, 1)
                dve.wait_ge(pe_step, 4)
                v.tensor_copy(kT.rearrange("p a b -> p (a b)"), ps[:, 5, :]).then_inc(dve_step, 1)
                dve.wait_ge(pe_step, 5)
                for h in range(2):
                    r = slice(h * D, (h + 1) * D)
                    s = ps[r, 7, :].rearrange("p (a b) -> p a b", b=P)[:, :, h * D:(h + 1) * D]
                    step(v.tensor_reduce(smax[r, :], s, AX.X, ALU.max))
                    last = v.tensor_tensor(sc[r], s, smax[r, :].rearrange("p (a o) -> p a o", o=1)
                                           .to_broadcast([D, HB, D]), ALU.subtract)
                last.then_inc(dve_step, 1)
                dve.wait_ge(act_step, 4)
                step(v.tensor_reduce(ssum, sc, AX.X, ALU.add))
                step(v.reciprocal(ssum, ssum))
                for h in range(2):
                    r = slice(h * D, (h + 1) * D)
                    last = v.tensor_tensor(at_w[r, :, h * D:(h + 1) * D], sc[r],
                                           ssum[r, :].rearrange("p (a o) -> p a o", o=1).to_broadcast([D, HB, D]), ALU.mult)
                last.then_inc(dve_step, 1)
                dve.wait_ge(pe_step, 8)
                v.tensor_copy(pmat.rearrange("p a b -> p (a b)"), ps[:, 2:4, :].rearrange("p a b -> p (a b)"))

        stream(1, final_rest, lambda t: wT_dram[bass.ds(t, 1)].rearrange("t p n -> (t p) n"), x1_dram,
               [pmat[:, p, :] for p in range(HB)], bfb, out)


_INS = ['x', 'src', 'dst', 'L0_gnn_W1', 'L0_gnn_b1', 'L0_gnn_W2', 'L0_gnn_b2', 'L0_mix_W_qkv', 'L0_mix_b_qkv',
        'L0_mix_W_out', 'L0_mix_b_out', 'L0_ffn_W_fx', 'L0_ffn_b_fx', 'L0_ffn_W_x', 'L0_ffn_b_x', 'L0_ffn_W_slice',
        'L0_ffn_b_slice', 'L0_ffn_W_q', 'L0_ffn_W_k', 'L0_ffn_W_v', 'L0_ffn_W_out', 'L0_ffn_b_out',
        'L0_ffn_temperature']


def kernel(**inputs):
    import numpy as _np
    import concourse.bacc as _bacc
    from concourse import mybir as _mybir
    from concourse.bass_utils import run_bass_kernel_spmd as _run

    nc = _bacc.Bacc("TRN2", target_bir_lowering=False, num_devices=1)
    arrays, args = {}, []
    for name in _INS:
        a = _np.ascontiguousarray(inputs[name])
        arrays[f"in_{name}_dram"] = a
        args.append(nc.dram_tensor(f"in_{name}_dram", a.shape, _mybir.dt.from_np(a.dtype), kind="ExternalInput").ap())
    out = nc.dram_tensor("out_0_dram", inputs["x"].shape, _mybir.dt.float32, kind="ExternalOutput").ap()
    gps_layer(nc, *args, out)
    r = _run(nc, [arrays], core_ids=[0])
    return r.results[0]["out_0_dram"]
```
